# Optimizing a Trainium2 kernel written in Bass

```python
import numpy as np
import jax
import jax.numpy as jnp

def _softmax(x, axis=-1):
    return jax.nn.softmax(x, axis=axis)
def _gelu(x):
    return jax.nn.gelu(x, approximate=True)
def _silu(x):
    return jax.nn.silu(x)
def _sigmoid(x):
    return jax.nn.sigmoid(x)
def _layernorm(x, axis=-1, eps=1e-5):
    m = jnp.mean(x, axis=axis, keepdims=True)
    v = jnp.var(x, axis=axis, keepdims=True)
    return (x - m) / jnp.sqrt(v + eps)
def _scatter_add(tgt, idx, src, axis=0):
    return tgt.at[idx].add(src)
def _segment_sum(src, seg, n):
    return jax.ops.segment_sum(src, seg, n)

kernel_name = 'mk_adj_preln_d4_adj_256_dfed64'

def setup_inputs(seed: int = 0):
    np.random.seed(seed)
    _w = jnp.asarray
    def _rec_inputs():
        import jax
        import jax.numpy as jnp
        _gk = jax.random.key(seed)
        x = 7.22e-05 + 1 * jax.random.normal(jax.random.fold_in(_gk, 1), (16, 1024, 256), jnp.float32)
        _a = jax.random.bernoulli(jax.random.fold_in(_gk, 2), 0.0078125, (16, 1024, 1024))
        _af = _a.astype(jnp.float32)
        adj = _af
        _nm = jnp.ones((16, 1024), dtype=bool)
        nodemask = jnp.where(_nm, 1.0, 0.0).astype(jnp.int32)
        return x, adj, nodemask
    x, adj, nodemask = _rec_inputs()
    def _L0_gnn_setup():
        import jax, jax.numpy as jnp
        import numpy as np
        EPS = 1e-05
        ALPHA = 0.2

        def _bn(x, gamma, beta):
            red = tuple(range(x.ndim - 1))
            mean = jnp.mean(x, axis=red, keepdims=True)
            var = jnp.mean(jnp.square(x - mean), axis=red, keepdims=True)
            return (x - mean) * jax.lax.rsqrt(var + EPS) * gamma + beta
        key = jax.random.key(seed)
        ks = jax.random.split(key, 5)
        B, N, Fin, Fout = (32, 1024, 256, 256)
        h = jax.random.normal(ks[0], (B, N, Fin), dtype=jnp.float32)
        adj = (jax.random.uniform(ks[1], (B, N, N), dtype=jnp.float32) > 0.9).astype(jnp.float32)
        W = jax.random.normal(ks[2], (Fout, Fin), dtype=jnp.float32) * (1.0 / np.sqrt(Fin))
        a1 = jax.random.normal(ks[3], (Fout,), dtype=jnp.float32) * 0.1
        a2 = jax.random.normal(ks[4], (Fout,), dtype=jnp.float32) * 0.1
        return {'h': h, 'adj': adj, 'W': W, 'a1': a1, 'a2': a2, 'g1': jnp.ones((N,), jnp.float32), 'b1': jnp.zeros((N,), jnp.float32), 'g2': jnp.ones((N,), jnp.float32), 'b2': jnp.zeros((N,), jnp.float32), 'g3': jnp.ones((Fout,), jnp.float32), 'b3': jnp.zeros((Fout,), jnp.float32)}
    _L0_gnn_all = _L0_gnn_setup()
    _L0_gnn_in = {k: v for k, v in _L0_gnn_all.items() if k in ('W', 'a1', 'a2', 'g1', 'b1', 'g2', 'b2', 'g3', 'b3', )}
    del _L0_gnn_all

    def _L1_gnn_setup():
        import jax, jax.numpy as jnp
        import numpy as np
        D_IN = 256
        D_HID = 512
        key = jax.random.key(seed)
        k1, k2, k3, k4, k5, k6 = jax.random.split(key, 6)
        x = jax.random.normal(k1, (8, 4096, D_IN), dtype=jnp.float32)
        adj = jax.random.uniform(k2, (8, 4096, 4096), dtype=jnp.float32)
        s1 = 1.0 / np.sqrt(D_IN)
        s2 = 1.0 / np.sqrt(D_HID)
        W1 = jax.random.uniform(k3, (D_IN, D_HID), dtype=jnp.float32, minval=-s1, maxval=s1)
        b1 = jax.random.uniform(k4, (D_HID,), dtype=jnp.float32, minval=-s1, maxval=s1)
        W2 = jax.random.uniform(k5, (D_HID, D_IN), dtype=jnp.float32, minval=-s2, maxval=s2)
        b2 = jax.random.uniform(k6, (D_IN,), dtype=jnp.float32, minval=-s2, maxval=s2)
        eps = jnp.zeros((1,), dtype=jnp.float32)
        return {'x': x, 'adj': adj, 'eps': eps, 'W1': W1, 'b1': b1, 'W2': W2, 'b2': b2}
    _L1_gnn_all = _L1_gnn_setup()
    _L1_gnn_in = {k: v for k, v in _L1_gnn_all.items() if k in ('eps', 'W1', 'b1', 'W2', 'b2', )}
    del _L1_gnn_all

    def _L2_gnn_setup():
        import jax, jax.numpy as jnp
        import numpy as np
        HIDDEN = 256
        NEG_INF = -1e+30
        key = jax.random.key(seed)
        k1, k2, k3, k4 = jax.random.split(key, 4)
        B, S, H = (4, 4096, HIDDEN)
        matrix = jax.random.normal(k1, (B, S, H), dtype=jnp.float32)
        mask = jax.random.randint(k2, (B, S), 0, 2, dtype=jnp.int32)
        adj = jax.random.uniform(k3, (B, S, S), dtype=jnp.float32)
        limit = float(np.sqrt(6.0 / (H + H)))
        W = jax.random.uniform(k4, (H, H), dtype=jnp.float32, minval=-limit, maxval=limit)
        return {'matrix': matrix, 'mask': mask, 'adj': adj, 'W': W}
    _L2_gnn_all = _L2_gnn_setup()
    _L2_gnn_in = {k: v for k, v in _L2_gnn_all.items() if k in ('W', )}
    del _L2_gnn_all

    def _L3_gnn_setup():
        import jax, jax.numpy as jnp
        import numpy as np
        key = jax.random.key(seed)
        k1, k2, k3, k4 = jax.random.split(key, 4)
        B, N, F_in, F_out = (8, 2048, 256, 256)
        x = jax.random.normal(k1, (B, N, F_in), dtype=jnp.float32)
        adj = jax.random.uniform(k2, (B, N, N), dtype=jnp.float32)
        stdv = 1.0 / np.sqrt(F_out)
        weight = jax.random.uniform(k3, (F_in, F_out), dtype=jnp.float32, minval=-stdv, maxval=stdv)
        bias = jax.random.uniform(k4, (F_out,), dtype=jnp.float32, minval=-stdv, maxval=stdv)
        return {'x': x, 'adj': adj, 'weight': weight, 'bias': bias}
    _L3_gnn_all = _L3_gnn_setup()
    _L3_gnn_in = {k: v for k, v in _L3_gnn_all.items() if k in ('weight', 'bias', )}
    del _L3_gnn_all

    return {
        "x": x,
        "adj": adj,
        "nodemask": nodemask,
        "L0_gnn_W": _L0_gnn_in["W"],
        "L0_gnn_a1": _L0_gnn_in["a1"],
        "L0_gnn_a2": _L0_gnn_in["a2"],
        "L0_gnn_g1": _L0_gnn_in["g1"],
        "L0_gnn_b1": _L0_gnn_in["b1"],
        "L0_gnn_g2": _L0_gnn_in["g2"],
        "L0_gnn_b2": _L0_gnn_in["b2"],
        "L0_gnn_g3": _L0_gnn_in["g3"],
        "L0_gnn_b3": _L0_gnn_in["b3"],
        "L1_gnn_eps": _L1_gnn_in["eps"],
        "L1_gnn_W1": _L1_gnn_in["W1"],
        "L1_gnn_b1": _L1_gnn_in["b1"],
        "L1_gnn_W2": _L1_gnn_in["W2"],
        "L1_gnn_b2": _L1_gnn_in["b2"],
        "L2_gnn_W": _L2_gnn_in["W"],
        "L3_gnn_weight": _L3_gnn_in["weight"],
        "L3_gnn_bias": _L3_gnn_in["bias"],
    }

def reference(x, adj, nodemask, L0_gnn_W, L0_gnn_a1, L0_gnn_a2, L0_gnn_g1, L0_gnn_b1, L0_gnn_g2, L0_gnn_b2, L0_gnn_g3, L0_gnn_b3, L1_gnn_eps, L1_gnn_W1, L1_gnn_b1, L1_gnn_W2, L1_gnn_b2, L2_gnn_W, L3_gnn_weight, L3_gnn_bias):
    import jax
    import jax.numpy as jnp
    def _L0_gnn_ref(h, adj, W, a1, a2, g1, b1, g2, b2, g3, b3):
        import jax, jax.numpy as jnp
        import numpy as np
        EPS = 1e-05
        ALPHA = 0.2

        def _bn(x, gamma, beta):
            red = tuple(range(x.ndim - 1))
            mean = jnp.mean(x, axis=red, keepdims=True)
            var = jnp.mean(jnp.square(x - mean), axis=red, keepdims=True)
            return (x - mean) * jax.lax.rsqrt(var + EPS) * gamma + beta
        Wh = jnp.einsum('bnf,of->bno', h, W)
        ei = Wh @ a1
        ej = Wh @ a2
        att = ei[:, :, None] + ej[:, None, :]
        att = _bn(att, g1, b1)
        att = jnp.where(att >= 0, att, ALPHA * att)
        att = _bn(att, g2, b2)
        att = jax.nn.softmax(att, axis=2)
        att = att * adj
        h_prime = jnp.einsum('bij,bjo->bio', att, Wh)
        h_prime = _bn(h_prime, g3, b3)
        return jax.nn.elu(h_prime)

    def _L1_gnn_ref(x, adj, eps, W1, b1, W2, b2):
        import jax, jax.numpy as jnp
        import numpy as np
        D_IN = 256
        D_HID = 512
        aggregated = jnp.einsum('bnm,bmd->bnd', adj, x)
        h = (1.0 + eps) * x + aggregated
        h = jax.nn.relu(h @ W1 + b1)
        return h @ W2 + b2

    def _L2_gnn_ref(matrix, mask, adj, W):
        import jax, jax.numpy as jnp
        import numpy as np
        HIDDEN = 256
        NEG_INF = -1e+30
        intermediate = jnp.einsum('bsh,hd->bsd', matrix, W)
        similarities = jnp.einsum('bsd,btd->bst', intermediate, matrix)
        similarities = similarities * adj
        key_mask = mask[:, None, :].astype(bool)
        masked = jnp.where(key_mask, similarities, NEG_INF)
        attn = jax.nn.softmax(masked, axis=-1)
        output = jnp.einsum('bst,bth->bsh', attn, matrix)
        return output

    def _L3_gnn_ref(x, adj, weight, bias):
        import jax, jax.numpy as jnp
        import numpy as np
        support = jnp.einsum('bni,io->bno', x, weight)
        out = jnp.einsum('bnm,bmo->bno', adj, support)
        return out + bias

    h = jnp.maximum(_layernorm(x, axis=-1), 0.0)
    x = x + _L0_gnn_ref(h, adj, L0_gnn_W, L0_gnn_a1, L0_gnn_a2, L0_gnn_g1, L0_gnn_b1, L0_gnn_g2, L0_gnn_b2, L0_gnn_g3, L0_gnn_b3)
    h = jnp.maximum(_layernorm(x, axis=-1), 0.0)
    x = x + _L1_gnn_ref(h, adj, L1_gnn_eps, L1_gnn_W1, L1_gnn_b1, L1_gnn_W2, L1_gnn_b2)
    h = jnp.maximum(_layernorm(x, axis=-1), 0.0)
    x = x + _L2_gnn_ref(h, nodemask, adj, L2_gnn_W)
    h = jnp.maximum(_layernorm(x, axis=-1), 0.0)
    x = x + _L3_gnn_ref(h, adj, L3_gnn_weight, L3_gnn_bias)
    return x


_drawn_inputs = setup_inputs


def setup_inputs(seed=0):
    import zlib

    import numpy as np

    out = dict(_drawn_inputs(seed))
    spreads = {'L0_gnn_g1': (1.0, 0.6),
     'L0_gnn_b1': (0.0, 0.51),
     'L0_gnn_g2': (1.0, 0.2),
     'L0_gnn_b2': (0.0, 0.295),
     'L0_gnn_g3': (1.0, 0.2),
     'L0_gnn_b3': (0.0, 0.1)}
    factors = {'L1_gnn_b1': 5.148, 'L3_gnn_bias': 5.219}
    for name, (base, spread) in spreads.items():
        noise = np.random.default_rng([zlib.crc32(name.encode()), seed]).standard_normal(out[name].shape)
        drawn = base * np.exp(spread * noise) if base else spread * noise
        out[name] = jnp.asarray(drawn.astype(out[name].dtype))
    for name, factor in factors.items():
        out[name] = (out[name] * factor).astype(out[name].dtype)
    return out
```

```python
from contextlib import ExitStack

import concourse.bass as bass
from concourse import mybir

ACT = mybir.ActivationFunctionType
ALU = mybir.AluOpType
F32 = mybir.dt.float32
F16 = mybir.dt.float16
BF16 = mybir.dt.bfloat16
I32 = mybir.dt.int32
AX = mybir.AxisListType.X

P = 128
EPS = 1e-5
SLOPE = 0.2
NEG = -1e30
BIG = 3.0e38


class Shapes:
    def __init__(self, x, w1):
        self.B, self.N, self.D = x.shape
        self.H = w1.shape[1]
        self.T = self.N // P
        self.KD = self.D // P
        self.KH = self.H // P


def after(e, sem, value):
    if not isinstance(value, int) or value > 0:
        e.wait_ge(sem, value)


def row_stats(e, n, T, D, x_rows, st, small, sums, ve, sems):
    ln_stats, ln_small, ln_var = sems
    for t in range(T):
        e.bn_stats(st[:, t, :], x_rows(t)).then_inc(ln_stats, 1)
    e.wait_ge(ln_stats, n * T + T)
    e.tensor_tensor(sums[:], st[:, :, 1], st[:, :, 4], ALU.add).then_inc(ln_small, 1)
    e.tensor_tensor(small[:, 0, :], st[:, :, 1], st[:, :, 4], ALU.subtract).then_inc(ln_small, 1)
    e.tensor_tensor(small[:, 1, :], st[:, :, 2], st[:, :, 5], ALU.add).then_inc(ln_small, 1)
    e.wait_ge(ln_small, n * 5 + 3)
    e.tensor_tensor(small[:, 2, :], small[:, 0, :], small[:, 0, :], ALU.mult).then_inc(ln_small, 1)
    e.wait_ge(ln_small, n * 5 + 4)
    e.scalar_tensor_tensor(small[:, 3, :], small[:, 2, :], D / 4.0, small[:, 1, :], ALU.mult, ALU.add).then_inc(ln_small, 1)
    e.wait_ge(ln_small, n * 5 + 5)
    e.tensor_scalar(ve[:], small[:, 3, :], 1.0 / D, EPS, ALU.mult, ALU.add).then_inc(ln_var, 1)


def split(e, hi, lo, src, copied, done):
    e.tensor_copy(hi, src).then_inc(copied[0], 1)
    e.wait_ge(copied[0], copied[1])
    e.tensor_tensor(lo, src, hi, ALU.subtract).then_inc(done, 1)


def nodes_block(nc, S, x, wt, w, a12, keep, wh_dram):
    B, N, D, T, KD = S.B, S.N, S.D, S.T, S.KD
    PAIRS = B // 2
    with ExitStack() as ctx:
        sb = lambda name, shape, dt: ctx.enter_context(nc.sbuf_tensor(name, shape, dt))
        ps = lambda name, shape, dt: ctx.enter_context(nc.psum_tensor(name, shape, dt))
        sem = lambda name: ctx.enter_context(nc.semaphore(name))
        xin = [sb(f"a_xin{q}", [P, T, D], F32) for q in range(2)]
        wt32 = sb("a_wt32", [P, KD, D], F32)
        w32 = sb("a_w32", [P, KD, D], F32)
        a32 = sb("a_a32", [P, KD, 2], F32)
        wt_hi = sb("a_wt_hi", [P, KD, D], F16)
        wt_lo = sb("a_wt_lo", [P, KD, D], F16)
        u32 = sb("a_u32", [P, KD, 2], F32)
        u_hi = sb("a_u_hi", [P, KD, 2], F16)
        u_lo = sb("a_u_lo", [P, KD, 2], F16)
        st = sb("a_st", [P, T, 6], F32)
        small, sums = sb("a_small", [P, 4, T], F32), sb("a_sums", [P, T], F32)
        ve = sb("a_ve", [P, T], F32)
        rstd = sb("a_rstd", [P, T], F32)
        shift = sb("a_shift", [P, T], F32)
        h32 = sb("a_h32", [P, T, D], F32)
        hh = sb("a_hh", [P, T, D], F16)
        hl = sb("a_hl", [P, T, D], F16)
        hth = sb("a_hth", [P, KD, N], F16)
        htl = sb("a_htl", [P, KD, N], F16)
        wh = [sb(f"a_wh{q}", [P, 2, T, D], F16) for q in range(2)]
        pt_hi = ps("a_pt_hi", [P, KD, N], F16)
        pt_lo = ps("a_pt_lo", [P, KD, N], F16)
        pw = [ps(f"a_pw{k}", [P, 2, D], F32) for k in range(2)]
        pe_ef = ps("a_pe_ef", [P, 256], F32)
        ef_ps = pe_ef[:, 0:2 * T].rearrange("p (t c) -> p t c", c=2)
        u_ps = ps("a_u_ps", [P, 512], F32)
        u_psv = u_ps[:, 0:2 * KD].rearrange("p (k c) -> p k c", c=2)

        w_loaded = sem("a_w_loaded")
        x_loaded = [sem(f"a_x_loaded{q}") for q in range(2)]
        consts = sem("a_consts")
        w_hi_done, w_lo_done = sem("a_w_hi_done"), sem("a_w_lo_done")
        u_done = sem("a_u_done")
        u_copied = sem("a_u_copied")
        ln_stats, ln_small, ln_var = sem("a_ln_stats"), sem("a_ln_small"), sem("a_ln_var")
        ln_rstd, ln_shift = sem("a_ln_rstd"), sem("a_ln_shift")
        h_ready, hh_ready, hl_ready = sem("a_h_ready"), sem("a_hh_ready"), sem("a_hl_ready")
        pt_hi_done, pt_lo_done = sem("a_pt_hi_done"), sem("a_pt_lo_done")
        hth_ready, htl_ready = sem("a_hth_ready"), sem("a_htl_ready")
        pw_done, whh_ready, pw_free = sem("a_pw_done"), sem("a_whh_ready"), sem("a_pw_free")
        ef_done, ef_ready = sem("a_ef_done"), sem("a_ef_ready")
        wh_stored = [sem(f"a_wh_stored{q}") for q in range(2)]
        block = ctx.enter_context(nc.Block())
        ident, ident16 = keep["ident"], keep["ident16"]
        G = T // 2

        @block.sync
        def _(e):
            load = lambda b, q: e.dma_start(
                xin[q][:], x[b].rearrange("(t p) d -> p t d", p=P)).then_inc(x_loaded[q], 16)
            for q in range(2):
                load(q, q)
            e.dma_start(wt32[:], wt.rearrange("(k p) o -> p k o", p=P)).then_inc(w_loaded, 16)
            e.dma_start(w32[:], w.rearrange("(k p) f -> p k f", p=P)).then_inc(w_loaded, 16)
            e.dma_start(a32[:], a12.rearrange("p (k c) -> p k c", c=2)).then_inc(w_loaded, 16)
            with e.Fori(0, PAIRS - 1) as i:
                for q in range(2):
                    b = i * 2 + q
                    e.wait_ge(h_ready, b * T + T)
                    load(b + 2, q)

        @block.gpsimd
        def _(e):
            e.memset(ident[:], 0.0).then_inc(consts, 1)
            e.wait_ge(consts, 1)
            e.affine_select(out=ident[:], in_=ident[:], compare_op=ALU.not_equal, fill=1.0,
                            base=0, pattern=[[-1, P]], channel_multiplier=1).then_inc(consts, 1)
            e.memset(keep["minus_half"][:], -0.5).then_inc(consts, 1)
            e.memset(keep["ones"][:], 1.0).then_inc(consts, 1)
            e.wait_ge(consts, 4)
            e.tensor_copy(ident16[:], ident[:]).then_inc(consts, 1)
            e.wait_ge(consts, 5)
            with e.Fori(0, B) as b:
                e.wait_ge(ln_var, b + 1)
                e.wait_ge(h_ready, b * T)
                e.tensor_tensor(rstd[:], ve[:], keep["minus_half"][:, 0:T], ALU.pow).then_inc(ln_rstd, 1)

        @block.vector
        def _(e):
            e.sem_inc(pw_free, 2)
            e.wait_ge(w_loaded, 48)
            split(e, wt_hi[:], wt_lo[:], wt32[:], (w_hi_done, 1), w_lo_done)
            e.wait_ge(u_done, 1)
            e.tensor_copy(u32[:], u_psv).then_inc(u_copied, 1)
            e.wait_ge(u_copied, 1)
            split(e, u_hi[:], u_lo[:], u32[:], (w_hi_done, 2), w_lo_done)
            with e.Fori(0, PAIRS) as i:
                for q in range(2):
                    b = i * 2 + q
                    e.wait_ge(x_loaded[q], i * 16 + 16)
                    row_stats(e, b, T, D, lambda t: xin[q][:, t, :], st, small, sums, ve, (ln_stats, ln_small, ln_var))
                    e.wait_ge(ln_rstd, b + 1)
                    e.scalar_tensor_tensor(shift[:], sums[:], -0.5, rstd[:],
                                           ALU.mult, ALU.mult).then_inc(ln_shift, 1)
                    e.wait_ge(hh_ready, b + 1)
                    e.wait_ge(pt_lo_done, b)
                    e.tensor_tensor(hl[:], h32[:], hh[:], ALU.subtract).then_inc(hl_ready, 1)
                    e.wait_ge(pt_hi_done, b + 1)
                    e.wait_ge(ef_done, b)
                    e.tensor_copy(hth[:], pt_hi[:]).then_inc(hth_ready, 1)
                    for g in range(G):
                        e.wait_ge(whh_ready, b * G + g + 1)
                        e.tensor_tensor(wh[q][:, 1, 2 * g:2 * g + 2, :], pw[g % 2][:],
                                        wh[q][:, 0, 2 * g:2 * g + 2, :], ALU.subtract).then_inc(pw_free, 1)
                    e.wait_ge(ef_done, b + 1)
                    for c, col in enumerate((keep["ecol"], keep["fcol"])):
                        e.tensor_copy(col[:, :, bass.ds(b, 1)], ef_ps[:, :, c:c + 1]).then_inc(ef_ready, 1)

        @block.scalar
        def _(e):
            with e.Fori(0, PAIRS) as i:
                for q in range(2):
                    b = i * 2 + q
                    e.wait_ge(ln_shift, b + 1)
                    e.wait_ge(hl_ready, b)
                    for t in range(T):
                        e.activation(h32[:, t, :], xin[q][:, t, :], ACT.Relu, bias=shift[:, t:t + 1],
                                     scale=rstd[:, t:t + 1]).then_inc(h_ready, 1)
                    e.wait_ge(h_ready, b * T + T)
                    e.wait_ge(pt_hi_done, b)
                    e.activation(hh[:], h32[:], ACT.Copy).then_inc(hh_ready, 1)
                    e.wait_ge(pt_lo_done, b + 1)
                    e.wait_ge(ef_done, b)
                    e.activation(htl[:], pt_lo[:], ACT.Copy).then_inc(htl_ready, 1)
                    e.wait_ge(wh_stored[q], i * 16)
                    for g in range(G):
                        e.wait_ge(pw_done, b * G + g + 1)
                        e.activation(wh[q][:, 0, 2 * g:2 * g + 2, :], pw[g % 2][:],
                                     ACT.Copy).then_inc(whh_ready, 1)
                    e.wait_ge(pw_free, b * G + G + 2)
                    e.dma_start(wh_dram[b], wh[q][:]).then_inc(wh_stored[q], 16)
            for q in range(2):
                e.wait_ge(wh_stored[q], 16 * PAIRS)

        @block.tensor
        def _(e):
            e.wait_ge(w_loaded, 48)
            for f in range(KD):
                for k in range(KD):
                    mm = e.matmul(u_psv[:, f, :], w32[:, k, f * P:(f + 1) * P], a32[:, k, :],
                                  start=(k == 0), stop=(k == KD - 1))
            mm.then_inc(u_done, 1)
            e.wait_ge(consts, 5)
            e.wait_ge(w_lo_done, 2)
            with e.Fori(0, B) as b:
                for src, dst, ready, done, free in ((hh, pt_hi, hh_ready, pt_hi_done, hth_ready),
                                                    (hl, pt_lo, hl_ready, pt_lo_done, htl_ready)):
                    e.wait_ge(ready, b + 1)
                    e.wait_ge(free, b)
                    for k in range(KD):
                        for t in range(T):
                            mm = e.transpose(dst[:, k, t * P:(t + 1) * P],
                                             src[:, t, k * P:(k + 1) * P], ident16[:])
                    mm.then_inc(done, 1)
                e.wait_ge(hth_ready, b + 1)
                e.wait_ge(htl_ready, b + 1)
                for g in range(G):
                    e.wait_ge(pw_free, b * G + g + 1)
                    for t in (2 * g, 2 * g + 1):
                        parts = [(ht, wp, k) for k in range(KD)
                                 for ht, wp in ((hth, wt_hi), (hth, wt_lo), (htl, wt_hi))]
                        for n, (ht, wp, k) in enumerate(parts):
                            mm = e.matmul(pw[g % 2][:, t % 2, :], ht[:, k, t * P:(t + 1) * P], wp[:, k, :],
                                          start=(n == 0), stop=(n == len(parts) - 1))
                    mm.then_inc(pw_done, 1)
                e.wait_ge(ef_ready, b * 2)
                for t in range(T):
                    parts = [(ht, up, k) for k in range(KD)
                             for ht, up in ((hth, u_hi), (hth, u_lo), (htl, u_hi))]
                    for n, (ht, up, k) in enumerate(parts):
                        mm = e.matmul(ef_ps[:, t, :], ht[:, k, t * P:(t + 1) * P], up[:, k, :],
                                      start=(n == 0), stop=(n == len(parts) - 1))
                mm.then_inc(ef_done, 1)


def tables_block(nc, S, vecs, keep, e9_dram, e_dram, ab9_dram, gd_dram, s_dram):
    B, N, D, T = S.B, S.N, S.D, S.T
    PAIRS = B // 2
    RING = 4
    with ExitStack() as ctx:
        sb = lambda name, shape, dt: ctx.enter_context(nc.sbuf_tensor(name, shape, dt))
        ps = lambda name, shape, dt: ctx.enter_context(nc.psum_tensor(name, shape, dt))
        sem = lambda name: ctx.enter_context(nc.semaphore(name))
        cols = sb("b_cols", [P, 4, T], F32)
        g1, b1, g2, b2 = (cols[:, k, :] for k in range(4))
        esum = sb("b_esum", [P, B], F32)
        ebar = sb("b_ebar", [P, B], F32)
        me = sb("b_me", [P, 1], F32)
        ed = sb("b_ed", [P, T * B], F32)
        esq = sb("b_esq", [P, 2], F32)
        vE = sb("b_vE", [P, 1], F32)
        fbar = sb("b_fbar", [P, T], F32)
        fd = sb("b_fd", [P, T, B], F32)
        fq = sb("b_fq", [P, T, B], F32)
        small = sb("b_small", [P, 16, T], F32)
        var1, ve1, r1, A, mean1, Er, Vr, t1, t2, t3, ve2, r2, A2, C2, k8, sg = (
            small[:, n, :] for n in range(16))
        ebd = sb("b_ebd", [P, B], F32)
        C = keep["C"]
        mv2 = sb("b_mv2", [P, T, 2], F32)
        st2 = sb("b_st2", [P, T, B, 12], F32)
        eb = [sb(f"b_eb{q}", [P, N], F32) for q in range(2)]
        ring = sb("b_ring", [P, RING, N], F32)
        ab = sb("b_ab", [P, 3, T], F32)
        gdc = sb("b_gdc", [P, 2, T, B], F32)
        rows = sb("b_rows", [P, 4, P], F32)
        parts = sb("b_parts", [P, 4, 3, P], BF16)
        rest = sb("b_rest", [P, 4, 2, P], F32)
        pm = ps("b_pm", [P, 512], F32)
        pt = ps("b_pt", [P, 4, P], F32)

        loaded, tab, tab_pe, tab_pow = sem("b_loaded"), sem("b_tab"), sem("b_tab_pe"), sem("b_tab_pow")
        e_stored = sem("b_e_stored")
        eb_loaded = [sem(f"b_eb_loaded{q}") for q in range(2)]
        relu_done, stats_done, ring_free = sem("b_relu_done"), sem("b_stats_done"), sem("b_ring_free")
        aggr_done, row_stored = sem("b_aggr_done"), sem("b_row_stored")
        tables_ready, e_parts_ready, rows_ready = sem("b_tables_ready"), sem("b_e_parts"), sem("b_rows_ready")
        block = ctx.enter_context(nc.Block())
        ecol, fcol, ident, ones = keep["ecol"], keep["fcol"], keep["ident"], keep["ones"]
        wide = lambda ap: ap.unsqueeze(2).to_broadcast([P, T, B])

        @block.sync
        def _(e):
            e.dma_start(cols[:], vecs.rearrange("p (k t) -> p k t", k=4)).then_inc(loaded, 16)
            e.wait_ge(e_parts_ready, 1)
            e.dma_start(e_dram, rows[:, 0, :]).then_inc(e_stored, 16)
            for r in range(3):
                for k in range(3):
                    e.dma_start(e9_dram[3 * r + k], parts[:, 0, k, :]).then_inc(row_stored, 16)
            e.wait_ge(e_stored, 16)
            load = lambda b, q: e.dma_start(
                eb[q][:].rearrange("p (t n) -> p t n", t=T),
                e_dram.rearrange("(t b) n -> b t n", b=B)[b].partition_broadcast(P)).then_inc(eb_loaded[q], 16)
            for q in range(2):
                load(q, q)
            with e.Fori(0, PAIRS - 1) as i:
                for q in range(2):
                    b = i * 2 + q
                    e.wait_ge(relu_done, b * T + T)
                    load(b + 2, q)
            e.wait_ge(rows_ready, 1)
            for kind in range(2):
                for k in range(3):
                    e.dma_start(gd_dram[kind, k], parts[:, 1 + kind, k, :]).then_inc(row_stored, 16)
                    for c in range(3):
                        e.dma_start(ab9_dram[3 * k + c, kind], parts[kind * T:(kind + 1) * T, 3, k, :]).then_inc(row_stored, 16)
            e.dma_start(s_dram, rows[2 * T:3 * T, 3, :]).then_inc(row_stored, 16)
            e.wait_ge(row_stored, 16 * (9 + 6 + 18 + 1))

        @block.gpsimd
        def _(e):
            e.wait_ge(tab, TAB_VAR1)
            e.tensor_tensor(r1, ve1, keep["minus_half"][:, 0:T], ALU.pow).then_inc(tab_pow, 1)
            e.wait_ge(tab, TAB_VAR2)
            e.tensor_tensor(r2, ve2, keep["minus_half"][:, 0:T], ALU.pow).then_inc(tab_pow, 1)

        @block.tensor
        def _(e):
            e.transpose(pt[:, 0, :], ecol[:].rearrange("p t b -> p (t b)"), ident[:]).then_inc(tab_pe, 1)
            e.wait_ge(tab, 1)
            e.matmul(pm[:, 0:B], ones[:], esum[:], start=True, stop=True).then_inc(tab_pe, 1)
            e.wait_ge(tab, TAB_ESQ)
            e.matmul(pm[:, B:B + 1], ones[:], esq[:, 0:1], start=True, stop=True).then_inc(tab_pe, 1)
            e.wait_ge(tables_ready, 1)
            for kind in range(2):
                e.transpose(pt[:, 1 + kind, :], gdc[:, kind].rearrange("p t b -> p (t b)"), ident[:])
            e.transpose(pt[0:3 * T, 3, :], ab[:].rearrange("p c t -> p (c t)"), ident[:]).then_inc(tab_pe, 1)

        @block.scalar
        def _(e):
            e.wait_ge(tab, TAB_C)
            with e.Fori(0, PAIRS) as i:
                for q in range(2):
                    b = i * 2 + q
                    e.wait_ge(eb_loaded[q], i * 16 + 16)
                    for t in range(T):
                        e.wait_ge(ring_free, b * T + t + 1)
                        e.activation(ring[:, t % RING, :], eb[q][:], ACT.Relu, bias=C[:, t, bass.ds(b, 1)],
                                     scale=A[:, t:t + 1]).then_inc(relu_done, 1)

        @block.vector
        def _(e):
            n = [0]

            def link(ins):
                n[0] += 1
                ins.then_inc(tab, 1)
                e.wait_ge(tab, n[0])

            e.sem_inc(ring_free, RING)
            link(e.tensor_reduce(esum[:], ecol[:].rearrange("p t b -> p b t"), AX, ALU.add))
            e.wait_ge(tab_pe, 1)
            link(e.tensor_copy(rows[:, 0, :], pt[:, 0, :]))
            link(e.tensor_copy(parts[:, 0, 0, :], rows[:, 0, :]))
            link(e.tensor_tensor(rest[:, 0, 0, :], rows[:, 0, :], parts[:, 0, 0, :], ALU.subtract))
            link(e.tensor_copy(parts[:, 0, 1, :], rest[:, 0, 0, :]))
            link(e.tensor_tensor(rest[:, 0, 1, :], rest[:, 0, 0, :], parts[:, 0, 1, :], ALU.subtract))
            e.tensor_copy(parts[:, 0, 2, :], rest[:, 0, 1, :]).then_inc(e_parts_ready, 1)
            e.wait_ge(tab_pe, 2)
            link(e.tensor_scalar(ebar[:], pm[:, 0:B], 1.0 / N, None, ALU.mult))
            link(e.tensor_reduce(me[:], ebar[:], AX, ALU.add))
            link(e.tensor_scalar(me[:], me[:], 1.0 / B, None, ALU.mult))
            link(e.tensor_scalar(ed[:], ecol[:].rearrange("p t b -> p (t b)"), me[:], None, ALU.subtract))
            link(e.tensor_tensor(ed[:], ed[:], ed[:], ALU.mult))
            link(e.tensor_reduce(esq[:, 0:1], ed[:], AX, ALU.add))
            assert n[0] == TAB_ESQ
            link(e.tensor_reduce(fbar[:], fcol[:], AX, ALU.add))
            link(e.tensor_scalar(fbar[:], fbar[:], 1.0 / B, None, ALU.mult))
            link(e.tensor_tensor(fd[:], fcol[:], wide(fbar[:]), ALU.subtract))
            link(e.tensor_tensor(fq[:], fd[:], fd[:], ALU.mult))
            link(e.tensor_reduce(t1, fq[:], AX, ALU.add))
            link(e.tensor_scalar(ebd[:], ebar[:], me[:], None, ALU.subtract))
            link(e.tensor_tensor(fq[:], fd[:], ebd[:].unsqueeze(1).to_broadcast([P, T, B]), ALU.mult))
            link(e.tensor_reduce(t2, fq[:], AX, ALU.add))
            link(e.scalar_tensor_tensor(t1, t2, 2.0, t1, ALU.mult, ALU.add))
            e.wait_ge(tab_pe, 3)
            link(e.tensor_scalar(vE[:], pm[:, B:B + 1], 1.0 / (N * B), None, ALU.mult))
            link(e.tensor_scalar(var1, t1, 1.0 / B, vE[:], ALU.mult, ALU.add))
            link(e.tensor_scalar(ve1, var1, EPS, None, ALU.add))
            assert n[0] == TAB_VAR1
            e.wait_ge(tab_pow, 1)
            e.wait_ge(loaded, 16)
            link(e.tensor_tensor(A, g1, r1, ALU.mult))
            link(e.tensor_scalar(mean1, fbar[:], me[:], None, ALU.add))
            link(e.tensor_tensor(C[:], fcol[:], wide(mean1), ALU.subtract))
            link(e.tensor_tensor(C[:], C[:], wide(A), ALU.mult))
            link(e.tensor_tensor(C[:], C[:], wide(b1), ALU.add))
            assert n[0] == TAB_C
            half = N // 2
            with e.Fori(0, B) as b:
                for t in range(T):
                    e.wait_ge(relu_done, b * T + t + 1)
                    e.bn_stats(st2[:, t, bass.ds(b, 1), 0:6], ring[:, t % RING, 0:half]).then_inc(stats_done, 1)
                    e.bn_stats(st2[:, t, bass.ds(b, 1), 6:12], ring[:, t % RING, half:N]).then_inc(ring_free, 1)
            e.wait_ge(stats_done, B * T)
            e.wait_ge(ring_free, B * T + RING)
            for t in range(T):
                e.bn_aggr(mv2[:, t, :], st2[:, t].rearrange("p b s -> p (b s)")).then_inc(aggr_done, 1)
            e.wait_ge(aggr_done, T)
            link(e.tensor_copy(Er, mv2[:, :, 0]))
            link(e.tensor_scalar(Vr, mv2[:, :, 1], 0.96, None, ALU.mult))
            link(e.tensor_tensor(t1, A, A, ALU.mult))
            link(e.tensor_tensor(t1, t1, var1, ALU.mult))
            link(e.scalar_tensor_tensor(t1, t1, SLOPE * SLOPE, Vr, ALU.mult, ALU.add))
            link(e.tensor_tensor(t2, Er, b1, ALU.subtract))
            link(e.tensor_tensor(t2, t2, Er, ALU.mult))
            link(e.scalar_tensor_tensor(t1, t2, 2 * SLOPE * (1 - SLOPE), t1, ALU.mult, ALU.add))
            link(e.tensor_scalar(ve2, t1, EPS, None, ALU.add))
            assert n[0] == TAB_VAR2
            e.wait_ge(tab_pow, 2)
            link(e.tensor_tensor(A2, g2, r2, ALU.mult))
            link(e.tensor_scalar(t1, b1, SLOPE, None, ALU.mult))
            link(e.scalar_tensor_tensor(t1, Er, 1 - SLOPE, t1, ALU.mult, ALU.add))
            link(e.tensor_tensor(t1, t1, A2, ALU.mult))
            link(e.tensor_tensor(C2, b2, t1, ALU.subtract))
            link(e.tensor_scalar(sg, A2, 0.0, 2.0, ALU.is_ge, ALU.mult))
            link(e.tensor_scalar(sg, sg, -1.0, None, ALU.add))
            link(e.tensor_copy(ab[:, 2, :], sg))
            link(e.tensor_tensor(k8, A2, sg, ALU.mult))
            link(e.tensor_scalar(k8, k8, 1 - SLOPE, None, ALU.mult))
            link(e.tensor_tensor(ab[:, 0, :], k8, A, ALU.mult))
            link(e.tensor_scalar(t3, A2, SLOPE, None, ALU.mult))
            link(e.tensor_tensor(ab[:, 1, :], t3, A, ALU.mult))
            link(e.tensor_tensor(gdc[:, 0], C[:], wide(k8), ALU.mult))
            link(e.tensor_tensor(gdc[:, 1], C[:], wide(t3), ALU.mult))
            e.tensor_tensor(gdc[:, 1], gdc[:, 1], wide(C2), ALU.add).then_inc(tables_ready, 1)
            e.wait_ge(tab_pe, 4)
            for r, rows_used in ((1, P), (2, P), (3, 3 * T)):
                link(e.tensor_copy(rows[0:rows_used, r, :], pt[0:rows_used, r, :]))
                link(e.tensor_copy(parts[0:rows_used, r, 0, :], rows[0:rows_used, r, :]))
                link(e.tensor_tensor(rest[0:rows_used, r, 0, :], rows[0:rows_used, r, :], parts[0:rows_used, r, 0, :], ALU.subtract))
                link(e.tensor_copy(parts[0:rows_used, r, 1, :], rest[0:rows_used, r, 0, :]))
                link(e.tensor_tensor(rest[0:rows_used, r, 1, :], rest[0:rows_used, r, 0, :], parts[0:rows_used, r, 1, :], ALU.subtract))
                last = e.tensor_copy(parts[0:rows_used, r, 2, :], rest[0:rows_used, r, 1, :])
                if r < 3:
                    link(last)
            last.then_inc(rows_ready, 1)


TAB_ESQ = 12
TAB_VAR1 = TAB_ESQ + 12
TAB_C = TAB_VAR1 + 5
TAB_VAR2 = TAB_C + 9


def attend_block(nc, S, adj, keep, wh_dram, e9_dram, ab9_dram, gd_dram, s_dram, hp_dram, g3b3):
    B, N, D, T, KD = S.B, S.N, S.D, S.T, S.KD
    ADJ = 4
    with ExitStack() as ctx:
        sb = lambda name, shape, dt: ctx.enter_context(nc.sbuf_tensor(name, shape, dt))
        ps = lambda name, shape, dt: ctx.enter_context(nc.psum_tensor(name, shape, dt))
        sem = lambda name: ctx.enter_context(nc.semaphore(name))
        ident = keep["ident"]
        erow = [sb(f"c_erow{q}", [P, N], BF16) for q in range(2)]
        lrow = [sb(f"c_lrow{q}", [P, 2, N], BF16) for q in range(2)]
        srow = sb("c_srow", [P, N], F32)
        wh = [sb(f"c_wh{q}", [P, 2, T, D], F16) for q in range(2)]
        adjr = sb("c_adjr", [P, ADJ, N], F32)
        relu = sb("c_relu", [P, 2, N], F32)
        logit = sb("c_logit", [P, 2, N], F32)
        prob = sb("c_prob", [P, 2, N], F32)
        masked = sb("c_masked", [P, 2, N], F32)
        negmax = sb("c_negmax", [P, 2], F32)
        rowsum = sb("c_rowsum", [P, 4], F32)
        rinv = sb("c_rinv", [P, 4], F32)
        pth = sb("c_pth", [P, 2, T, P], F16)
        ptl = sb("c_ptl", [P, 2, T, P], F16)
        hp = [sb(f"c_hp{q}", [P, T, D], F32) for q in range(2)]
        st3 = sb("c_st3", [P, KD, B * T // 2, 6], F32)
        mv3 = sb("c_mv3", [P, KD, 2], F32)
        sc3 = sb("c_sc3", [P, 6, KD], F32)
        g3b3_sb = sb("c_g3b3", [P, 2, KD], F32)
        diag = sb("c_diag", [P, 2, KD, P], F32)
        p_relu = ps("c_p_relu", [P, N], F32)
        p_lin = ps("c_p_lin", [P, N], F32)
        p_t = ps("c_p_t", [P, T, P], F32)
        p_o = ps("c_p_o", [P, 512], F32)
        p_s = ps("c_p_s", [P, KD, 2 * P], F32)

        rows_cleared = sem("c_rows_cleared")
        const_loaded = sem("c_const_loaded")
        rows_loaded = [sem(f"c_rows_loaded{q}") for q in range(2)]
        wh_loaded = [sem(f"c_wh_loaded{q}") for q in range(2)]
        adj_loaded = [sem(f"c_adj_loaded{k}") for k in range(ADJ)]
        lin_done, relu_done, signed_done = sem("c_lin_done"), sem("c_relu_done"), sem("c_signed_done")
        logit_done, prob_done, masked_done = sem("c_logit_done"), sem("c_prob_done"), sem("c_masked_done")
        pt_done, pth_done, ptl_done = sem("c_pt_done"), sem("c_pth_done"), sem("c_ptl_done")
        pv_done, rinv_done, hp_done = sem("c_pv_done"), sem("c_rinv_done"), sem("c_hp_done")
        ht_done, st3_done = sem("c_ht_done"), sem("c_st3_done")
        hp_stored = [sem(f"c_hp_stored{q}") for q in range(2)]
        fin, fin_pow, fin_pe = sem("c_fin"), sem("c_fin_pow"), sem("c_fin_pe")
        block = ctx.enter_context(nc.Block())
        TILES = B * T

        def pairs(e, step):
            with e.Fori(0, B // 2) as i:
                for q in range(2):
                    step(i, q, i * 2 + q)

        @block.sync
        def _(e):
            e.dma_start(srow[:].rearrange("p (t n) -> p t n", t=T),
                        s_dram.partition_broadcast(P)).then_inc(const_loaded, 16)
            e.dma_start(g3b3_sb[:], g3b3.rearrange("p (c k) -> p c k", c=2)).then_inc(const_loaded, 16)
            e.wait_ge(rows_cleared, 4)
            for q in range(2):
                e.dma_start(lrow[q][0:9].rearrange("r c n -> r (c n)"),
                            ab9_dram.rearrange("r c t n -> r (c t n)")).then_inc(const_loaded, 16)

            def load_rows(b, q):
                e.dma_start(erow[q][0:9].rearrange("r (t n) -> r t n", t=T),
                            e9_dram.rearrange("r (t b) n -> b r t n", b=B)[b]).then_inc(rows_loaded[q], 16)
                for kind in range(2):
                    e.dma_start(lrow[q][9:12, kind].rearrange("r (t n) -> r t n", t=T),
                                gd_dram[kind].rearrange("r (t b) n -> b r t n", b=B)[b]).then_inc(rows_loaded[q], 16)
                e.dma_start(wh[q][:], wh_dram[b]).then_inc(wh_loaded[q], 16)

            for q in range(2):
                load_rows(q, q)
            def store(b, q):
                e.wait_ge(hp_done, b * T + T)
                e.dma_start(hp_dram[b], hp[q][:]).then_inc(hp_stored[q], 16)

            with e.Fori(0, B // 2 - 1) as i:
                for q in range(2):
                    b = i * 2 + q
                    e.wait_ge(pv_done, b * T + T)
                    load_rows(b + 2, q)
                    store(b, q)
            for q in range(2):
                store(B - 2 + q, q)

        @block.gpsimd
        def _(e):
            for q in range(2):
                e.memset(erow[q][:], 1.0).then_inc(rows_cleared, 1)
                e.memset(lrow[q][:], 0.0).then_inc(rows_cleared, 1)
            load = lambda b, t: e.dma_start(
                adjr[:, t % ADJ, :], adj[b, t * P:(t + 1) * P, :]).then_inc(adj_loaded[t % ADJ], 16)

            def mask(b, t):
                g = b * T + t
                e.wait_ge(prob_done, g + 1)
                e.wait_ge(adj_loaded[t % ADJ], (b * (T // ADJ) + t // ADJ + 1) * 16)
                after(e, pt_done, g - 1)
                e.tensor_tensor(masked[:, t % 2, :], prob[:, t % 2, :], adjr[:, t % ADJ, :],
                                ALU.mult).then_inc(masked_done, 1)

            for t in range(ADJ):
                load(0, t)

            def graph(b, last=False):
                for t in range(T):
                    mask(b, t)
                    e.wait_ge(masked_done, b * T + t + 1)
                    if t + ADJ < T:
                        load(b, t + ADJ)
                    elif not last:
                        load(b + 1, t + ADJ - T)

            graph(0)
            with e.Fori(1, B - 1) as b:
                graph(b)
            graph(B - 1, last=True)
            e.wait_ge(fin, FIN_VAR)
            e.tensor_tensor(sc3[:, 1, :], sc3[:, 0, :], keep["minus_half"][:, 0:KD], ALU.pow).then_inc(fin_pow, 1)

        @block.tensor
        def _(e):
            e.wait_ge(const_loaded, 64)

            def lin(b, q, i, t):
                g = b * T + t
                if t == 0:
                    e.wait_ge(rows_loaded[q], i * 48 + 48)
                e.wait_ge(relu_done, g)
                for h in range(2):
                    e.matmul(p_relu[:, h * 512:(h + 1) * 512], erow[q][:, t * P:(t + 1) * P],
                             lrow[q][:, 0, h * 512:(h + 1) * 512], start=True, stop=True)
                e.wait_ge(logit_done, g)
                for h in range(2):
                    mm = e.matmul(p_lin[:, h * 512:(h + 1) * 512], erow[q][:, t * P:(t + 1) * P],
                                  lrow[q][:, 1, h * 512:(h + 1) * 512], start=True, stop=True)
                mm.then_inc(lin_done, 1)

            def turn(g, t):
                e.wait_ge(masked_done, g + 1)
                e.wait_ge(ptl_done, g)
                for j in range(T):
                    mm = e.transpose(p_t[:, j, :], masked[:, t % 2, j * P:(j + 1) * P], ident[:])
                mm.then_inc(pt_done, 1)

            def pv(g, q, i, t):
                if t == 0:
                    e.wait_ge(wh_loaded[q], i * 16 + 16)
                e.wait_ge(ptl_done, g + 1)
                e.wait_ge(hp_done, g)
                parts = [(pp, w, j) for j in range(T) for pp, w in ((pth, 0), (pth, 1), (ptl, 0))]
                for n, (pp, w, j) in enumerate(parts):
                    mm = e.matmul(p_o[:, 0:D], pp[:, t % 2, j, :], wh[q][:, w, j, :],
                                  start=(n == 0), stop=(n == len(parts) - 1))
                mm.then_inc(pv_done, 1)

            def flip(g, q, t):
                e.wait_ge(hp_done, g + 1)
                if t % 2 == 0:
                    e.wait_ge(st3_done, g)
                for k in range(KD):
                    mm = e.transpose(p_s[:, k, (t % 2) * P:(t % 2 + 1) * P], hp[q][:, t, k * P:(k + 1) * P], ident[:])
                if t % 2:
                    mm.then_inc(ht_done, 1)

            LAGS = ((2, turn), (3, pv), (4, flip))

            def slot(i, q, t, first=False):
                b = i * 2 + q
                lin(b, q, i, t)
                for lag, what in LAGS:
                    if first and t < lag:
                        continue
                    tt = (t - lag) % T
                    late = t < lag
                    g = b * T + t - lag
                    if what is turn:
                        turn(g, tt)
                    elif what is pv:
                        if late:
                            pv(g, 1 - q, i if q else i - 1, tt)
                        else:
                            pv(g, q, i, tt)
                    else:
                        flip(g, 1 - q if late else q, tt)

            for q in range(2):
                for t in range(T):
                    slot(0, q, t, first=(q == 0))
            with e.Fori(1, B // 2) as i:
                for q in range(2):
                    for t in range(T):
                        slot(i, q, t)
            for t in range(4):
                for lag, what in LAGS:
                    if t < lag:
                        g, tt = TILES + t - lag, T + t - lag
                        if what is turn:
                            turn(g, tt)
                        elif what is pv:
                            pv(g, 1, B // 2 - 1, tt)
                        else:
                            flip(g, 1, tt)
            e.wait_ge(fin, FIN_DIAG)
            for c in range(2):
                for k in range(KD):
                    mm = e.matmul(p_relu[:, (c * KD + k) * P:(c * KD + k + 1) * P], keep["ones"][:],
                                  diag[:, c, k, :], start=True, stop=True)
            mm.then_inc(fin_pe, 1)

        @block.scalar
        def _(e):
            def relus(b, t):
                g = b * T + t
                e.wait_ge(lin_done, g + 1)
                after(e, logit_done, g - 1)
                e.activation(relu[:, t % 2, :], p_relu[:], ACT.Relu).then_inc(relu_done, 1)

            def exps(b, t):
                g = b * T + t
                e.wait_ge(logit_done, g + 1)
                after(e, masked_done, g - 1)
                after(e, rinv_done, g - 3)
                e.activation(prob[:, t % 2, :], logit[:, t % 2, :], ACT.Exp, bias=negmax[:, t % 2:t % 2 + 1],
                             scale=-1.0, accum_out=rowsum[:, t % 4:t % 4 + 1]).then_inc(prob_done, 1)

            def highs(g, t):
                e.wait_ge(pt_done, g + 1)
                after(e, pv_done, g - 1)
                e.activation(pth[:, t % 2], p_t[:], ACT.Copy).then_inc(pth_done, 1)

            def graph(b, first=False):
                for t in range(T):
                    relus(b, t)
                    if not (first and t < 2):
                        highs(b * T + t - 2, (t - 2) % T)
                    exps(b, t)
            graph(0, True)
            with e.Fori(1, B) as b:
                graph(b)
            for t in range(2):
                highs(TILES + t - 2, T + t - 2)

        @block.vector
        def _(e):
            def inverse(g, t):
                e.reciprocal(rinv[:, t % 4:t % 4 + 1], rowsum[:, t % 4:t % 4 + 1]).then_inc(rinv_done, 1)

            def logits(b, t):
                g = b * T + t
                e.wait_ge(relu_done, g + 1)
                e.tensor_tensor(relu[:, t % 2, :], relu[:, t % 2, :], srow[:], ALU.mult).then_inc(signed_done, 1)
                e.wait_ge(signed_done, g + 1)
                after(e, prob_done, g - 1)
                if not isinstance(g, int) or g >= 2:
                    inverse(g - 2, (t - 2) % T)
                e.tensor_tensor_reduce(logit[:, t % 2, :], relu[:, t % 2, :], p_lin[:], -1.0, BIG,
                                       ALU.add, ALU.min, negmax[:, t % 2:t % 2 + 1]).then_inc(logit_done, 1)

            def lows(g, t):
                e.wait_ge(pth_done, g + 1)
                after(e, pv_done, g - 1)
                e.tensor_tensor(ptl[:, t % 2], p_t[:], pth[:, t % 2], ALU.subtract).then_inc(ptl_done, 1)

            def outs(g, q, i, t):
                if t == 0 and not isinstance(i, int):
                    e.wait_ge(hp_stored[q], i * 16)
                    e.wait_ge(ht_done, (i * 2 + q - 1) * (T // 2))
                e.wait_ge(rinv_done, g + 1)
                e.wait_ge(pv_done, g + 1)
                e.tensor_scalar(hp[q][:, t, :], p_o[:, 0:D], rinv[:, t % 4:t % 4 + 1], None,
                                ALU.mult).then_inc(hp_done, 1)

            def stats(g2, n):
                e.wait_ge(ht_done, g2)
                for k in range(KD):
                    e.bn_stats(st3[:, k, n, :] if isinstance(n, int) else st3[:, k, bass.ds(n, 1), :],
                               p_s[:, k, :]).then_inc(st3_done, 1)

            def slot(i, q, t, first=False):
                b = i * 2 + q
                logits(b, t)
                if not (first and t < 2):
                    lows(b * T + t - 2, (t - 2) % T)
                if not (first and t < 3):
                    late = t < 3
                    outs(b * T + t - 3, 1 - q if late else q, (i if q else i - 1) if late else i, (t - 3) % T)
                if t % 2 == 1 and not (first and t < 5):
                    n = b * (T // 2) + (t - 5) // 2
                    stats(n + 1, n)

            for q in range(2):
                for t in range(T):
                    slot(0, q, t, first=(q == 0))
            with e.Fori(1, B // 2) as i:
                for q in range(2):
                    for t in range(T):
                        slot(i, q, t)
            for t in range(3):
                if t < 2:
                    e.wait_ge(prob_done, TILES + t - 1)
                    inverse(TILES + t - 2, T + t - 2)
                    lows(TILES + t - 2, T + t - 2)
                outs(TILES + t - 3, 1, B // 2 - 1, T + t - 3)
                if t == 1:
                    stats(TILES // 2 - 1, TILES // 2 - 2)
            stats(TILES // 2, TILES // 2 - 1)
            e.wait_ge(st3_done, TILES)
            n = [0]

            def link(ins):
                n[0] += 1
                ins.then_inc(fin, 1)
                e.wait_ge(fin, n[0])
            for k in range(KD):
                link(e.bn_aggr(mv3[:, k, :], st3[:, k].rearrange("p n s -> p (n s)")))
            link(e.tensor_scalar(sc3[:, 0, :], mv3[:, :, 1], EPS, None, ALU.add))
            assert n[0] == FIN_VAR
            e.wait_ge(fin_pow, 1)
            link(e.tensor_tensor(sc3[:, 2, :], g3b3_sb[:, 0, :], sc3[:, 1, :], ALU.mult))
            link(e.tensor_tensor(sc3[:, 3, :], mv3[:, :, 0], sc3[:, 2, :], ALU.mult))
            link(e.tensor_tensor(sc3[:, 4, :], g3b3_sb[:, 1, :], sc3[:, 3, :], ALU.subtract))
            for c, src in ((0, 2), (1, 4)):
                for k in range(KD):
                    link(e.tensor_scalar(diag[:, c, k, :], ident[:], sc3[:, src, k:k + 1], None, ALU.mult))
            assert n[0] == FIN_DIAG
            e.wait_ge(fin_pe, 1)
            link(e.tensor_copy(keep["norm3"][:].rearrange("p c d -> p (c d)"), p_relu[:, 0:2 * D]))
            for q in range(2):
                e.wait_ge(hp_stored[q], 16 * (B // 2))


FIN_VAR = 3
FIN_DIAG = FIN_VAR + 3 + 4


def layers_block(nc, S, x, adj, adj_t, mask, w1, w2, wl2, w3, b1c, b2r, b3r, eps, keep, hp_dram, out):
    B, N, D, T, KD, H, KH = S.B, S.N, S.D, S.T, S.KD, S.H, S.KH
    PAIRS = B // 2
    BANKS = 4
    RING = 3
    LNS = 6

    order = []
    for q in range(2):
        order += [("agg", q, d) for d in range(KD)] + [("hid", q, f) for f in range(KH)]
        order += [("mlp", q, g) for g in range(2)]
    for q in range(2):
        order += [("hi2", q, 0), ("lo2", q, 0)] + [("int", q, d) for d in range(KD)]
        for s in range(T + 2):
            order += [("sim", q, s)] if s < T else []
            order += [("turn", q, s - 1)] if 1 <= s <= T else []
            order += [("pv", q, s - 2)] if s >= 2 else []
    for q in range(2):
        order += [("hi3", q, 0), ("lo3", q, 0)] + [("sup", q, g) for g in range(2)]
        order += [("out", q, g) for g in range(2)]
    place = {key: n for n, key in enumerate(order)}
    COUNT = len(order)
    assert COUNT % BANKS == 0

    with ExitStack() as ctx:
        sb = lambda name, shape, dt: ctx.enter_context(nc.sbuf_tensor(name, shape, dt))
        ps = lambda name, shape, dt: ctx.enter_context(nc.psum_tensor(name, shape, dt))
        sem = lambda name: ctx.enter_context(nc.semaphore(name))
        ident, ident16, norm3 = keep["ident"], keep["ident16"], keep["norm3"]
        two = lambda name, shape, dt: [sb(f"d_{name}{q}", shape, dt) for q in range(2)]
        xs = two("x", [P, T, D], F32)
        adjt = two("adjt", [P, T, N], F16)
        hh, hl = two("hh", [P, T, D], F16), two("hl", [P, T, D], F16)
        hth, htl = two("hth", [P, KD, N], F16), two("htl", [P, KD, N], F16)
        zh, zl = two("zh", [P, KD, N], F16), two("zl", [P, KD, N], F16)
        hidh, hidl = two("hidh", [P, KH, N], F16), two("hidl", [P, KH, N], F16)
        suph = [hidh[q][:].rearrange("p f n -> p (f n)")[:, 0:T * D].rearrange("p (t d) -> p t d", t=T) for q in range(2)]
        supl = [hidl[q][:].rearrange("p f n -> p (f n)")[:, 0:T * D].rearrange("p (t d) -> p t d", t=T) for q in range(2)]
        kept, nomask = two("kept", [P, N], BF16), two("nomask", [P, N], BF16)
        negrow = two("negrow", [P, N], BF16)
        maski = sb("d_maski", [P, N], I32)
        z = sb("d_z", [P, T, D], F32)
        tmp = sb("d_tmp", [P, T, D], F32)
        hid32 = tmp[:].rearrange("p t d -> p (t d)").rearrange("p (a n) -> p a n", a=2)
        adjr = sb("d_adjr", [P, RING, N], F32)
        y = sb("d_y", [P, 2, N], F32)
        pth, ptl = sb("d_pth", [P, 2, T, P], F16), sb("d_ptl", [P, 2, T, P], F16)
        w1h, w1l = sb("d_w1h", [P, KD, H], F16), sb("d_w1l", [P, KD, H], F16)
        w2h, w2l = sb("d_w2h", [P, KH, D], F16), sb("d_w2l", [P, KH, D], F16)
        wlh, wll = sb("d_wlh", [P, KD, D], F16), sb("d_wll", [P, KD, D], F16)
        w3h, w3l = sb("d_w3h", [P, KD, D], F16), sb("d_w3l", [P, KD, D], F16)
        b1 = sb("d_b1", [P, KH], F32)
        bias16 = sb("d_bias16", [P, 2, D], F16)
        bias_lo = sb("d_bias_lo", [P, 2, D], F16)
        ones16 = sb("d_ones16", [P, P], F16)
        onesb = sb("d_onesb", [P, P], BF16)
        eps1 = sb("d_eps1", [P, 1], F32)
        diah, dial = sb("d_diah", [P, P], F16), sb("d_dial", [P, P], F16)
        st, small, sums = sb("d_st", [P, T, 6], F32), sb("d_small", [P, 4, T], F32), sb("d_sums", [P, T], F32)
        ve, rstd, shift = (sb(f"d_{n}", [P, T], F32) for n in ("ve", "rstd", "shift"))
        rowmax, negmax = sb("d_rowmax", [P, 2], F32), sb("d_negmax", [P, 2], F32)
        rowsum, rinv = sb("d_rowsum", [P, 4], F32), sb("d_rinv", [P, 2], F32)
        hold = sb("d_hold", [P, 1], F32)
        bank = [ps(f"d_bank{k}", [P, N], F32) for k in range(BANKS)]
        stage32 = tmp[:].rearrange("p t d -> p (t d)")
        bias32 = z[:].rearrange("p t d -> p (t d)")[:, 0:2 * D].rearrange("p (c d) -> p c d", c=2)
        dia32 = z[:].rearrange("p t d -> p (t d)")[:, 2 * D:2 * D + P]

        w_loaded, w_hi, w_lo, setup = sem("d_w_loaded"), sem("d_w_hi"), sem("d_w_lo"), sem("d_setup")
        cleared = sem("d_cleared")
        bias_moved = sem("d_bias_moved")
        z_loaded, z_scaled, z_ready, z_min, z_exp, z_used = (
            sem(f"d_{n}") for n in ("z_loaded", "z_scaled", "z_ready", "z_min", "z_exp", "z_used"))
        x_loaded = [sem(f"d_x_loaded{q}") for q in range(2)]
        x_first = sem("d_x_first")
        adjt_loaded = [sem(f"d_adjt_loaded{q}") for q in range(2)]
        row_loaded = [sem(f"d_row_loaded{k}") for k in range(RING)]
        row_kept, row_masked = sem("d_row_kept"), sem("d_row_masked")
        mask_loaded, mask_ready, neg_ready = sem("d_mask_loaded"), sem("d_mask_ready"), sem("d_neg_ready")
        ln_stats, ln_small, ln_var = sem("d_ln_stats"), sem("d_ln_small"), sem("d_ln_var")
        ln_rstd, ln_shift = sem("d_ln_rstd"), sem("d_ln_shift")
        h_ready, hh_ready, hl_ready = sem("d_h_ready"), sem("d_hh_ready"), sem("d_hl_ready")
        bank_full, bank_free = sem("d_bank_full"), sem("d_bank_free")
        hi_done = sem("d_hi_done")
        hid32_done = sem("d_hid32_done")
        max_done, prob_done, rinv_done = sem("d_max_done"), sem("d_prob_done"), sem("d_rinv_done")
        held = sem("d_held")
        stored = [sem(f"d_stored{q}") for q in range(2)]
        block = ctx.enter_context(nc.Block())

        his, HIS = {}, 0
        for key in order:
            if key[0] in ("agg", "hid", "int", "turn", "sup"):
                HIS += 1
                his[key] = HIS
        full = lambda i, key: i * COUNT + place[key] + 1
        free = lambda i, key: i * COUNT + place[key] + 1 + BANKS
        hi = lambda i, key: i * HIS + his[key]
        tile = lambda key: bank[place[key] % BANKS]
        ln = lambda i, layer, q: i * LNS + 2 * (layer - 1) + q
        sims = lambda i, q, s: (i * 2 + q) * T + s

        @block.sync
        def _(e):
            for n, (src, k, width) in enumerate(((w1, KD, H), (w2, KH, D), (wl2, KD, D), (w3, KD, D))):
                e.wait_ge(w_lo, n) if n else None
                e.dma_start(stage32[:, 0:k * width].rearrange("p (k o) -> p k o", k=k),
                            src.rearrange("(k p) o -> p k o", p=P)).then_inc(w_loaded, 16)
            e.dma_start(bias32[0:1, 0, :], b2r).then_inc(bias_moved, 16)
            e.dma_start(bias32[0:1, 1, :], b3r).then_inc(bias_moved, 16)
            e.dma_start(b1[:], b1c).then_inc(bias_moved, 16)
            e.dma_start(eps1[:], eps.partition_broadcast(P)).then_inc(bias_moved, 16)
            e.wait_ge(setup, 3)
            e.dma_start(bias16[1:2, :, :], bias_lo[0:1, :, :]).then_inc(bias_moved, 16)
            e.wait_ge(setup, 6)

            with e.Fori(0, PAIRS) as i:
                for q in range(2):
                    b = i * 2 + q
                    e.wait_ge(z_used, b)
                    e.dma_start(z[:], hp_dram[b]).then_inc(z_loaded, 16)
                    e.wait_ge(stored[q], i * 16)
                    e.dma_start(xs[q][:], x[b].rearrange("(t p) d -> p t d", p=P)).then_inc(x_loaded[q], 16)
                    e.wait_ge(neg_ready, b)
                    e.dma_start(maski[:], mask[b].partition_broadcast(P)).then_inc(mask_loaded, 16)
                for q in range(2):
                    for s in range(T):
                        g = q * T + s
                        if g >= RING:
                            p = g - RING
                            e.wait_ge(bank_free, free(i, ("sim", p // T, p % T)))
                        e.dma_start(adjr[:, g % RING, :], adj[i * 2 + q, s * P:(s + 1) * P, :]).then_inc(row_loaded[g % RING], 16)
                for q in range(2):
                    e.wait_ge(bank_free, free(i, ("out", q, 1)))
                    e.dma_start(out[i * 2 + q].rearrange("(t p) d -> p t d", p=P), xs[q][:]).then_inc(stored[q], 16)
            for q in range(2):
                e.wait_ge(stored[q], 16 * PAIRS)

        ROWS = [len([g for g in range(2 * T) if g % RING == k]) for k in range(RING)]

        @block.gpsimd
        def _(e):
            e.memset(ones16[:], 1.0).then_inc(cleared, 1)
            e.memset(onesb[:], 1.0).then_inc(cleared, 1)
            e.memset(bias16[:], 0.0).then_inc(cleared, 1)
            for q in range(2):
                e.memset(negrow[q][:], 0.0).then_inc(cleared, 1)

            def load_adjt(b, q):
                e.dma_start(adjt[q][:], adj_t[b].rearrange("(t p) n -> p t n", p=P)).then_inc(adjt_loaded[q], 16)

            def rstds(n):
                e.wait_ge(ln_var, n + 1)
                e.wait_ge(h_ready, n * T)
                e.tensor_tensor(rstd[:], ve[:], keep["minus_half"][:, 0:T], ALU.pow).then_inc(ln_rstd, 1)

            for q in range(2):
                load_adjt(q, q)
            def pair(i, last=False):
                for q in range(2):
                    b = i * 2 + q
                    e.wait_ge(z_loaded, b * 16 + 16)
                    e.tensor_tensor(z[:], z[:], norm3[:, 0, :].unsqueeze(1).to_broadcast([P, T, D]), ALU.mult).then_inc(z_scaled, 1)
                    e.wait_ge(z_scaled, b + 1)
                    e.tensor_tensor(z[:], z[:], norm3[:, 1, :].unsqueeze(1).to_broadcast([P, T, D]), ALU.add).then_inc(z_ready, 1)
                    rstds(ln(i, 1, q))
                for q in range(2):
                    rstds(ln(i, 2, q))
                for q in range(2):
                    e.wait_ge(mask_ready, 2 * (i * 2 + q + 1))
                    for s in range(T):
                        g = q * T + s
                        e.wait_ge(row_loaded[g % RING], i * (16 * ROWS[g % RING]) + 16 * (g // RING + 1))
                        row = adjr[:, g % RING, :]
                        e.tensor_tensor(row, row, kept[q][:], ALU.mult).then_inc(row_kept, 1)
                        e.wait_ge(row_kept, sims(i, q, s) + 1)
                        e.tensor_tensor(row, row, nomask[q][:], ALU.add).then_inc(row_masked, 1)
                    rstds(ln(i, 3, q))
                if not last:
                    for q in range(2):
                        e.wait_ge(bank_full, full(i, ("out", q, 1)))
                        load_adjt(i * 2 + q + 2, q)

            with e.Fori(0, PAIRS - 1) as i:
                pair(i)
            pair(PAIRS - 1, last=True)

        @block.tensor
        def _(e):
            def into(i, key):
                e.wait_ge(bank_free, i * COUNT + place[key] + 1)
                return tile(key)

            def products(dst, parts, last):
                for n, (a, m) in enumerate(parts):
                    mm = e.matmul(dst, a, m, start=(n == 0), stop=(n == len(parts) - 1))
                if last:
                    mm.then_inc(bank_full, 1)

            halves = [slice(h * 512, (h + 1) * 512) for h in range(N // 512)]
            cut = lambda n: slice(n * P, (n + 1) * P)
            e.wait_ge(cleared, 5)
            e.wait_ge(setup, 6)

            def layer1(i, q):
                e.wait_ge(adjt_loaded[q], i * 16 + 16)
                e.wait_ge(hl_ready, ln(i, 1, q) + 1)
                for d in range(KD):
                    key = ("agg", q, d)
                    dst = into(i, key)
                    for h, half in enumerate(halves):
                        blocks = range(h * T // 2, (h + 1) * T // 2)
                        for t in blocks:
                            for a, dia in ((hh[q], diah), (hh[q], dial), (hl[q], diah)):
                                e.matmul(dst[:, cut(t)], a[:, t, cut(d)], dia[:], stop=False, skip_group_check=True,
                                         start=(t == blocks[0] and a is hh[q] and dia is diah))
                        for t in range(T):
                            for a in (hh[q], hl[q]):
                                mm = e.matmul(dst[:, half], a[:, t, cut(d)], adjt[q][:, t, half], start=False,
                                              stop=(t == T - 1 and a is hl[q]), skip_group_check=True)
                    mm.then_inc(bank_full, 1)
                e.wait_ge(bank_free, free(i, ("agg", q, KD - 1)))
                for f in range(KH):
                    dst = into(i, ("hid", q, f))
                    for h, half in enumerate(halves):
                        products(dst[:, half], [(w[:, k, cut(f)], m[q][:, k, half]) for k in range(KD)
                                                for w, m in ((w1h, zh), (w1h, zl), (w1l, zh))], h == len(halves) - 1)
                e.wait_ge(bank_free, free(i, ("hid", q, KH - 1)))
                for g in range(2):
                    dst = into(i, ("mlp", q, g))
                    for t in range(T // 2):
                        parts = [(a[q][:, f, cut(g * T // 2 + t)], w[:, f, :]) for f in range(KH)
                                 for a, w in ((hidh, w2h), (hidh, w2l), (hidl, w2h))]
                        products(dst[:, t * D:(t + 1) * D], parts + [(ones16[:], bias16[:, 0, :])], t == T // 2 - 1)

            def turns(i, q, layer):
                for name, src, ready in (("hi", hh[q], hh_ready), ("lo", hl[q], hl_ready)):
                    dst = into(i, (f"{name}{layer}", q, 0))
                    dst = dst[:].bitcast(F16).rearrange("p (k n) -> p k n", k=KD)
                    e.wait_ge(ready, ln(i, layer, q) + 1)
                    for k in range(KD):
                        for t in range(T):
                            mm = e.transpose(dst[:, k, cut(t)], src[:, t, cut(k)], ident16[:])
                    mm.then_inc(bank_full, 1)
                e.wait_ge(bank_free, free(i, (f"lo{layer}", q, 0)))

            def layer2(i, q):
                turns(i, q, 2)
                for d in range(KD):
                    dst = into(i, ("int", q, d))
                    for h, half in enumerate(halves):
                        products(dst[:, half], [(w[:, k, cut(d)], m[q][:, k, half]) for k in range(KD)
                                                for w, m in ((wlh, hth), (wlh, htl), (wll, hth))], h == len(halves) - 1)
                e.wait_ge(bank_free, free(i, ("int", q, KD - 1)))
                e.wait_ge(neg_ready, i * 2 + q + 1)
                for s in range(T + 2):
                    if s < T:
                        dst = into(i, ("sim", q, s))
                        for h, half in enumerate(halves):
                            parts = [(a[q][:, k, cut(s)], m[q][:, k, half]) for k in range(KD)
                                     for a, m in ((zh, hth), (zh, htl), (zl, hth))]
                            products(dst[:, half], parts + [(onesb[:], negrow[q][:, half])], h == len(halves) - 1)
                    if 1 <= s <= T:
                        r = s - 1
                        dst = into(i, ("turn", q, r))
                        e.wait_ge(prob_done, sims(i, q, r) + 1)
                        for t in range(T):
                            mm = e.transpose(dst[:, cut(t)], y[:, r % 2, cut(t)], ident[:])
                        mm.then_inc(bank_full, 1)
                    if s >= 2:
                        r = s - 2
                        dst = into(i, ("pv", q, r))
                        e.wait_ge(bank_free, free(i, ("turn", q, r)))
                        products(dst[:, 0:D], [(a[:, r % 2, t, :], m[q][:, t, :]) for t in range(T)
                                               for a, m in ((pth, hh), (pth, hl), (ptl, hh))], True)

            def layer3(i, q):
                turns(i, q, 3)
                for g in range(2):
                    dst = into(i, ("sup", q, g))
                    for t in range(T // 2):
                        products(dst[:, t * D:(t + 1) * D],
                                 [(a[q][:, k, cut(g * T // 2 + t)], w[:, k, :]) for k in range(KD)
                                  for a, w in ((hth, w3h), (hth, w3l), (htl, w3h))], t == T // 2 - 1)
                e.wait_ge(bank_free, free(i, ("sup", q, 1)))
                for g in range(2):
                    dst = into(i, ("out", q, g))
                    for t in range(T // 2):
                        parts = [(adjt[q][:, m, cut(g * T // 2 + t)], sp[:, m, :]) for m in range(T) for sp in (suph[q], supl[q])]
                        products(dst[:, t * D:(t + 1) * D], parts + [(ones16[:], bias16[:, 1, :])], t == T // 2 - 1)

            with e.Fori(0, PAIRS) as i:
                for layer in (layer1, layer2, layer3):
                    for q in range(2):
                        layer(i, q)

        @block.scalar
        def _(e):
            def norm(i, layer, q):
                n = ln(i, layer, q)
                e.wait_ge(ln_shift, n + 1)
                for t in range(T):
                    e.activation(tmp[:, t, :], xs[q][:, t, :], ACT.Relu, bias=shift[:, t:t + 1],
                                 scale=rstd[:, t:t + 1]).then_inc(h_ready, 1)
                e.wait_ge(h_ready, n * T + T)
                e.activation(hh[q][:], tmp[:], ACT.Copy).then_inc(hh_ready, 1)

            def high(i, key, dst, src, func=ACT.Copy, **more):
                e.wait_ge(bank_full, full(i, key))
                e.activation(dst, src, func, **more).then_inc(hi_done, 1)

            with e.Fori(0, PAIRS) as i:
                for q in range(2):
                    e.wait_ge(z_min, i * 2 + q + 1)
                    e.activation(tmp[:], tmp[:], ACT.Exp).then_inc(z_exp, 1)
                    norm(i, 1, q)
                for q in range(2):
                    for d in range(KD):
                        high(i, ("agg", q, d), zh[q][:, d, :], tile(("agg", q, d))[:])
                    for f in range(KH):
                        key = ("hid", q, f)
                        high(i, key, hidh[q][:, f, :], tile(key)[:], ACT.Relu, bias=b1[:, f:f + 1])
                        if f >= 2:
                            e.wait_ge(bank_free, free(i, ("hid", q, f - 2)))
                        else:
                            e.wait_ge(hl_ready, ln(i, 2, q))
                        e.activation(hid32[:, f % 2, :], tile(key)[:], ACT.Relu, bias=b1[:, f:f + 1]).then_inc(hid32_done, 1)
                    norm(i, 2, q)
                for q in range(2):
                    for d in range(KD):
                        high(i, ("int", q, d), zh[q][:, d, :], tile(("int", q, d))[:])
                    for s in range(T + 1):
                        if s >= 1:
                            r = s - 1
                            if r >= 2:
                                e.wait_ge(bank_full, full(i, ("pv", q, r - 2)))
                            key = ("turn", q, r)
                            high(i, key, pth[:, r % 2], tile(key)[:].rearrange("p (t n) -> p t n", t=T))
                        if s < T:
                            e.wait_ge(max_done, sims(i, q, s) + 1)
                            e.activation(y[:, s % 2, :], y[:, s % 2, :], ACT.Exp, bias=negmax[:, s % 2:s % 2 + 1],
                                         accum_out=rowsum[:, s % 4:s % 4 + 1]).then_inc(prob_done, 1)
                    norm(i, 3, q)
                for q in range(2):
                    for g in range(2):
                        key = ("sup", q, g)
                        high(i, key, suph[q][:, g * T // 2:(g + 1) * T // 2, :], tile(key)[:].rearrange("p (t d) -> p t d", d=D))

        @block.vector
        def _(e):
            e.sem_inc(bank_free, BANKS)
            for n, (h, l, k, width) in enumerate(((w1h, w1l, KD, H), (w2h, w2l, KH, D), (wlh, wll, KD, D), (w3h, w3l, KD, D))):
                e.wait_ge(w_loaded, 16 * n + 16)
                src = stage32[:, 0:k * width].rearrange("p (k o) -> p k o", k=k)
                split(e, h[:], l[:], src, (w_hi, n + 1), w_lo)
            e.wait_ge(bias_moved, 64)
            e.wait_ge(cleared, 5)
            e.tensor_copy(bias16[0:1], bias32[0:1]).then_inc(setup, 1)
            e.wait_ge(setup, 1)
            e.tensor_tensor(bias_lo[0:1], bias32[0:1], bias16[0:1], ALU.subtract).then_inc(setup, 1)
            e.tensor_scalar(eps1[:], eps1[:], 1.0, None, ALU.add).then_inc(setup, 1)
            e.wait_ge(setup, 3)
            e.tensor_scalar(dia32, ident[:], eps1[:], None, ALU.mult).then_inc(setup, 1)
            e.wait_ge(setup, 4)
            e.tensor_copy(diah[:], dia32).then_inc(setup, 1)
            e.wait_ge(setup, 5)
            e.wait_ge(bias_moved, 80)
            e.tensor_tensor(dial[:], dia32, diah[:], ALU.subtract).then_inc(setup, 1)

            def norm(i, layer, q):
                n = ln(i, layer, q)
                row_stats(e, n, T, D, lambda t: xs[q][:, t, :], st, small, sums, ve, (ln_stats, ln_small, ln_var))
                e.wait_ge(ln_rstd, n + 1)
                e.scalar_tensor_tensor(shift[:], sums[:], -0.5, rstd[:], ALU.mult, ALU.mult).then_inc(ln_shift, 1)
                e.wait_ge(hh_ready, n + 1)
                e.tensor_tensor(hl[q][:], tmp[:], hh[q][:], ALU.subtract).then_inc(hl_ready, 1)

            def low(i, key, dst, src, high):
                e.wait_ge(hi_done, hi(i, key))
                e.tensor_tensor(dst, src, high, ALU.subtract).then_inc(bank_free, 1)

            def inverse(i, q, r):
                e.wait_ge(prob_done, sims(i, q, r) + 1)
                e.reciprocal(rinv[:, r % 2:r % 2 + 1], rowsum[:, r % 4:r % 4 + 1]).then_inc(rinv_done, 1)

            def turned(i, q, layer):
                for name, dst in (("hi", hth[q]), ("lo", htl[q])):
                    key = (f"{name}{layer}", q, 0)
                    e.wait_ge(bank_full, full(i, key))
                    e.tensor_copy(dst[:], tile(key)[:].bitcast(F16).rearrange("p (k n) -> p k n", k=KD)).then_inc(bank_free, 1)

            def add(i, key, q, g):
                e.wait_ge(bank_full, full(i, key))
                rows = xs[q][:, g * T // 2:(g + 1) * T // 2, :]
                e.tensor_tensor(rows, tile(key)[:].rearrange("p (t d) -> p t d", d=D), rows, ALU.add).then_inc(bank_free, 1)

            with e.Fori(0, PAIRS) as i:
                for q in range(2):
                    b = i * 2 + q
                    e.wait_ge(z_ready, b + 1)
                    e.tensor_scalar(tmp[:], z[:], 0.0, None, ALU.min).then_inc(z_min, 1)
                    e.wait_ge(x_loaded[q], i * 16 + 16)
                    e.scalar_tensor_tensor(xs[q][:], z[:], 0.0, xs[q][:], ALU.max, ALU.add).then_inc(z_used, 1)
                    e.wait_ge(z_used, b + 1)
                    e.wait_ge(z_exp, b + 1)
                    e.scalar_tensor_tensor(xs[q][:], tmp[:], -1.0, xs[q][:], ALU.add, ALU.add).then_inc(x_first, 1)
                    e.wait_ge(x_first, b + 1)
                    norm(i, 1, q)
                    e.wait_ge(mask_loaded, b * 16 + 16)
                    e.tensor_scalar(nomask[q][:], maski[:], 0, None, ALU.is_equal).then_inc(mask_ready, 1)
                    e.wait_ge(mask_ready, 2 * b + 1)
                    e.tensor_scalar(kept[q][:], nomask[q][:], -1.0, 1.0, ALU.mult, ALU.add).then_inc(mask_ready, 1)
                    e.tensor_scalar(negrow[q][0:1, :], nomask[q][0:1, :], NEG, None, ALU.mult).then_inc(neg_ready, 1)
                for q in range(2):
                    for d in range(KD):
                        key = ("agg", q, d)
                        low(i, key, zl[q][:, d, :], tile(key)[:], zh[q][:, d, :])
                    for f in range(KH):
                        key = ("hid", q, f)
                        e.wait_ge(hid32_done, (i * 2 + q) * KH + f + 1)
                        e.tensor_tensor(hidl[q][:, f, :], hid32[:, f % 2, :], hidh[q][:, f, :], ALU.subtract).then_inc(bank_free, 1)
                    for g in range(2):
                        add(i, ("mlp", q, g), q, g)
                    e.wait_ge(bank_free, free(i, ("mlp", q, 1)))
                    norm(i, 2, q)
                for q in range(2):
                    turned(i, q, 2)
                    for d in range(KD):
                        key = ("int", q, d)
                        low(i, key, zl[q][:, d, :], tile(key)[:], zh[q][:, d, :])
                    for s in range(T + 2):
                        if s < T:
                            key = ("sim", q, s)
                            n = sims(i, q, s)
                            e.wait_ge(bank_full, full(i, key))
                            e.wait_ge(row_masked, n + 1)
                            if s >= 2:
                                e.wait_ge(bank_full, full(i, ("turn", q, s - 2)))
                                inverse(i, q, s - 2)
                            else:
                                e.wait_ge(held, 2 * (i * 2 + q) + s)
                                e.memset(hold[:], 0.0).then_inc(held, 1)
                            e.tensor_tensor_reduce(y[:, s % 2, :], tile(key)[:], adjr[:, (q * T + s) % RING, :], 1.0, -BIG,
                                                   ALU.mult, ALU.max, rowmax[:, s % 2:s % 2 + 1]).then_inc(bank_free, 1)
                            e.wait_ge(bank_free, free(i, key))
                            e.tensor_scalar(negmax[:, s % 2:s % 2 + 1], rowmax[:, s % 2:s % 2 + 1], -1.0, None,
                                            ALU.mult).then_inc(max_done, 1)
                        if 1 <= s <= T:
                            key = ("turn", q, s - 1)
                            low(i, key, ptl[:, (s - 1) % 2], tile(key)[:].rearrange("p (t n) -> p t n", t=T), pth[:, (s - 1) % 2])
                        if s >= 2:
                            r = s - 2
                            if s >= T:
                                inverse(i, q, r)
                            e.wait_ge(rinv_done, sims(i, q, r) + 1)
                            e.wait_ge(bank_full, full(i, ("pv", q, r)))
                            e.scalar_tensor_tensor(xs[q][:, r, :], tile(("pv", q, r))[:, 0:D], rinv[:, r % 2:r % 2 + 1],
                                                   xs[q][:, r, :], ALU.mult, ALU.add).then_inc(bank_free, 1)
                    e.wait_ge(bank_free, free(i, ("pv", q, T - 1)))
                    norm(i, 3, q)
                for q in range(2):
                    turned(i, q, 3)
                    for g in range(2):
                        key = ("sup", q, g)
                        part = slice(g * T // 2, (g + 1) * T // 2)
                        low(i, key, supl[q][:, part, :], tile(key)[:].rearrange("p (t d) -> p t d", d=D), suph[q][:, part, :])
                    for g in range(2):
                        add(i, ("out", q, g), q, g)


def graph_layers(nc, x, adj, adj_t, mask, wt, w, a12, vecs, g3b3, w1, w2, wl2, w3, b1c, b2r, b3r, eps, out):
    S = Shapes(x, w1)
    B, N, D, T, KD = S.B, S.N, S.D, S.T, S.KD
    dram = lambda name, shape, dt: nc.dram_tensor(name, shape, dt, kind="Internal").ap()
    wh_dram = dram("wh_dram", [B, P, 2, T, D], F16)
    hp_dram = dram("hp_dram", [B, P, T, D], F32)
    e_dram = dram("e_dram", [P, P], F32)
    e9_dram = dram("e9_dram", [9, P, P], BF16)
    ab9_dram = dram("ab9_dram", [9, 2, T, P], BF16)
    gd_dram = dram("gd_dram", [2, 3, P, P], BF16)
    s_dram = dram("s_dram", [T, P], F32)
    with ExitStack() as ctx:
        sb = lambda name, shape, dt: ctx.enter_context(nc.sbuf_tensor(name, shape, dt))
        keep = {
            "ident": sb("ident", [P, P], F32),
            "ident16": sb("ident16", [P, P], F16),
            "ones": sb("ones", [P, P], F32),
            "minus_half": sb("minus_half", [P, T], F32),
            "norm3": sb("norm3", [P, 2, D], F32),
        }
        with ExitStack() as first:
            fsb = lambda name, shape, dt: first.enter_context(nc.sbuf_tensor(name, shape, dt))
            keep["ecol"] = fsb("ecol", [P, T, B], F32)
            keep["fcol"] = fsb("fcol", [P, T, B], F32)
            keep["C"] = fsb("att_shift", [P, T, B], F32)
            nodes_block(nc, S, x, wt, w, a12, keep, wh_dram)
            tables_block(nc, S, vecs, keep, e9_dram, e_dram, ab9_dram, gd_dram, s_dram)
        attend_block(nc, S, adj, keep, wh_dram, e9_dram, ab9_dram, gd_dram, s_dram, hp_dram, g3b3)
        layers_block(nc, S, x, adj, adj_t, mask, w1, w2, wl2, w3, b1c, b2r, b3r, eps, keep, hp_dram, out)


def kernel(**inputs):
    import numpy as np
    import concourse.bacc as bacc
    from concourse.bass_utils import run_bass_kernel_spmd

    a = {k: np.asarray(v) for k, v in inputs.items()}
    column = lambda v: v.reshape(-1, P).T
    arrays = {
        "x": a["x"],
        "adj": a["adj"],
        "adj_t": a["adj"].transpose(0, 2, 1),
        "mask": a["nodemask"],
        "wt": a["L0_gnn_W"].T,
        "w": a["L0_gnn_W"],
        "a12": np.stack([column(a["L0_gnn_a1"]), column(a["L0_gnn_a2"])], axis=2).reshape(P, -1),
        "vecs": np.concatenate([column(a[f"L0_gnn_{n}"]) for n in ("g1", "b1", "g2", "b2")], axis=1),
        "g3b3": np.concatenate([column(a["L0_gnn_g3"]), column(a["L0_gnn_b3"])], axis=1),
        "w1": a["L1_gnn_W1"],
        "w2": a["L1_gnn_W2"],
        "wl2": a["L2_gnn_W"],
        "w3": a["L3_gnn_weight"],
        "b1c": column(a["L1_gnn_b1"]),
        "b2r": a["L1_gnn_b2"].reshape(1, -1),
        "b3r": a["L3_gnn_bias"].reshape(1, -1),
        "eps": a["L1_gnn_eps"],
    }
    arrays = {f"in_{k}": np.ascontiguousarray(v) for k, v in arrays.items()}
    nc = bacc.Bacc("TRN2", target_bir_lowering=False, num_devices=1)
    args = [nc.dram_tensor(k, v.shape, mybir.dt.from_np(v.dtype), kind="ExternalInput").ap() for k, v in arrays.items()]
    out = nc.dram_tensor("out", a["x"].shape, F32, kind="ExternalOutput").ap()
    graph_layers(nc, *args, out)
    result = run_bass_kernel_spmd(nc, [arrays], core_ids=[0])
    return result.results[0]["out"]
```

```python
from contextlib import ExitStack

import concourse.bass as bass
from concourse import mybir

ACT = mybir.ActivationFunctionType
ALU = mybir.AluOpType
F32 = mybir.dt.float32
F16 = mybir.dt.float16
BF16 = mybir.dt.bfloat16
I32 = mybir.dt.int32
AX = mybir.AxisListType.X

P = 128
EPS = 1e-5
SLOPE = 0.2
NEG = -1e30
BIG = 3.0e38


class Shapes:
    def __init__(self, x, w1):
        self.B, self.N, self.D = x.shape
        self.H = w1.shape[1]
        self.T = self.N // P
        self.KD = self.D // P
        self.KH = self.H // P


def after(e, sem, value):
    if not isinstance(value, int) or value > 0:
        e.wait_ge(sem, value)


def row_stats(e, n, T, D, x_rows, st, small, sums, ve, sems):
    ln_stats, ln_small, ln_var = sems
    for t in range(T):
        e.bn_stats(st[:, t, :], x_rows(t)).then_inc(ln_stats, 1)
    e.wait_ge(ln_stats, n * T + T)
    e.tensor_tensor(sums[:], st[:, :, 1], st[:, :, 4], ALU.add).then_inc(ln_small, 1)
    e.tensor_tensor(small[:, 0, :], st[:, :, 1], st[:, :, 4], ALU.subtract).then_inc(ln_small, 1)
    e.tensor_tensor(small[:, 1, :], st[:, :, 2], st[:, :, 5], ALU.add).then_inc(ln_small, 1)
    e.wait_ge(ln_small, n * 5 + 3)
    e.tensor_tensor(small[:, 2, :], small[:, 0, :], small[:, 0, :], ALU.mult).then_inc(ln_small, 1)
    e.wait_ge(ln_small, n * 5 + 4)
    e.scalar_tensor_tensor(small[:, 3, :], small[:, 2, :], D / 4.0, small[:, 1, :], ALU.mult, ALU.add).then_inc(ln_small, 1)
    e.wait_ge(ln_small, n * 5 + 5)
    e.tensor_scalar(ve[:], small[:, 3, :], 1.0 / D, EPS, ALU.mult, ALU.add).then_inc(ln_var, 1)


def split(e, hi, lo, src, copied, done):
    e.tensor_copy(hi, src).then_inc(copied[0], 1)
    e.wait_ge(copied[0], copied[1])
    e.tensor_tensor(lo, src, hi, ALU.subtract).then_inc(done, 1)


def nodes_block(nc, S, x, wt, w, a12, keep, wh_dram):
    B, N, D, T, KD = S.B, S.N, S.D, S.T, S.KD
    PAIRS = B // 2
    with ExitStack() as ctx:
        sb = lambda name, shape, dt: ctx.enter_context(nc.sbuf_tensor(name, shape, dt))
        ps = lambda name, shape, dt: ctx.enter_context(nc.psum_tensor(name, shape, dt))
        sem = lambda name: ctx.enter_context(nc.semaphore(name))
        xin = [sb(f"a_xin{q}", [P, T, D], F32) for q in range(2)]
        wt32 = sb("a_wt32", [P, KD, D], F32)
        w32 = sb("a_w32", [P, KD, D], F32)
        a32 = sb("a_a32", [P, KD, 2], F32)
        wt_hi = sb("a_wt_hi", [P, KD, D], F16)
        wt_lo = sb("a_wt_lo", [P, KD, D], F16)
        u32 = sb("a_u32", [P, KD, 2], F32)
        u_hi = sb("a_u_hi", [P, KD, 2], F16)
        u_lo = sb("a_u_lo", [P, KD, 2], F16)
        st = sb("a_st", [P, T, 6], F32)
        small = sb("a_small", [P, 4, T], F32)
        sums = [sb(f"a_sums{q}", [P, T], F32) for q in range(2)]
        ve = sb("a_ve", [P, T], F32)
        rstd = sb("a_rstd", [P, 2, T], F32)
        shift = sb("a_shift", [P, 2, T], F32)
        h32 = sb("a_h32", [P, T, D], F32)
        hh = [sb(f"a_hh{q}", [P, T, D], F16) for q in range(2)]
        hl = sb("a_hl", [P, T, D], F16)
        hth = sb("a_hth", [P, KD, N], F16)
        htl = sb("a_htl", [P, KD, N], F16)
        wh = [sb(f"a_wh{q}", [P, 2, T, D], F16) for q in range(2)]
        pt_hi = ps("a_pt_hi", [P, KD, N], F16)
        pt_lo = ps("a_pt_lo", [P, KD, N], F16)
        PW = 2
        pw = [ps(f"a_pw{k}", [P, 2, D], F32) for k in range(PW)]
        bank_of = lambda q, g: pw[(q * (T // 2) + g) % PW]
        pe_ef = ps("a_pe_ef", [P, 256], F32)
        ef_ps = pe_ef[:, 0:2 * T].rearrange("p (t c) -> p t c", c=2)
        u_ps = ps("a_u_ps", [P, 512], F32)
        u_psv = u_ps[:, 0:2 * KD].rearrange("p (k c) -> p k c", c=2)

        w_loaded = sem("a_w_loaded")
        x_loaded = [sem(f"a_x_loaded{q}") for q in range(2)]
        consts = sem("a_consts")
        w_hi_done, w_lo_done = sem("a_w_hi_done"), sem("a_w_lo_done")
        u_done = sem("a_u_done")
        u_copied = sem("a_u_copied")
        ln_stats, ln_small, ln_var = sem("a_ln_stats"), sem("a_ln_small"), sem("a_ln_var")
        ln_rstd, ln_shift = sem("a_ln_rstd"), sem("a_ln_shift")
        h_ready, hh_ready, hl_ready = sem("a_h_ready"), sem("a_hh_ready"), sem("a_hl_ready")
        pt_hi_done, pt_lo_done = sem("a_pt_hi_done"), sem("a_pt_lo_done")
        hth_ready, htl_ready = sem("a_hth_ready"), sem("a_htl_ready")
        pw_done, whh_ready, pw_free = sem("a_pw_done"), sem("a_whh_ready"), sem("a_pw_free")
        ef_done, ef_ready = sem("a_ef_done"), sem("a_ef_ready")
        wh_stored = [sem(f"a_wh_stored{q}") for q in range(2)]
        block = ctx.enter_context(nc.Block())
        ident, ident16 = keep["ident"], keep["ident16"]
        G = T // 2

        @block.sync
        def _(e):
            load = lambda b, q: e.dma_start(
                xin[q][:], x[b].rearrange("(t p) d -> p t d", p=P)).then_inc(x_loaded[q], 16)
            for q in range(2):
                load(q, q)
            e.dma_start(wt32[:], wt.rearrange("(k p) o -> p k o", p=P)).then_inc(w_loaded, 16)
            e.dma_start(w32[:], w.rearrange("(k p) f -> p k f", p=P)).then_inc(w_loaded, 16)
            e.dma_start(a32[:], a12.rearrange("p (k c) -> p k c", c=2)).then_inc(w_loaded, 16)
            with e.Fori(0, PAIRS - 1) as i:
                for q in range(2):
                    b = i * 2 + q
                    e.wait_ge(h_ready, b * T + T)
                    load(b + 2, q)

        @block.gpsimd
        def _(e):
            e.memset(ident[:], 0.0).then_inc(consts, 1)
            e.wait_ge(consts, 1)
            e.affine_select(out=ident[:], in_=ident[:], compare_op=ALU.not_equal, fill=1.0,
                            base=0, pattern=[[-1, P]], channel_multiplier=1).then_inc(consts, 1)
            e.memset(keep["minus_half"][:], -0.5).then_inc(consts, 1)
            e.memset(keep["ones"][:], 1.0).then_inc(consts, 1)
            e.wait_ge(consts, 4)
            e.tensor_copy(ident16[:], ident[:]).then_inc(consts, 1)
            e.wait_ge(consts, 5)

            def rstds(b, q):
                e.wait_ge(ln_var, b + 1)
                after(e, h_ready, (b - 1) * T)
                e.tensor_tensor(rstd[:, q, :], ve[:], keep["minus_half"][:, 0:T], ALU.pow).then_inc(ln_rstd, 1)

            for q in range(2):
                rstds(q, q)
            with e.Fori(1, PAIRS) as i:
                for q in range(2):
                    rstds(i * 2 + q, q)

        @block.vector
        def _(e):
            e.sem_inc(pw_free, PW)
            e.wait_ge(w_loaded, 48)
            split(e, wt_hi[:], wt_lo[:], wt32[:], (w_hi_done, 1), w_lo_done)
            e.wait_ge(u_done, 1)
            e.tensor_copy(u32[:], u_psv).then_inc(u_copied, 1)
            e.wait_ge(u_copied, 1)
            split(e, u_hi[:], u_lo[:], u32[:], (w_hi_done, 2), w_lo_done)

            def stats(b, q, i):
                e.wait_ge(x_loaded[q], i * 16 + 16)
                row_stats(e, b, T, D, lambda t: xin[q][:, t, :], st, small, sums[q], ve, (ln_stats, ln_small, ln_var))

            def shifts(b, q):
                e.wait_ge(ln_rstd, b + 1)
                e.scalar_tensor_tensor(shift[:, q, :], sums[q][:], -0.5, rstd[:, q, :],
                                       ALU.mult, ALU.mult).then_inc(ln_shift, 1)

            def products(b, i, q, ahead):
                e.wait_ge(hh_ready, b + 1)
                e.tensor_tensor(hl[:], h32[:], hh[q][:], ALU.subtract).then_inc(hl_ready, 1)
                e.wait_ge(pt_hi_done, b + 1)
                after(e, ef_done, b)
                e.tensor_copy(hth[:], pt_hi[:]).then_inc(hth_ready, 1)
                if ahead:
                    stats(b + 2, q, i + 1)
                for g in range(G):
                    e.wait_ge(whh_ready, b * G + g + 1)
                    e.tensor_tensor(wh[q][:, 1, 2 * g:2 * g + 2, :], bank_of(q, g)[:],
                                    wh[q][:, 0, 2 * g:2 * g + 2, :], ALU.subtract).then_inc(pw_free, 1)
                    if g == 1 and ahead:
                        shifts(b + 2, q)
                e.wait_ge(ef_done, b + 1)
                for c, col in enumerate((keep["ecol"], keep["fcol"])):
                    e.tensor_copy(col[:, :, bass.ds(b, 1)] if not isinstance(b, int) else col[:, :, b:b + 1],
                                  ef_ps[:, :, c:c + 1]).then_inc(ef_ready, 1)

            for q in range(2):
                stats(q, q, 0)
                shifts(q, q)
            with e.Fori(0, PAIRS - 1) as i:
                for q in range(2):
                    products(i * 2 + q, i, q, True)
            for q in range(2):
                products(B - 2 + q, PAIRS - 1, q, False)

        @block.scalar
        def _(e):
            def h_values(b, q):
                e.wait_ge(ln_shift, b + 1)
                after(e, hl_ready, b)
                for t in range(T):
                    e.activation(h32[:, t, :], xin[q][:, t, :], ACT.Relu, bias=shift[:, q, t:t + 1],
                                 scale=rstd[:, q, t:t + 1]).then_inc(h_ready, 1)

            def h_high(b, q):
                e.wait_ge(h_ready, b * T + T)
                after(e, pt_hi_done, b - 1)
                e.activation(hh[q][:], h32[:], ACT.Copy).then_inc(hh_ready, 1)

            def step(b, i, q, ahead=True):
                e.wait_ge(pt_lo_done, b + 1)
                after(e, ef_done, b)
                e.activation(htl[:], pt_lo[:], ACT.Copy).then_inc(htl_ready, 1)
                if ahead:
                    h_values(b + 1, 1 - q)
                after(e, wh_stored[q], i * 16)
                for g in range(G):
                    e.wait_ge(pw_done, b * G + g + 1)
                    e.activation(wh[q][:, 0, 2 * g:2 * g + 2, :], bank_of(q, g)[:],
                                 ACT.Copy).then_inc(whh_ready, 1)
                    if g == 1 and ahead:
                        h_high(b + 1, 1 - q)
                e.wait_ge(pw_free, b * G + G + PW)
                e.dma_start(wh_dram[b], wh[q][:]).then_inc(wh_stored[q], 16)

            h_values(0, 0)
            h_high(0, 0)
            with e.Fori(0, PAIRS - 1) as i:
                for q in range(2):
                    step(i * 2 + q, i, q)
            for q in range(2):
                step(B - 2 + q, PAIRS - 1, q, ahead=(q == 0))
            for q in range(2):
                e.wait_ge(wh_stored[q], 16 * PAIRS)

        @block.tensor
        def _(e):
            e.wait_ge(w_loaded, 48)
            for f in range(KD):
                for k in range(KD):
                    mm = e.matmul(u_psv[:, f, :], w32[:, k, f * P:(f + 1) * P], a32[:, k, :],
                                  start=(k == 0), stop=(k == KD - 1))
            mm.then_inc(u_done, 1)
            e.wait_ge(consts, 5)
            e.wait_ge(w_lo_done, 2)
            with e.Fori(0, PAIRS) as i:
                for q in range(2):
                    b = i * 2 + q
                    for src, dst, ready, done, free in ((hh[q], pt_hi, hh_ready, pt_hi_done, hth_ready),
                                                        (hl, pt_lo, hl_ready, pt_lo_done, htl_ready)):
                        e.wait_ge(ready, b + 1)
                        e.wait_ge(free, b)
                        for k in range(KD):
                            for t in range(T):
                                mm = e.transpose(dst[:, k, t * P:(t + 1) * P],
                                                 src[:, t, k * P:(k + 1) * P], ident16[:])
                        mm.then_inc(done, 1)
                    e.wait_ge(hth_ready, b + 1)
                    e.wait_ge(htl_ready, b + 1)
                    for g in range(G):
                        e.wait_ge(pw_free, b * G + g + 1)
                        for t in (2 * g, 2 * g + 1):
                            parts = [(ht, wp, k) for k in range(KD)
                                     for ht, wp in ((hth, wt_hi), (hth, wt_lo), (htl, wt_hi))]
                            for n, (ht, wp, k) in enumerate(parts):
                                mm = e.matmul(bank_of(q, g)[:, t % 2, :], ht[:, k, t * P:(t + 1) * P], wp[:, k, :],
                                              start=(n == 0), stop=(n == len(parts) - 1))
                        mm.then_inc(pw_done, 1)
                    e.wait_ge(ef_ready, b * 2)
                    for t in range(T):
                        parts = [(ht, up, k) for k in range(KD)
                                 for ht, up in ((hth, u_hi), (hth, u_lo), (htl, u_hi))]
                        for n, (ht, up, k) in enumerate(parts):
                            mm = e.matmul(ef_ps[:, t, :], ht[:, k, t * P:(t + 1) * P], up[:, k, :],
                                          start=(n == 0), stop=(n == len(parts) - 1))
                    mm.then_inc(ef_done, 1)


def tables_block(nc, S, vecs, keep, e9_dram, e_dram, ab9_dram, gd_dram, s_dram):
    B, N, D, T = S.B, S.N, S.D, S.T
    PAIRS = B // 2
    RING = 4
    with ExitStack() as ctx:
        sb = lambda name, shape, dt: ctx.enter_context(nc.sbuf_tensor(name, shape, dt))
        ps = lambda name, shape, dt: ctx.enter_context(nc.psum_tensor(name, shape, dt))
        sem = lambda name: ctx.enter_context(nc.semaphore(name))
        cols = sb("b_cols", [P, 4, T], F32)
        g1, b1, g2, b2 = (cols[:, k, :] for k in range(4))
        esum = sb("b_esum", [P, B], F32)
        ebar = sb("b_ebar", [P, B], F32)
        me = sb("b_me", [P, 1], F32)
        ed = sb("b_ed", [P, T * B], F32)
        esq = sb("b_esq", [P, 2], F32)
        vE = sb("b_vE", [P, 1], F32)
        fbar = sb("b_fbar", [P, T], F32)
        fd = sb("b_fd", [P, T, B], F32)
        fq = sb("b_fq", [P, T, B], F32)
        small = sb("b_small", [P, 16, T], F32)
        var1, ve1, r1, A, mean1, Er, Vr, t1, t2, t3, ve2, r2, A2, C2, k8, sg = (
            small[:, n, :] for n in range(16))
        ebd = sb("b_ebd", [P, B], F32)
        C = keep["C"]
        mv2 = sb("b_mv2", [P, T, 2], F32)
        st2 = sb("b_st2", [P, T, B, 12], F32)
        eb = [sb(f"b_eb{q}", [P, N], F32) for q in range(2)]
        ring = sb("b_ring", [P, RING, N], F32)
        ab = sb("b_ab", [P, 3, T], F32)
        gdc = sb("b_gdc", [P, 2, T, B], F32)
        rows = sb("b_rows", [P, 4, P], F32)
        parts = sb("b_parts", [P, 4, 3, P], BF16)
        rest = sb("b_rest", [P, 4, 2, P], F32)
        pm = ps("b_pm", [P, 512], F32)
        pt = ps("b_pt", [P, 4, P], F32)

        loaded, tab, tab_pe, tab_pow = sem("b_loaded"), sem("b_tab"), sem("b_tab_pe"), sem("b_tab_pow")
        e_stored = sem("b_e_stored")
        eb_loaded = [sem(f"b_eb_loaded{q}") for q in range(2)]
        relu_done, stats_done, ring_free = sem("b_relu_done"), sem("b_stats_done"), sem("b_ring_free")
        aggr_done, row_stored = sem("b_aggr_done"), sem("b_row_stored")
        tables_ready, e_parts_ready, rows_ready = sem("b_tables_ready"), sem("b_e_parts"), sem("b_rows_ready")
        block = ctx.enter_context(nc.Block())
        ecol, fcol, ident, ones = keep["ecol"], keep["fcol"], keep["ident"], keep["ones"]
        wide = lambda ap: ap.unsqueeze(2).to_broadcast([P, T, B])

        @block.sync
        def _(e):
            e.dma_start(cols[:], vecs.rearrange("p (k t) -> p k t", k=4)).then_inc(loaded, 16)
            e.wait_ge(e_parts_ready, 1)
            e.dma_start(e_dram, rows[:, 0, :]).then_inc(e_stored, 16)
            for r in range(3):
                for k in range(3):
                    e.dma_start(e9_dram[3 * r + k], parts[:, 0, k, :]).then_inc(row_stored, 16)
            e.wait_ge(e_stored, 16)
            load = lambda b, q: e.dma_start(
                eb[q][:].rearrange("p (t n) -> p t n", t=T),
                e_dram.rearrange("(t b) n -> b t n", b=B)[b].partition_broadcast(P)).then_inc(eb_loaded[q], 16)
            for q in range(2):
                load(q, q)
            with e.Fori(0, PAIRS - 1) as i:
                for q in range(2):
                    b = i * 2 + q
                    e.wait_ge(relu_done, b * T + T)
                    load(b + 2, q)
            e.wait_ge(rows_ready, 1)
            for kind in range(2):
                for k in range(3):
                    e.dma_start(gd_dram[kind, k], parts[:, 1 + kind, k, :]).then_inc(row_stored, 16)
                    for c in range(3):
                        e.dma_start(ab9_dram[3 * k + c, kind], parts[kind * T:(kind + 1) * T, 3, k, :]).then_inc(row_stored, 16)
            e.dma_start(s_dram, rows[2 * T:3 * T, 3, :]).then_inc(row_stored, 16)
            e.wait_ge(row_stored, 16 * (9 + 6 + 18 + 1))

        @block.gpsimd
        def _(e):
            e.wait_ge(tab, TAB_VAR1)
            e.tensor_tensor(r1, ve1, keep["minus_half"][:, 0:T], ALU.pow).then_inc(tab_pow, 1)
            e.wait_ge(tab, TAB_VAR2)
            e.tensor_tensor(r2, ve2, keep["minus_half"][:, 0:T], ALU.pow).then_inc(tab_pow, 1)

        @block.tensor
        def _(e):
            e.transpose(pt[:, 0, :], ecol[:].rearrange("p t b -> p (t b)"), ident[:]).then_inc(tab_pe, 1)
            e.wait_ge(tab, 1)
            e.matmul(pm[:, 0:B], ones[:], esum[:], start=True, stop=True).then_inc(tab_pe, 1)
            e.wait_ge(tab, TAB_ESQ)
            e.matmul(pm[:, B:B + 1], ones[:], esq[:, 0:1], start=True, stop=True).then_inc(tab_pe, 1)
            e.wait_ge(tables_ready, 1)
            for kind in range(2):
                e.transpose(pt[:, 1 + kind, :], gdc[:, kind].rearrange("p t b -> p (t b)"), ident[:])
            e.transpose(pt[0:3 * T, 3, :], ab[:].rearrange("p c t -> p (c t)"), ident[:]).then_inc(tab_pe, 1)

        @block.scalar
        def _(e):
            e.wait_ge(tab, TAB_C)
            with e.Fori(0, PAIRS) as i:
                for q in range(2):
                    b = i * 2 + q
                    e.wait_ge(eb_loaded[q], i * 16 + 16)
                    for t in range(T):
                        e.wait_ge(ring_free, b * T + t + 1)
                        e.activation(ring[:, t % RING, :], eb[q][:], ACT.Relu, bias=C[:, t, bass.ds(b, 1)],
                                     scale=A[:, t:t + 1]).then_inc(relu_done, 1)

        @block.vector
        def _(e):
            n = [0]

            def link(ins):
                n[0] += 1
                ins.then_inc(tab, 1)
                e.wait_ge(tab, n[0])

            e.sem_inc(ring_free, RING)
            link(e.tensor_reduce(esum[:], ecol[:].rearrange("p t b -> p b t"), AX, ALU.add))
            e.wait_ge(tab_pe, 1)
            link(e.tensor_copy(rows[:, 0, :], pt[:, 0, :]))
            link(e.tensor_copy(parts[:, 0, 0, :], rows[:, 0, :]))
            link(e.tensor_tensor(rest[:, 0, 0, :], rows[:, 0, :], parts[:, 0, 0, :], ALU.subtract))
            link(e.tensor_copy(parts[:, 0, 1, :], rest[:, 0, 0, :]))
            link(e.tensor_tensor(rest[:, 0, 1, :], rest[:, 0, 0, :], parts[:, 0, 1, :], ALU.subtract))
            e.tensor_copy(parts[:, 0, 2, :], rest[:, 0, 1, :]).then_inc(e_parts_ready, 1)
            e.wait_ge(tab_pe, 2)
            link(e.tensor_scalar(ebar[:], pm[:, 0:B], 1.0 / N, None, ALU.mult))
            link(e.tensor_reduce(me[:], ebar[:], AX, ALU.add))
            link(e.tensor_scalar(me[:], me[:], 1.0 / B, None, ALU.mult))
            link(e.tensor_scalar(ed[:], ecol[:].rearrange("p t b -> p (t b)"), me[:], None, ALU.subtract))
            link(e.tensor_tensor(ed[:], ed[:], ed[:], ALU.mult))
            link(e.tensor_reduce(esq[:, 0:1], ed[:], AX, ALU.add))
            assert n[0] == TAB_ESQ
            link(e.tensor_reduce(fbar[:], fcol[:], AX, ALU.add))
            link(e.tensor_scalar(fbar[:], fbar[:], 1.0 / B, None, ALU.mult))
            link(e.tensor_tensor(fd[:], fcol[:], wide(fbar[:]), ALU.subtract))
            link(e.tensor_tensor(fq[:], fd[:], fd[:], ALU.mult))
            link(e.tensor_reduce(t1, fq[:], AX, ALU.add))
            link(e.tensor_scalar(ebd[:], ebar[:], me[:], None, ALU.subtract))
            link(e.tensor_tensor(fq[:], fd[:], ebd[:].unsqueeze(1).to_broadcast([P, T, B]), ALU.mult))
            link(e.tensor_reduce(t2, fq[:], AX, ALU.add))
            link(e.scalar_tensor_tensor(t1, t2, 2.0, t1, ALU.mult, ALU.add))
            e.wait_ge(tab_pe, 3)
            link(e.tensor_scalar(vE[:], pm[:, B:B + 1], 1.0 / (N * B), None, ALU.mult))
            link(e.tensor_scalar(var1, t1, 1.0 / B, vE[:], ALU.mult, ALU.add))
            link(e.tensor_scalar(ve1, var1, EPS, None, ALU.add))
            assert n[0] == TAB_VAR1
            e.wait_ge(tab_pow, 1)
            e.wait_ge(loaded, 16)
            link(e.tensor_tensor(A, g1, r1, ALU.mult))
            link(e.tensor_scalar(mean1, fbar[:], me[:], None, ALU.add))
            link(e.tensor_tensor(C[:], fcol[:], wide(mean1), ALU.subtract))
            link(e.tensor_tensor(C[:], C[:], wide(A), ALU.mult))
            link(e.tensor_tensor(C[:], C[:], wide(b1), ALU.add))
            assert n[0] == TAB_C
            half = N // 2
            with e.Fori(0, B) as b:
                for t in range(T):
                    e.wait_ge(relu_done, b * T + t + 1)
                    e.bn_stats(st2[:, t, bass.ds(b, 1), 0:6], ring[:, t % RING, 0:half]).then_inc(stats_done, 1)
                    e.bn_stats(st2[:, t, bass.ds(b, 1), 6:12], ring[:, t % RING, half:N]).then_inc(ring_free, 1)
            e.wait_ge(stats_done, B * T)
            e.wait_ge(ring_free, B * T + RING)
            for t in range(T):
                e.bn_aggr(mv2[:, t, :], st2[:, t].rearrange("p b s -> p (b s)")).then_inc(aggr_done, 1)
            e.wait_ge(aggr_done, T)
            link(e.tensor_copy(Er, mv2[:, :, 0]))
            link(e.tensor_scalar(Vr, mv2[:, :, 1], 0.96, None, ALU.mult))
            link(e.tensor_tensor(t1, A, A, ALU.mult))
            link(e.tensor_tensor(t1, t1, var1, ALU.mult))
            link(e.scalar_tensor_tensor(t1, t1, SLOPE * SLOPE, Vr, ALU.mult, ALU.add))
            link(e.tensor_tensor(t2, Er, b1, ALU.subtract))
            link(e.tensor_tensor(t2, t2, Er, ALU.mult))
            link(e.scalar_tensor_tensor(t1, t2, 2 * SLOPE * (1 - SLOPE), t1, ALU.mult, ALU.add))
            link(e.tensor_scalar(ve2, t1, EPS, None, ALU.add))
            assert n[0] == TAB_VAR2
            e.wait_ge(tab_pow, 2)
            link(e.tensor_tensor(A2, g2, r2, ALU.mult))
            link(e.tensor_scalar(t1, b1, SLOPE, None, ALU.mult))
            link(e.scalar_tensor_tensor(t1, Er, 1 - SLOPE, t1, ALU.mult, ALU.add))
            link(e.tensor_tensor(t1, t1, A2, ALU.mult))
            link(e.tensor_tensor(C2, b2, t1, ALU.subtract))
            link(e.tensor_scalar(sg, A2, 0.0, 2.0, ALU.is_ge, ALU.mult))
            link(e.tensor_scalar(sg, sg, -1.0, None, ALU.add))
            link(e.tensor_copy(ab[:, 2, :], sg))
            link(e.tensor_tensor(k8, A2, sg, ALU.mult))
            link(e.tensor_scalar(k8, k8, 1 - SLOPE, None, ALU.mult))
            link(e.tensor_tensor(ab[:, 0, :], k8, A, ALU.mult))
            link(e.tensor_scalar(t3, A2, SLOPE, None, ALU.mult))
            link(e.tensor_tensor(ab[:, 1, :], t3, A, ALU.mult))
            link(e.tensor_tensor(gdc[:, 0], C[:], wide(k8), ALU.mult))
            link(e.tensor_tensor(gdc[:, 1], C[:], wide(t3), ALU.mult))
            e.tensor_tensor(gdc[:, 1], gdc[:, 1], wide(C2), ALU.add).then_inc(tables_ready, 1)
            e.wait_ge(tab_pe, 4)
            for r, rows_used in ((1, P), (2, P), (3, 3 * T)):
                link(e.tensor_copy(rows[0:rows_used, r, :], pt[0:rows_used, r, :]))
                link(e.tensor_copy(parts[0:rows_used, r, 0, :], rows[0:rows_used, r, :]))
                link(e.tensor_tensor(rest[0:rows_used, r, 0, :], rows[0:rows_used, r, :], parts[0:rows_used, r, 0, :], ALU.subtract))
                link(e.tensor_copy(parts[0:rows_used, r, 1, :], rest[0:rows_used, r, 0, :]))
                link(e.tensor_tensor(rest[0:rows_used, r, 1, :], rest[0:rows_used, r, 0, :], parts[0:rows_used, r, 1, :], ALU.subtract))
                last = e.tensor_copy(parts[0:rows_used, r, 2, :], rest[0:rows_used, r, 1, :])
                if r < 3:
                    link(last)
            last.then_inc(rows_ready, 1)


TAB_ESQ = 12
TAB_VAR1 = TAB_ESQ + 12
TAB_C = TAB_VAR1 + 5
TAB_VAR2 = TAB_C + 9


def attend_block(nc, S, adj, keep, wh_dram, e9_dram, ab9_dram, gd_dram, s_dram, hp_dram, g3b3):
    B, N, D, T, KD = S.B, S.N, S.D, S.T, S.KD
    ADJ = 4
    with ExitStack() as ctx:
        sb = lambda name, shape, dt: ctx.enter_context(nc.sbuf_tensor(name, shape, dt))
        ps = lambda name, shape, dt: ctx.enter_context(nc.psum_tensor(name, shape, dt))
        sem = lambda name: ctx.enter_context(nc.semaphore(name))
        ident = keep["ident"]
        erow = [sb(f"c_erow{q}", [P, N], BF16) for q in range(2)]
        lrow = [sb(f"c_lrow{q}", [P, 2, N], BF16) for q in range(2)]
        srow = sb("c_srow", [P, N], F32)
        wh = [sb(f"c_wh{q}", [P, 2, T, D], F16) for q in range(2)]
        adjr = sb("c_adjr", [P, ADJ, N], F32)
        relu = sb("c_relu", [P, 2, N], F32)
        logit = sb("c_logit", [P, 2, N], F32)
        prob = sb("c_prob", [P, 2, N], F32)
        masked = sb("c_masked", [P, 2, N], F32)
        negmax = sb("c_negmax", [P, 2], F32)
        rowsum = sb("c_rowsum", [P, 4], F32)
        rinv = sb("c_rinv", [P, 4], F32)
        pth = sb("c_pth", [P, 2, T, P], F16)
        ptl = sb("c_ptl", [P, 2, T, P], F16)
        hp = [sb(f"c_hp{q}", [P, T, D], F32) for q in range(2)]
        st3 = sb("c_st3", [P, KD, B * T // 2, 6], F32)
        mv3 = sb("c_mv3", [P, KD, 2], F32)
        sc3 = sb("c_sc3", [P, 6, KD], F32)
        g3b3_sb = sb("c_g3b3", [P, 2, KD], F32)
        diag = sb("c_diag", [P, 2, KD, P], F32)
        p_relu = ps("c_p_relu", [P, N], F32)
        p_lin = ps("c_p_lin", [P, N], F32)
        p_t = ps("c_p_t", [P, T, P], F32)
        p_o = ps("c_p_o", [P, 512], F32)
        p_s = ps("c_p_s", [P, KD, 2 * P], F32)

        rows_cleared = sem("c_rows_cleared")
        const_loaded = sem("c_const_loaded")
        rows_loaded = [sem(f"c_rows_loaded{q}") for q in range(2)]
        wh_loaded = [sem(f"c_wh_loaded{q}") for q in range(2)]
        adj_loaded = [sem(f"c_adj_loaded{k}") for k in range(ADJ)]
        lin_done, relu_done, signed_done = sem("c_lin_done"), sem("c_relu_done"), sem("c_signed_done")
        logit_done, prob_done, masked_done = sem("c_logit_done"), sem("c_prob_done"), sem("c_masked_done")
        pt_done, pth_done, ptl_done = sem("c_pt_done"), sem("c_pth_done"), sem("c_ptl_done")
        pv_done, rinv_done, hp_done = sem("c_pv_done"), sem("c_rinv_done"), sem("c_hp_done")
        ht_done, st3_done = sem("c_ht_done"), sem("c_st3_done")
        hp_stored = [sem(f"c_hp_stored{q}") for q in range(2)]
        fin, fin_pow, fin_pe = sem("c_fin"), sem("c_fin_pow"), sem("c_fin_pe")
        block = ctx.enter_context(nc.Block())
        TILES = B * T

        def pairs(e, step):
            with e.Fori(0, B // 2) as i:
                for q in range(2):
                    step(i, q, i * 2 + q)

        @block.sync
        def _(e):
            e.dma_start(srow[:].rearrange("p (t n) -> p t n", t=T),
                        s_dram.partition_broadcast(P)).then_inc(const_loaded, 16)
            e.dma_start(g3b3_sb[:], g3b3.rearrange("p (c k) -> p c k", c=2)).then_inc(const_loaded, 16)
            e.wait_ge(rows_cleared, 4)
            for q in range(2):
                e.dma_start(lrow[q][0:9].rearrange("r c n -> r (c n)"),
                            ab9_dram.rearrange("r c t n -> r (c t n)")).then_inc(const_loaded, 16)

            def load_rows(b, q):
                e.dma_start(erow[q][0:9].rearrange("r (t n) -> r t n", t=T),
                            e9_dram.rearrange("r (t b) n -> b r t n", b=B)[b]).then_inc(rows_loaded[q], 16)
                for kind in range(2):
                    e.dma_start(lrow[q][9:12, kind].rearrange("r (t n) -> r t n", t=T),
                                gd_dram[kind].rearrange("r (t b) n -> b r t n", b=B)[b]).then_inc(rows_loaded[q], 16)
                e.dma_start(wh[q][:], wh_dram[b]).then_inc(wh_loaded[q], 16)

            for q in range(2):
                load_rows(q, q)
            def store(b, q):
                e.wait_ge(hp_done, b * T + T)
                e.dma_start(hp_dram[b], hp[q][:]).then_inc(hp_stored[q], 16)

            with e.Fori(0, B // 2 - 1) as i:
                for q in range(2):
                    b = i * 2 + q
                    e.wait_ge(pv_done, b * T + T)
                    load_rows(b + 2, q)
                    store(b, q)
            for q in range(2):
                store(B - 2 + q, q)

        @block.gpsimd
        def _(e):
            for q in range(2):
                e.memset(erow[q][:], 1.0).then_inc(rows_cleared, 1)
                e.memset(lrow[q][:], 0.0).then_inc(rows_cleared, 1)
            load = lambda b, t: e.dma_start(
                adjr[:, t % ADJ, :], adj[b, t * P:(t + 1) * P, :]).then_inc(adj_loaded[t % ADJ], 16)

            def mask(b, t):
                g = b * T + t
                e.wait_ge(prob_done, g + 1)
                e.wait_ge(adj_loaded[t % ADJ], (b * (T // ADJ) + t // ADJ + 1) * 16)
                after(e, pt_done, g - 1)
                e.tensor_tensor(masked[:, t % 2, :], prob[:, t % 2, :], adjr[:, t % ADJ, :],
                                ALU.mult).then_inc(masked_done, 1)

            for t in range(ADJ):
                load(0, t)

            def graph(b, last=False):
                for t in range(T):
                    mask(b, t)
                    e.wait_ge(masked_done, b * T + t + 1)
                    if t + ADJ < T:
                        load(b, t + ADJ)
                    elif not last:
                        load(b + 1, t + ADJ - T)

            graph(0)
            with e.Fori(1, B - 1) as b:
                graph(b)
            graph(B - 1, last=True)
            e.wait_ge(fin, FIN_VAR)
            e.tensor_tensor(sc3[:, 1, :], sc3[:, 0, :], keep["minus_half"][:, 0:KD], ALU.pow).then_inc(fin_pow, 1)

        @block.tensor
        def _(e):
            e.wait_ge(const_loaded, 64)

            def lin(b, q, i, t):
                g = b * T + t
                if t == 0:
                    e.wait_ge(rows_loaded[q], i * 48 + 48)
                e.wait_ge(relu_done, g)
                for h in range(2):
                    e.matmul(p_relu[:, h * 512:(h + 1) * 512], erow[q][:, t * P:(t + 1) * P],
                             lrow[q][:, 0, h * 512:(h + 1) * 512], start=True, stop=True)
                e.wait_ge(logit_done, g)
                for h in range(2):
                    mm = e.matmul(p_lin[:, h * 512:(h + 1) * 512], erow[q][:, t * P:(t + 1) * P],
                                  lrow[q][:, 1, h * 512:(h + 1) * 512], start=True, stop=True)
                mm.then_inc(lin_done, 1)

            def turn(g, t):
                e.wait_ge(masked_done, g + 1)
                e.wait_ge(ptl_done, g)
                for j in range(T):
                    mm = e.transpose(p_t[:, j, :], masked[:, t % 2, j * P:(j + 1) * P], ident[:])
                mm.then_inc(pt_done, 1)

            def pv(g, q, i, t):
                if t == 0:
                    e.wait_ge(wh_loaded[q], i * 16 + 16)
                e.wait_ge(ptl_done, g + 1)
                e.wait_ge(hp_done, g)
                parts = [(pp, w, j) for j in range(T) for pp, w in ((pth, 0), (pth, 1), (ptl, 0))]
                for n, (pp, w, j) in enumerate(parts):
                    mm = e.matmul(p_o[:, 0:D], pp[:, t % 2, j, :], wh[q][:, w, j, :],
                                  start=(n == 0), stop=(n == len(parts) - 1))
                mm.then_inc(pv_done, 1)

            def flip(g, q, t):
                e.wait_ge(hp_done, g + 1)
                if t % 2 == 0:
                    e.wait_ge(st3_done, g)
                for k in range(KD):
                    mm = e.transpose(p_s[:, k, (t % 2) * P:(t % 2 + 1) * P], hp[q][:, t, k * P:(k + 1) * P], ident[:])
                if t % 2:
                    mm.then_inc(ht_done, 1)

            LAGS = ((2, turn), (3, pv), (4, flip))

            def slot(i, q, t, first=False):
                b = i * 2 + q
                lin(b, q, i, t)
                for lag, what in LAGS:
                    if first and t < lag:
                        continue
                    tt = (t - lag) % T
                    late = t < lag
                    g = b * T + t - lag
                    if what is turn:
                        turn(g, tt)
                    elif what is pv:
                        if late:
                            pv(g, 1 - q, i if q else i - 1, tt)
                        else:
                            pv(g, q, i, tt)
                    else:
                        flip(g, 1 - q if late else q, tt)

            for q in range(2):
                for t in range(T):
                    slot(0, q, t, first=(q == 0))
            with e.Fori(1, B // 2) as i:
                for q in range(2):
                    for t in range(T):
                        slot(i, q, t)
            for t in range(4):
                for lag, what in LAGS:
                    if t < lag:
                        g, tt = TILES + t - lag, T + t - lag
                        if what is turn:
                            turn(g, tt)
                        elif what is pv:
                            pv(g, 1, B // 2 - 1, tt)
                        else:
                            flip(g, 1, tt)
            e.wait_ge(fin, FIN_DIAG)
            for c in range(2):
                for k in range(KD):
                    mm = e.matmul(p_relu[:, (c * KD + k) * P:(c * KD + k + 1) * P], keep["ones"][:],
                                  diag[:, c, k, :], start=True, stop=True)
            mm.then_inc(fin_pe, 1)

        @block.scalar
        def _(e):
            def relus(b, t):
                g = b * T + t
                e.wait_ge(lin_done, g + 1)
                after(e, logit_done, g - 1)
                e.activation(relu[:, t % 2, :], p_relu[:], ACT.Relu).then_inc(relu_done, 1)

            def exps(b, t):
                g = b * T + t
                e.wait_ge(logit_done, g + 1)
                after(e, masked_done, g - 1)
                after(e, rinv_done, g - 3)
                e.activation(prob[:, t % 2, :], logit[:, t % 2, :], ACT.Exp, bias=negmax[:, t % 2:t % 2 + 1],
                             scale=-1.0, accum_out=rowsum[:, t % 4:t % 4 + 1]).then_inc(prob_done, 1)

            def highs(g, t):
                e.wait_ge(pt_done, g + 1)
                after(e, pv_done, g - 1)
                e.activation(pth[:, t % 2], p_t[:], ACT.Copy).then_inc(pth_done, 1)

            def graph(b, first=False):
                for t in range(T):
                    relus(b, t)
                    if not (first and t < 2):
                        highs(b * T + t - 2, (t - 2) % T)
                    exps(b, t)
            graph(0, True)
            with e.Fori(1, B) as b:
                graph(b)
            for t in range(2):
                highs(TILES + t - 2, T + t - 2)

        @block.vector
        def _(e):
            def inverse(g, t):
                e.reciprocal(rinv[:, t % 4:t % 4 + 1], rowsum[:, t % 4:t % 4 + 1]).then_inc(rinv_done, 1)

            def logits(b, t):
                g = b * T + t
                e.wait_ge(relu_done, g + 1)
                e.tensor_tensor(relu[:, t % 2, :], relu[:, t % 2, :], srow[:], ALU.mult).then_inc(signed_done, 1)
                e.wait_ge(signed_done, g + 1)
                after(e, prob_done, g - 1)
                if not isinstance(g, int) or g >= 2:
                    inverse(g - 2, (t - 2) % T)
                e.tensor_tensor_reduce(logit[:, t % 2, :], relu[:, t % 2, :], p_lin[:], -1.0, BIG,
                                       ALU.add, ALU.min, negmax[:, t % 2:t % 2 + 1]).then_inc(logit_done, 1)

            def lows(g, t):
                e.wait_ge(pth_done, g + 1)
                after(e, pv_done, g - 1)
                e.tensor_tensor(ptl[:, t % 2], p_t[:], pth[:, t % 2], ALU.subtract).then_inc(ptl_done, 1)

            def outs(g, q, i, t):
                if t == 0 and not isinstance(i, int):
                    e.wait_ge(hp_stored[q], i * 16)
                    e.wait_ge(ht_done, (i * 2 + q - 1) * (T // 2))
                e.wait_ge(rinv_done, g + 1)
                e.wait_ge(pv_done, g + 1)
                e.tensor_scalar(hp[q][:, t, :], p_o[:, 0:D], rinv[:, t % 4:t % 4 + 1], None,
                                ALU.mult).then_inc(hp_done, 1)

            def stats(g2, n):
                e.wait_ge(ht_done, g2)
                for k in range(KD):
                    e.bn_stats(st3[:, k, n, :] if isinstance(n, int) else st3[:, k, bass.ds(n, 1), :],
                               p_s[:, k, :]).then_inc(st3_done, 1)

            def slot(i, q, t, first=False):
                b = i * 2 + q
                logits(b, t)
                if not (first and t < 2):
                    lows(b * T + t - 2, (t - 2) % T)
                if not (first and t < 3):
                    late = t < 3
                    outs(b * T + t - 3, 1 - q if late else q, (i if q else i - 1) if late else i, (t - 3) % T)
                if t % 2 == 1 and not (first and t < 5):
                    n = b * (T // 2) + (t - 5) // 2
                    stats(n + 1, n)

            for q in range(2):
                for t in range(T):
                    slot(0, q, t, first=(q == 0))
            with e.Fori(1, B // 2) as i:
                for q in range(2):
                    for t in range(T):
                        slot(i, q, t)
            for t in range(3):
                if t < 2:
                    e.wait_ge(prob_done, TILES + t - 1)
                    inverse(TILES + t - 2, T + t - 2)
                    lows(TILES + t - 2, T + t - 2)
                outs(TILES + t - 3, 1, B // 2 - 1, T + t - 3)
                if t == 1:
                    stats(TILES // 2 - 1, TILES // 2 - 2)
            stats(TILES // 2, TILES // 2 - 1)
            e.wait_ge(st3_done, TILES)
            n = [0]

            def link(ins):
                n[0] += 1
                ins.then_inc(fin, 1)
                e.wait_ge(fin, n[0])
            for k in range(KD):
                link(e.bn_aggr(mv3[:, k, :], st3[:, k].rearrange("p n s -> p (n s)")))
            link(e.tensor_scalar(sc3[:, 0, :], mv3[:, :, 1], EPS, None, ALU.add))
            assert n[0] == FIN_VAR
            e.wait_ge(fin_pow, 1)
            link(e.tensor_tensor(sc3[:, 2, :], g3b3_sb[:, 0, :], sc3[:, 1, :], ALU.mult))
            link(e.tensor_tensor(sc3[:, 3, :], mv3[:, :, 0], sc3[:, 2, :], ALU.mult))
            link(e.tensor_tensor(sc3[:, 4, :], g3b3_sb[:, 1, :], sc3[:, 3, :], ALU.subtract))
            for c, src in ((0, 2), (1, 4)):
                for k in range(KD):
                    link(e.tensor_scalar(diag[:, c, k, :], ident[:], sc3[:, src, k:k + 1], None, ALU.mult))
            assert n[0] == FIN_DIAG
            e.wait_ge(fin_pe, 1)
            link(e.tensor_copy(keep["norm3"][:].rearrange("p c d -> p (c d)"), p_relu[:, 0:2 * D]))
            for q in range(2):
                e.wait_ge(hp_stored[q], 16 * (B // 2))


FIN_VAR = 3
FIN_DIAG = FIN_VAR + 3 + 4


def layers_block(nc, S, x, adj, adj_t, mask, w1, w2, wl2, w3, b1c, b2r, b3r, eps, keep, hp_dram, out):
    B, N, D, T, KD, H, KH = S.B, S.N, S.D, S.T, S.KD, S.H, S.KH
    PAIRS = B // 2
    BANKS = 4
    RING = 3
    LNS = 6

    order = []
    turned_in = lambda layer, q: [("hi%d" % layer, q, 0), ("lo%d" % layer, q, 0)]
    for q in range(2):
        order += [("agg", q, d) for d in range(KD)] + [("hid", q, f) for f in range(KH)]
        order += turned_in(2, 0) if q == 1 else []
        order += [("mlp", q, g) for g in range(2)]
    for q in range(2):
        order += [("int", q, d) for d in range(KD)]
        for s in range(T + 3):
            order += [("sim", q, s)] if s < T else []
            order += [("turn", q, s - 2)] if 2 <= s <= T + 1 else []
            order += turned_in(*((2, 1), (3, 0))[q]) if s == T + 1 else []
            order += [("pv", q, s - 3)] if s >= 3 else []
    for q in range(2):
        order += [("sup", q, g) for g in range(2)] + [("out", q, 0)]
        order += turned_in(3, 1) if q == 0 else []
        order += [("out", q, 1)]
    place = {key: n for n, key in enumerate(order)}
    COUNT = len(order)
    assert COUNT % BANKS == 0

    with ExitStack() as ctx:
        sb = lambda name, shape, dt: ctx.enter_context(nc.sbuf_tensor(name, shape, dt))
        ps = lambda name, shape, dt: ctx.enter_context(nc.psum_tensor(name, shape, dt))
        sem = lambda name: ctx.enter_context(nc.semaphore(name))
        ident, ident16, norm3 = keep["ident"], keep["ident16"], keep["norm3"]
        two = lambda name, shape, dt: [sb(f"d_{name}{q}", shape, dt) for q in range(2)]
        xs = two("x", [P, T, D], F32)
        adjt = two("adjt", [P, T, N], F16)
        hh, hl = two("hh", [P, T, D], F16), two("hl", [P, T, D], F16)
        hth, htl = two("hth", [P, KD, N], F16), two("htl", [P, KD, N], F16)
        zx = two("zx", [P, T, D], F32)
        zparts = [zx[q][:].rearrange("p t d -> p (t d)").bitcast(F16).rearrange("p (c k n) -> p c k n", c=2, k=KD) for q in range(2)]
        zh, zl = [v[:, 0] for v in zparts], [v[:, 1] for v in zparts]
        hidh, hidl = two("hidh", [P, KH, N], F16), two("hidl", [P, KH, N], F16)
        suph = [hidh[q][:].rearrange("p f n -> p (f n)")[:, 0:T * D].rearrange("p (t d) -> p t d", t=T) for q in range(2)]
        supl = [hidl[q][:].rearrange("p f n -> p (f n)")[:, 0:T * D].rearrange("p (t d) -> p t d", t=T) for q in range(2)]
        kept, nomask = two("kept", [P, N], BF16), two("nomask", [P, N], BF16)
        negrow = two("negrow", [P, N], BF16)
        maski = sb("d_maski", [P, N], I32)
        z = sb("d_z", [P, T, D], F32)
        tmp = sb("d_tmp", [P, T, D], F32)
        hid32 = tmp[:].rearrange("p t d -> p (t d)").rearrange("p (a n) -> p a n", a=2)
        adjr = sb("d_adjr", [P, RING, N], F32)
        h32 = {(1, 0): tmp, (1, 1): z, (2, 0): z, (2, 1): tmp, (3, 0): tmp, (3, 1): tmp}
        normed = lambda layer, q: zx[0] if (layer, q) == (1, 0) else xs[q]
        y = sb("d_y", [P, 2, N], F32)
        pth, ptl = sb("d_pth", [P, 2, T, P], F16), sb("d_ptl", [P, 2, T, P], F16)
        w1h, w1l = sb("d_w1h", [P, KD, H], F16), sb("d_w1l", [P, KD, H], F16)
        w2h, w2l = sb("d_w2h", [P, KH, D], F16), sb("d_w2l", [P, KH, D], F16)
        wlh, wll = sb("d_wlh", [P, KD, D], F16), sb("d_wll", [P, KD, D], F16)
        w3h, w3l = sb("d_w3h", [P, KD, D], F16), sb("d_w3l", [P, KD, D], F16)
        b1 = sb("d_b1", [P, KH], F32)
        bias16 = sb("d_bias16", [P, 2, D], F16)
        bias_lo = sb("d_bias_lo", [P, 2, D], F16)
        ones16 = sb("d_ones16", [P, P], F16)
        onesb = sb("d_onesb", [P, P], BF16)
        eps1 = sb("d_eps1", [P, 1], F32)
        diah, dial = sb("d_diah", [P, P], F16), sb("d_dial", [P, P], F16)
        st, small, sums = sb("d_st", [P, T, 6], F32), sb("d_small", [P, 4, T], F32), sb("d_sums", [P, T], F32)
        ve, rstd, shift = (sb(f"d_{n}", [P, T], F32) for n in ("ve", "rstd", "shift"))
        rowmax, negmax = sb("d_rowmax", [P, 2], F32), sb("d_negmax", [P, 2], F32)
        rowsum, rinv = sb("d_rowsum", [P, 4], F32), sb("d_rinv", [P, 4], F32)
        hold = sb("d_hold", [P, 1], F32)
        bank = [ps(f"d_bank{k}", [P, N], F32) for k in range(BANKS)]
        stage32 = tmp[:].rearrange("p t d -> p (t d)")
        bias32 = z[:].rearrange("p t d -> p (t d)")[:, 0:2 * D].rearrange("p (c d) -> p c d", c=2)
        dia32 = z[:].rearrange("p t d -> p (t d)")[:, 2 * D:2 * D + P]

        w_loaded, w_hi, w_lo, setup = sem("d_w_loaded"), sem("d_w_hi"), sem("d_w_lo"), sem("d_setup")
        cleared = sem("d_cleared")
        bias_moved = sem("d_bias_moved")
        z_loaded, z_scaled, z_ready, z_min, z_exp = (
            sem(f"d_{n}") for n in ("z_loaded", "z_scaled", "z_ready", "z_min", "z_exp"))
        x_loaded = [sem(f"d_x_loaded{q}") for q in range(2)]
        x_plus, x_first, x_moved = sem("d_x_plus"), sem("d_x_first"), sem("d_x_moved")
        adjt_loaded = [[sem(f"d_adjt_loaded{q}{h}") for h in range(2)] for q in range(2)]
        row_loaded = [sem(f"d_row_loaded{k}") for k in range(RING)]
        row_kept, row_masked = sem("d_row_kept"), sem("d_row_masked")
        mask_loaded, mask_ready, neg_ready = sem("d_mask_loaded"), sem("d_mask_ready"), sem("d_neg_ready")
        ln_stats, ln_small, ln_var = sem("d_ln_stats"), sem("d_ln_small"), sem("d_ln_var")
        ln_rstd, ln_shift = sem("d_ln_rstd"), sem("d_ln_shift")
        h_ready, hh_ready, hl_ready = sem("d_h_ready"), sem("d_hh_ready"), sem("d_hl_ready")
        bank_full, bank_free = sem("d_bank_full"), sem("d_bank_free")
        hi_done = sem("d_hi_done")
        hid32_done, hidh_done = sem("d_hid32_done"), sem("d_hidh_done")
        max_done, prob_done, rinv_done = sem("d_max_done"), sem("d_prob_done"), sem("d_rinv_done")
        held = sem("d_held")
        stored = [sem(f"d_stored{q}") for q in range(2)]
        block = ctx.enter_context(nc.Block())

        his, HIS = {}, 0
        for key in order:
            if key[0] in ("agg", "hi2", "int", "turn", "hi3", "sup"):
                HIS += 1
                his[key] = HIS
        full = lambda i, key: i * COUNT + place[key] + 1
        free = lambda i, key: i * COUNT + place[key] + 1 + BANKS
        hi = lambda i, key: i * HIS + his[key]
        tile = lambda key: bank[place[key] % BANKS]
        ln = lambda i, layer, q: i * LNS + 2 * (layer - 1) + q
        sims = lambda i, q, s: (i * 2 + q) * T + s

        @block.sync
        def _(e):
            for n, (src, k, width) in enumerate(((w1, KD, H), (w2, KH, D), (wl2, KD, D), (w3, KD, D))):
                e.wait_ge(w_lo, n) if n else None
                e.dma_start(stage32[:, 0:k * width].rearrange("p (k o) -> p k o", k=k),
                            src.rearrange("(k p) o -> p k o", p=P)).then_inc(w_loaded, 16)
            e.dma_start(bias32[0:1, 0, :], b2r).then_inc(bias_moved, 16)
            e.dma_start(bias32[0:1, 1, :], b3r).then_inc(bias_moved, 16)
            e.dma_start(b1[:], b1c).then_inc(bias_moved, 16)
            e.dma_start(eps1[:], eps.partition_broadcast(P)).then_inc(bias_moved, 16)
            e.wait_ge(setup, 3)
            e.dma_start(bias16[1:2, :, :], bias_lo[0:1, :, :]).then_inc(bias_moved, 16)
            e.wait_ge(setup, 6)

            def load_z(b):
                e.dma_start(z[:], hp_dram[b]).then_inc(z_loaded, 16)

            def load_x(b, q):
                e.dma_start(zx[q][:], x[b].rearrange("(t p) d -> p t d", p=P)).then_inc(x_loaded[q], 16)

            def load_row(i, g):
                q, s = g // T, g % T
                e.dma_start(adjr[:, g % RING, :], adj[i * 2 + q, s * P:(s + 1) * P, :]).then_inc(row_loaded[g % RING], 16)

            def pair(i, last=False):
                for g in range(RING):
                    load_row(i, g)
                for q in range(2):
                    b = i * 2 + q
                    after(e, neg_ready, b)
                    e.dma_start(maski[:], mask[b].partition_broadcast(P)).then_inc(mask_loaded, 16)
                if not last:
                    e.wait_ge(hl_ready, ln(i, 2, 0) + 1)
                    load_z(i * 2 + 2)
                for g in range(RING, 2 * T):
                    p = g - RING
                    e.wait_ge(bank_free, free(i, ("sim", p // T, p % T)))
                    load_row(i, g)
                    if p == T - 1 and not last:
                        load_x(i * 2 + 2, 0)
                if not last:
                    e.wait_ge(bank_free, free(i, ("sim", 1, T - 1)))
                    load_x(i * 2 + 3, 1)
                    e.wait_ge(x_first, i * 2 + 3)
                    load_z(i * 2 + 3)
                for q in range(2):
                    e.wait_ge(bank_free, free(i, ("out", q, 1)))
                    e.dma_start(out[i * 2 + q].rearrange("(t p) d -> p t d", p=P), xs[q][:]).then_inc(stored[q], 16)

            load_z(0)
            for q in range(2):
                load_x(q, q)
            e.wait_ge(x_first, 1)
            load_z(1)
            with e.Fori(0, PAIRS - 1) as i:
                pair(i)
            pair(PAIRS - 1, last=True)
            for q in range(2):
                e.wait_ge(stored[q], 16 * PAIRS)

        ROWS = [len([g for g in range(2 * T) if g % RING == k]) for k in range(RING)]

        @block.gpsimd
        def _(e):
            e.memset(ones16[:], 1.0).then_inc(cleared, 1)
            e.memset(onesb[:], 1.0).then_inc(cleared, 1)
            e.memset(bias16[:], 0.0).then_inc(cleared, 1)
            for q in range(2):
                e.memset(negrow[q][:], 0.0).then_inc(cleared, 1)

            def load_adjt(b, q, h):
                part = slice(h * (N // 2), (h + 1) * (N // 2))
                e.dma_start(adjt[q][:, :, part], adj_t[b].rearrange("(t p) n -> p t n", p=P)[:, :, part]).then_inc(adjt_loaded[q][h], 16)

            def rstds(n):
                e.wait_ge(ln_var, n + 1)
                after(e, h_ready, n * T)
                e.tensor_tensor(rstd[:], ve[:], keep["minus_half"][:, 0:T], ALU.pow).then_inc(ln_rstd, 1)

            def scale_z(b):
                e.wait_ge(z_loaded, b * 16 + 16)
                e.tensor_tensor(z[:], z[:], norm3[:, 0, :].unsqueeze(1).to_broadcast([P, T, D]), ALU.mult).then_inc(z_scaled, 1)
                e.wait_ge(z_scaled, b + 1)
                e.tensor_tensor(z[:], z[:], norm3[:, 1, :].unsqueeze(1).to_broadcast([P, T, D]), ALU.add).then_inc(z_ready, 1)

            def mask_rows(i, q, first, past):
                e.wait_ge(mask_ready, 2 * (i * 2 + q + 1))
                for s in range(first, past):
                    g = q * T + s
                    e.wait_ge(row_loaded[g % RING], i * (16 * ROWS[g % RING]) + 16 * (g // RING + 1))
                    row = adjr[:, g % RING, :]
                    e.tensor_tensor(row, row, kept[q][:], ALU.mult).then_inc(row_kept, 1)
                    e.wait_ge(row_kept, sims(i, q, s) + 1)
                    e.tensor_tensor(row, row, nomask[q][:], ALU.add).then_inc(row_masked, 1)

            def pair(i, last=False):
                rstds(ln(i, 1, 1))
                rstds(ln(i, 2, 0))
                if not last:
                    scale_z(i * 2 + 2)
                mask_rows(i, 0, 0, RING)
                rstds(ln(i, 2, 1))
                mask_rows(i, 0, RING, T)
                mask_rows(i, 1, 0, RING)
                rstds(ln(i, 3, 0))
                mask_rows(i, 1, RING, T)
                rstds(ln(i, 3, 1))
                if not last:
                    rstds(ln(i + 1, 1, 0))
                    for h in range(2):
                        e.wait_ge(bank_full, full(i, ("out", 0, h)))
                        load_adjt(i * 2 + 2, 0, h)
                    scale_z(i * 2 + 3)
                    for h in range(2):
                        e.wait_ge(bank_full, full(i, ("out", 1, h)))
                        load_adjt(i * 2 + 3, 1, h)

            for q in range(2):
                for h in range(2):
                    load_adjt(q, q, h)
            scale_z(0)
            rstds(0)
            scale_z(1)
            with e.Fori(0, PAIRS - 1) as i:
                pair(i)
            pair(PAIRS - 1, last=True)

        @block.tensor
        def _(e):
            def into(i, key):
                e.wait_ge(bank_free, i * COUNT + place[key] + 1)
                return tile(key)

            def products(dst, parts, last):
                for n, (a, m) in enumerate(parts):
                    mm = e.matmul(dst, a, m, start=(n == 0), stop=(n == len(parts) - 1))
                if last:
                    mm.then_inc(bank_full, 1)

            def add_products(dst, parts, first=False, last=False):
                for n, (a, m) in enumerate(parts):
                    mm = e.matmul(dst, a, m, start=(first and n == 0), stop=(last and n == len(parts) - 1), skip_group_check=True)
                return mm

            halves = [slice(h * 512, (h + 1) * 512) for h in range(N // 512)]
            cut = lambda n: slice(n * P, (n + 1) * P)

            def by_columns(i, keys, parts, ready, also=None):
                for step in range(2):
                    e.wait_ge(*ready[step])
                    if step == 1 and also:
                        e.wait_ge(*also)
                    for key in keys:
                        dst = tile(key) if step else into(i, key)
                        for half in halves:
                            mm = add_products(dst[:, half], parts(key, step, half), first=(step == 0), last=(step == 1))
                        if step == 1:
                            mm.then_inc(bank_full, 1)

            def by_rows(i, keys, parts, ready):
                per_bank = 512 // D
                for step in range(2):
                    e.wait_ge(*ready[step]) if ready[step] else None
                    for key in keys:
                        dst = tile(key) if step else into(i, key)
                        for t in range(T // 2):
                            mm = add_products(dst[:, t * D:(t + 1) * D], parts(key, step, key[2] * T // 2 + t),
                                              first=(step == 0 and t % per_bank == 0), last=(step == 1))
                        if step == 1:
                            mm.then_inc(bank_full, 1)

            e.wait_ge(cleared, 5)
            e.wait_ge(setup, 6)

            def turns(i, q, layer):
                for name, src, ready in (("hi", hh[q], hh_ready), ("lo", hl[q], hl_ready)):
                    dst = into(i, (f"{name}{layer}", q, 0))
                    dst = dst[:].bitcast(F16).rearrange("p (k n) -> p k n", k=KD)
                    e.wait_ge(ready, ln(i, layer, q) + 1)
                    for k in range(KD):
                        for t in range(T):
                            mm = e.transpose(dst[:, k, cut(t)], src[:, t, cut(k)], ident16[:])
                    mm.then_inc(bank_full, 1)

            def layer1(i, q):
                e.wait_ge(hl_ready, ln(i, 1, q) + 1)
                for d in range(KD):
                    key = ("agg", q, d)
                    dst = into(i, key)
                    for h, half in enumerate(halves):
                        blocks = range(h * T // 2, (h + 1) * T // 2)
                        if d == 0:
                            e.wait_ge(adjt_loaded[q][h], i * 16 + 16)
                        for t in blocks:
                            for a, dia in ((hh[q], diah), (hh[q], dial), (hl[q], diah)):
                                e.matmul(dst[:, cut(t)], a[:, t, cut(d)], dia[:], stop=False, skip_group_check=True,
                                         start=(t == blocks[0] and a is hh[q] and dia is diah))
                        for t in range(T):
                            for a in (hh[q], hl[q]):
                                mm = e.matmul(dst[:, half], a[:, t, cut(d)], adjt[q][:, t, half], start=False,
                                              stop=(t == T - 1 and a is hl[q]), skip_group_check=True)
                    mm.then_inc(bank_full, 1)
                def hid(key, step, half):
                    return [(w[:, step, cut(key[2])], m[q][:, step, half]) for w, m in ((w1h, zh), (w1l, zh), (w1h, zl))]
                by_columns(i, [("hid", q, f) for f in range(2)], hid,
                           [(bank_free, free(i, ("agg", q, 0))), (bank_free, free(i, ("agg", q, 1)))])
                for f in range(2, KH):
                    key = ("hid", q, f)
                    dst = into(i, key)
                    for h, half in enumerate(halves):
                        products(dst[:, half], hid(key, 0, half) + hid(key, 1, half), h == len(halves) - 1)

                def mlp(key, step, t):
                    fs = (KH - 1,) if step else range(KH - 1)
                    parts = [(a[q][:, f, cut(t)], w[:, f, :]) for f in fs for a, w in ((hidh, w2h), (hidh, w2l), (hidl, w2h))]
                    return parts + [(ones16[:], bias16[:, 0, :])] * step
                if q == 1:
                    turns(i, 0, 2)
                by_rows(i, [("mlp", q, 0)], mlp, [(bank_free, free(i, ("hid", q, KH - 2))), (bank_free, free(i, ("hid", q, KH - 1)))])
                by_rows(i, [("mlp", q, 1)], mlp, [None, None])

            def layer2(i, q):
                e.wait_ge(bank_free, free(i, ("lo2", q, 0)))
                for d in range(KD):
                    dst = into(i, ("int", q, d))
                    for h, half in enumerate(halves):
                        products(dst[:, half], [(w[:, k, cut(d)], m[q][:, k, half]) for k in range(KD)
                                                for w, m in ((wlh, hth), (wlh, htl), (wll, hth))], h == len(halves) - 1)

                def sim(key, step, half):
                    return [(a[q][:, step, cut(key[2])], m[q][:, step, half])
                            for a, m in ((zh, hth), (zh, htl), (zl, hth))] + [(onesb[:], negrow[q][:, half])] * step
                by_columns(i, [("sim", q, s) for s in range(2)], sim,
                           [(bank_free, free(i, ("int", q, 0))), (bank_free, free(i, ("int", q, 1)))], (neg_ready, i * 2 + q + 1))
                for s in range(2, T + 3):
                    if s < T:
                        key = ("sim", q, s)
                        dst = into(i, key)
                        for h, half in enumerate(halves):
                            products(dst[:, half], sim(key, 0, half) + sim(key, 1, half), h == len(halves) - 1)
                    if s <= T + 1:
                        r = s - 2
                        dst = into(i, ("turn", q, r))
                        e.wait_ge(prob_done, sims(i, q, r) + 1)
                        for t in range(T):
                            mm = e.transpose(dst[:, cut(t)], y[:, r % 2, cut(t)], ident[:])
                        mm.then_inc(bank_full, 1)
                    if s == T + 1:
                        turns(i, *((1, 2), (0, 3))[q])
                    if s >= 3:
                        r = s - 3
                        dst = into(i, ("pv", q, r))
                        e.wait_ge(bank_free, free(i, ("turn", q, r)))
                        products(dst[:, 0:D], [(a[:, r % 2, t, :], m[q][:, t, :]) for t in range(T)
                                               for a, m in ((pth, hh), (pth, hl), (ptl, hh))], True)

            def layer3(i, q):
                e.wait_ge(bank_free, free(i, ("lo3", q, 0)))
                for g in range(2):
                    dst = into(i, ("sup", q, g))
                    for t in range(T // 2):
                        products(dst[:, t * D:(t + 1) * D],
                                 [(a[q][:, k, cut(g * T // 2 + t)], w[:, k, :]) for k in range(KD)
                                  for a, w in ((hth, w3h), (hth, w3l), (htl, w3h))], t == T // 2 - 1)

                def outs(key, step, t):
                    parts = [(adjt[q][:, m, cut(t)], sp[:, m, :]) for m in range(step * T // 2, (step + 1) * T // 2)
                             for sp in (suph[q], supl[q])]
                    return parts + [(ones16[:], bias16[:, 1, :])] * step
                by_rows(i, [("out", q, 0)], outs, [(bank_free, free(i, ("sup", q, 0))), (bank_free, free(i, ("sup", q, 1)))])
                if q == 0:
                    turns(i, 1, 3)
                by_rows(i, [("out", q, 1)], outs, [None, None])

            with e.Fori(0, PAIRS) as i:
                for layer in (layer1, layer2, layer3):
                    for q in range(2):
                        layer(i, q)

        @block.scalar
        def _(e):
            def exp_z(b):
                e.wait_ge(z_min, b + 1)
                e.activation(z[:], z[:], ACT.Exp).then_inc(z_exp, 1)

            def h_values(i, layer, q):
                n = ln(i, layer, q)
                if (layer, q) == (2, 0):
                    e.wait_ge(hl_ready, n)
                e.wait_ge(ln_shift, n + 1)
                for t in range(T):
                    e.activation(h32[layer, q][:, t, :], normed(layer, q)[:, t, :], ACT.Relu, bias=shift[:, t:t + 1],
                                 scale=rstd[:, t:t + 1]).then_inc(h_ready, 1)

            def h_high(i, layer, q):
                n = ln(i, layer, q)
                e.wait_ge(h_ready, n * T + T)
                e.activation(hh[q][:], h32[layer, q][:], ACT.Copy).then_inc(hh_ready, 1)

            def high(i, key, dst, src, func=ACT.Copy, **more):
                e.wait_ge(bank_full, full(i, key))
                e.activation(dst, src, func, **more).then_inc(hi_done, 1)

            def turned(i, q, layer):
                key = (f"hi{layer}", q, 0)
                high(i, key, hth[q][:], tile(key)[:].bitcast(F16).rearrange("p (k n) -> p k n", k=KD))

            def hidden(i, q, f):
                key = ("hid", q, f)
                high(i, key, hidh[q][:, f, :], tile(key)[:], ACT.Relu, bias=b1[:, f:f + 1])

            def layer1(i, q):
                n, m = ((1, 1), (2, 0))[q]
                h_values(i, n, m)
                if q == 0:
                    e.wait_ge(x_moved, i + 1)
                else:
                    h_high(i, n, m)
                for d in range(KD):
                    high(i, ("agg", q, d), zh[q][:, d, :], tile(("agg", q, d))[:])
                    if d == 0 and q == 0:
                        h_high(i, n, m)
                for f in range(KH):
                    key = ("hid", q, f)
                    e.wait_ge(bank_full, full(i, key))
                    if f >= 2 or q == 1:
                        e.wait_ge(bank_free, free(i, ("hid", q, f - 2) if f >= 2 else ("hid", 0, f + 2)))
                    else:
                        e.wait_ge(hl_ready, ln(i, 1, 0) + 1)
                    e.activation(hid32[:, f % 2, :], tile(key)[:], ACT.Relu, bias=b1[:, f:f + 1]).then_inc(hid32_done, 1)
                if q == 1:
                    turned(i, 0, 2)

            def layer2(i, q, last):
                n, m = ((2, 1), (3, 0))[q]
                for d in range(KD):
                    high(i, ("int", q, d), zh[q][:, d, :], tile(("int", q, d))[:])
                for s in range(T + 2):
                    if s >= 2:
                        r = s - 2
                        if r >= 2:
                            e.wait_ge(bank_full, full(i, ("pv", q, r - 2)))
                        key = ("turn", q, r)
                        high(i, key, pth[:, r % 2], tile(key)[:].rearrange("p (t n) -> p t n", t=T))
                    if s < T:
                        e.wait_ge(max_done, sims(i, q, s) + 1)
                        e.activation(y[:, s % 2, :], y[:, s % 2, :], ACT.Exp, bias=negmax[:, s % 2:s % 2 + 1],
                                     accum_out=rowsum[:, s % 4:s % 4 + 1]).then_inc(prob_done, 1)
                    if s == 2:
                        h_values(i, n, m)
                    if s == 3:
                        h_high(i, n, m)
                    if s == 6 and q == 1 and not last:
                        exp_z(i * 2 + 2)
                turned(i, *((1, 2), (0, 3))[q])

            def layer3(i, q, last):
                for g in range(2):
                    key = ("sup", q, g)
                    high(i, key, suph[q][:, g * T // 2:(g + 1) * T // 2, :], tile(key)[:].rearrange("p (t d) -> p t d", d=D))
                if q == 0:
                    h_values(i, 3, 1)
                    h_high(i, 3, 1)
                    turned(i, 1, 3)
                elif not last:
                    h_values(i + 1, 1, 0)
                    h_high(i + 1, 1, 0)
                    exp_z(i * 2 + 3)

            def pair(i, last=False):
                for q in range(2):
                    layer1(i, q)
                for q in range(2):
                    layer2(i, q, last)
                for q in range(2):
                    layer3(i, q, last)

            exp_z(0)
            h_values(0, 1, 0)
            h_high(0, 1, 0)
            exp_z(1)
            with e.Fori(0, PAIRS - 1) as i:
                pair(i)
            pair(PAIRS - 1, last=True)

        @block.vector
        def _(e):
            e.sem_inc(bank_free, BANKS)
            for n, (h, l, k, width) in enumerate(((w1h, w1l, KD, H), (w2h, w2l, KH, D), (wlh, wll, KD, D), (w3h, w3l, KD, D))):
                e.wait_ge(w_loaded, 16 * n + 16)
                src = stage32[:, 0:k * width].rearrange("p (k o) -> p k o", k=k)
                split(e, h[:], l[:], src, (w_hi, n + 1), w_lo)
            e.wait_ge(bias_moved, 64)
            e.wait_ge(cleared, 5)
            e.tensor_copy(bias16[0:1], bias32[0:1]).then_inc(setup, 1)
            e.wait_ge(setup, 1)
            e.tensor_tensor(bias_lo[0:1], bias32[0:1], bias16[0:1], ALU.subtract).then_inc(setup, 1)
            e.tensor_scalar(eps1[:], eps1[:], 1.0, None, ALU.add).then_inc(setup, 1)
            e.wait_ge(setup, 3)
            e.tensor_scalar(dia32, ident[:], eps1[:], None, ALU.mult).then_inc(setup, 1)
            e.wait_ge(setup, 4)
            e.tensor_copy(diah[:], dia32).then_inc(setup, 1)
            e.wait_ge(setup, 5)
            e.wait_ge(bias_moved, 80)
            e.tensor_tensor(dial[:], dia32, diah[:], ALU.subtract).then_inc(setup, 1)

            def split_signs(b, q, i):
                e.wait_ge(z_ready, b + 1)
                e.wait_ge(x_loaded[q], i * 16 + 16)
                e.scalar_tensor_tensor(zx[q][:], z[:], 0.0, zx[q][:], ALU.max, ALU.add).then_inc(x_plus, 1)
                e.tensor_scalar(z[:], z[:], 0.0, None, ALU.min).then_inc(z_min, 1)

            def join_signs(b, q, dst):
                e.wait_ge(x_plus, b + 1)
                e.wait_ge(z_exp, b + 1)
                e.scalar_tensor_tensor(dst, z[:], -1.0, zx[q][:], ALU.add, ALU.add).then_inc(x_first, 1)

            def stats(i, layer, q):
                row_stats(e, ln(i, layer, q), T, D, lambda t: normed(layer, q)[:, t, :], st, small, sums, ve,
                          (ln_stats, ln_small, ln_var))

            def shifts(i, layer, q):
                n = ln(i, layer, q)
                e.wait_ge(ln_rstd, n + 1)
                e.scalar_tensor_tensor(shift[:], sums[:], -0.5, rstd[:], ALU.mult, ALU.mult).then_inc(ln_shift, 1)

            def h_low(i, layer, q):
                e.wait_ge(hh_ready, ln(i, layer, q) + 1)
                e.tensor_tensor(hl[q][:], h32[layer, q][:], hh[q][:], ALU.subtract).then_inc(hl_ready, 1)

            def low(i, key, dst, src, high):
                e.wait_ge(hi_done, hi(i, key))
                e.tensor_tensor(dst, src, high, ALU.subtract).then_inc(bank_free, 1)

            def z_low(i, key):
                name, q, d = key
                low(i, key, zl[q][:, d, :], tile(key)[:], zh[q][:, d, :])

            def hidden_low(i, q, f):
                n = (i * 2 + q) * KH + f
                e.wait_ge(hid32_done, n + 1)
                e.tensor_copy(hidh[q][:, f, :], hid32[:, f % 2, :]).then_inc(hidh_done, 1)
                e.wait_ge(hidh_done, n + 1)
                e.tensor_tensor(hidl[q][:, f, :], hid32[:, f % 2, :], hidh[q][:, f, :], ALU.subtract).then_inc(bank_free, 1)

            def sup_low(i, q, g):
                key = ("sup", q, g)
                part = slice(g * T // 2, (g + 1) * T // 2)
                low(i, key, supl[q][:, part, :], tile(key)[:].rearrange("p (t d) -> p t d", d=D), suph[q][:, part, :])

            def inverse(i, q, r):
                e.wait_ge(prob_done, sims(i, q, r) + 1)
                e.reciprocal(rinv[:, r % 4:r % 4 + 1], rowsum[:, r % 4:r % 4 + 1]).then_inc(rinv_done, 1)

            def turned(i, q, layer):
                key = (f"lo{layer}", q, 0)
                e.wait_ge(hi_done, hi(i, (f"hi{layer}", q, 0)))
                e.wait_ge(bank_full, full(i, key))
                e.tensor_copy(htl[q][:], tile(key)[:].bitcast(F16).rearrange("p (k n) -> p k n", k=KD)).then_inc(bank_free, 2)

            def add(i, key, q, g):
                e.wait_ge(bank_full, full(i, key))
                rows = xs[q][:, g * T // 2:(g + 1) * T // 2, :]
                e.tensor_tensor(rows, tile(key)[:].rearrange("p (t d) -> p t d", d=D), rows, ALU.add).then_inc(bank_free, 1)

            def masks(i, q):
                b = i * 2 + q
                e.wait_ge(mask_loaded, b * 16 + 16)
                e.tensor_scalar(nomask[q][:], maski[:], 0, None, ALU.is_equal).then_inc(mask_ready, 1)
                e.wait_ge(mask_ready, 2 * b + 1)
                e.tensor_scalar(kept[q][:], nomask[q][:], -1.0, 1.0, ALU.mult, ALU.add).then_inc(mask_ready, 1)
                e.tensor_scalar(negrow[q][0:1, :], nomask[q][0:1, :], NEG, None, ALU.mult).then_inc(neg_ready, 1)

            def move_x(i):
                after(e, stored[0], 16 * i)
                e.wait_ge(x_first, 2 * i + 1)
                e.tensor_copy(xs[0][:], zx[0][:]).then_inc(x_moved, 1)

            def layer1(i, q):
                if q == 0:
                    e.wait_ge(stored[1], i * 16)
                    join_signs(i * 2 + 1, 1, xs[1][:])
                    e.wait_ge(x_first, i * 2 + 2)
                    stats(i, 1, 1)
                    shifts(i, 1, 1)
                    z_low(i, ("agg", 0, 0))
                    h_low(i, 1, 1)
                    z_low(i, ("agg", 0, 1))
                else:
                    stats(i, 2, 0)
                    shifts(i, 2, 0)
                    h_low(i, 2, 0)
                    for d in range(KD):
                        z_low(i, ("agg", 1, d))
                for f in range(KH):
                    hidden_low(i, q, f)
                if q == 1:
                    turned(i, 0, 2)
                masks(i, q)
                for g in range(2):
                    add(i, ("mlp", q, g), q, g)
                e.wait_ge(bank_free, free(i, ("mlp", q, 1)))

            def layer2(i, q, last):
                norm = ((2, 1), (3, 0))[q]
                for d in range(KD):
                    z_low(i, ("int", q, d))
                for s in range(T + 3):
                    if s < T:
                        key = ("sim", q, s)
                        n = sims(i, q, s)
                        e.wait_ge(bank_full, full(i, key))
                        e.wait_ge(row_masked, n + 1)
                        if s >= 2:
                            e.wait_ge(bank_full, full(i, ("turn", q, s - 2)))
                            inverse(i, q, s - 2)
                        else:
                            e.wait_ge(held, 2 * (i * 2 + q) + s)
                            e.memset(hold[:], 0.0).then_inc(held, 1)
                        e.tensor_tensor_reduce(y[:, s % 2, :], tile(key)[:], adjr[:, (q * T + s) % RING, :], 1.0, -BIG,
                                               ALU.mult, ALU.max, rowmax[:, s % 2:s % 2 + 1]).then_inc(bank_free, 1)
                        e.wait_ge(bank_free, free(i, key))
                        e.tensor_scalar(negmax[:, s % 2:s % 2 + 1], rowmax[:, s % 2:s % 2 + 1], -1.0, None,
                                        ALU.mult).then_inc(max_done, 1)
                    if 2 <= s <= T + 1:
                        r = s - 2
                        if s >= T:
                            inverse(i, q, r)
                        key = ("turn", q, r)
                        low(i, key, ptl[:, r % 2], tile(key)[:].rearrange("p (t n) -> p t n", t=T), pth[:, r % 2])
                    if s == T + 1:
                        turned(i, *((1, 2), (0, 3))[q])
                    if s >= 3:
                        r = s - 3
                        e.wait_ge(rinv_done, sims(i, q, r) + 1)
                        e.wait_ge(bank_full, full(i, ("pv", q, r)))
                        e.scalar_tensor_tensor(xs[q][:, r, :], tile(("pv", q, r))[:, 0:D], rinv[:, r % 4:r % 4 + 1],
                                               xs[q][:, r, :], ALU.mult, ALU.add).then_inc(bank_free, 1)
                    if s == 1:
                        stats(i, *norm)
                    if s == 2:
                        shifts(i, *norm)
                    if s == 4:
                        h_low(i, *norm)
                    if s == 5 and q == 1 and not last:
                        split_signs(i * 2 + 2, 0, i + 1)
                e.wait_ge(bank_free, free(i, ("pv", q, T - 1)))

            def layer3(i, q, last):
                if q == 0:
                    stats(i, 3, 1)
                    sup_low(i, q, 0)
                    shifts(i, 3, 1)
                    sup_low(i, q, 1)
                    if not last:
                        join_signs(i * 2 + 2, 0, zx[0][:])
                    h_low(i, 3, 1)
                    add(i, ("out", 0, 0), 0, 0)
                    turned(i, 1, 3)
                    if not last:
                        e.wait_ge(x_first, i * 2 + 3)
                        stats(i + 1, 1, 0)
                    add(i, ("out", 0, 1), 0, 1)
                else:
                    if not last:
                        shifts(i + 1, 1, 0)
                    for g in range(2):
                        sup_low(i, q, g)
                    if not last:
                        h_low(i + 1, 1, 0)
                    add(i, ("out", 1, 0), 1, 0)
                    if not last:
                        split_signs(i * 2 + 3, 1, i + 1)
                        move_x(i + 1)
                    add(i, ("out", 1, 1), 1, 1)

            def pair(i, last=False):
                for q in range(2):
                    layer1(i, q)
                for q in range(2):
                    layer2(i, q, last)
                for q in range(2):
                    layer3(i, q, last)

            split_signs(0, 0, 0)
            join_signs(0, 0, zx[0][:])
            e.wait_ge(x_first, 1)
            stats(0, 1, 0)
            shifts(0, 1, 0)
            move_x(0)
            h_low(0, 1, 0)
            split_signs(1, 1, 0)
            with e.Fori(0, PAIRS - 1) as i:
                pair(i)
            pair(PAIRS - 1, last=True)


def graph_layers(nc, x, adj, adj_t, mask, wt, w, a12, vecs, g3b3, w1, w2, wl2, w3, b1c, b2r, b3r, eps, out):
    S = Shapes(x, w1)
    B, N, D, T, KD = S.B, S.N, S.D, S.T, S.KD
    dram = lambda name, shape, dt: nc.dram_tensor(name, shape, dt, kind="Internal").ap()
    wh_dram = dram("wh_dram", [B, P, 2, T, D], F16)
    hp_dram = dram("hp_dram", [B, P, T, D], F32)
    e_dram = dram("e_dram", [P, P], F32)
    e9_dram = dram("e9_dram", [9, P, P], BF16)
    ab9_dram = dram("ab9_dram", [9, 2, T, P], BF16)
    gd_dram = dram("gd_dram", [2, 3, P, P], BF16)
    s_dram = dram("s_dram", [T, P], F32)
    with ExitStack() as ctx:
        sb = lambda name, shape, dt: ctx.enter_context(nc.sbuf_tensor(name, shape, dt))
        keep = {
            "ident": sb("ident", [P, P], F32),
            "ident16": sb("ident16", [P, P], F16),
            "ones": sb("ones", [P, P], F32),
            "minus_half": sb("minus_half", [P, T], F32),
            "norm3": sb("norm3", [P, 2, D], F32),
        }
        with ExitStack() as first:
            fsb = lambda name, shape, dt: first.enter_context(nc.sbuf_tensor(name, shape, dt))
            keep["ecol"] = fsb("ecol", [P, T, B], F32)
            keep["fcol"] = fsb("fcol", [P, T, B], F32)
            keep["C"] = fsb("att_shift", [P, T, B], F32)
            nodes_block(nc, S, x, wt, w, a12, keep, wh_dram)
            tables_block(nc, S, vecs, keep, e9_dram, e_dram, ab9_dram, gd_dram, s_dram)
        attend_block(nc, S, adj, keep, wh_dram, e9_dram, ab9_dram, gd_dram, s_dram, hp_dram, g3b3)
        layers_block(nc, S, x, adj, adj_t, mask, w1, w2, wl2, w3, b1c, b2r, b3r, eps, keep, hp_dram, out)


def kernel(**inputs):
    import numpy as np
    import concourse.bacc as bacc
    from concourse.bass_utils import run_bass_kernel_spmd

    a = {k: np.asarray(v) for k, v in inputs.items()}
    column = lambda v: v.reshape(-1, P).T
    arrays = {
        "x": a["x"],
        "adj": a["adj"],
        "adj_t": a["adj"].transpose(0, 2, 1),
        "mask": a["nodemask"],
        "wt": a["L0_gnn_W"].T,
        "w": a["L0_gnn_W"],
        "a12": np.stack([column(a["L0_gnn_a1"]), column(a["L0_gnn_a2"])], axis=2).reshape(P, -1),
        "vecs": np.concatenate([column(a[f"L0_gnn_{n}"]) for n in ("g1", "b1", "g2", "b2")], axis=1),
        "g3b3": np.concatenate([column(a["L0_gnn_g3"]), column(a["L0_gnn_b3"])], axis=1),
        "w1": a["L1_gnn_W1"],
        "w2": a["L1_gnn_W2"],
        "wl2": a["L2_gnn_W"],
        "w3": a["L3_gnn_weight"],
        "b1c": column(a["L1_gnn_b1"]),
        "b2r": a["L1_gnn_b2"].reshape(1, -1),
        "b3r": a["L3_gnn_bias"].reshape(1, -1),
        "eps": a["L1_gnn_eps"],
    }
    arrays = {f"in_{k}": np.ascontiguousarray(v) for k, v in arrays.items()}
    nc = bacc.Bacc("TRN2", target_bir_lowering=False, num_devices=1)
    args = [nc.dram_tensor(k, v.shape, mybir.dt.from_np(v.dtype), kind="ExternalInput").ap() for k, v in arrays.items()]
    out = nc.dram_tensor("out", a["x"].shape, F32, kind="ExternalOutput").ap()
    graph_layers(nc, *args, out)
    result = run_bass_kernel_spmd(nc, [arrays], core_ids=[0])
    return result.results[0]["out"]
```

```python
from contextlib import ExitStack

import concourse.bass as bass
from concourse import mybir

ACT = mybir.ActivationFunctionType
ALU = mybir.AluOpType
F32 = mybir.dt.float32
F16 = mybir.dt.float16
BF16 = mybir.dt.bfloat16
I32 = mybir.dt.int32
AX = mybir.AxisListType.X

P = 128
EPS = 1e-5
SLOPE = 0.2
NEG = -1e30
BIG = 3.0e38


class Shapes:
    def __init__(self, x, w1):
        self.B, self.N, self.D = x.shape
        self.H = w1.shape[1]
        self.T = self.N // P
        self.KD = self.D // P
        self.KH = self.H // P


FIRST = 1


def after(e, sem, value):
    if not isinstance(value, int) or value > 0:
        e.wait_ge(sem, value)


def row_stats(e, n, T, D, x_rows, st, small, sums, ve, sems):
    for t in range(T):
        e.bn_stats(st[:, t, :], x_rows(t)).then_inc(sems[0], 1)
    row_stats_end(e, n, T, D, st, small, sums, ve, sems)


def row_stats_end(e, n, T, D, st, small, sums, ve, sems):
    ln_stats, ln_small, ln_var = sems
    e.wait_ge(ln_stats, n * T + T)
    e.tensor_tensor(sums[:], st[:, :, 1], st[:, :, 4], ALU.add).then_inc(ln_small, 1)
    e.tensor_tensor(small[:, 0, :], st[:, :, 1], st[:, :, 4], ALU.subtract).then_inc(ln_small, 1)
    e.tensor_tensor(small[:, 1, :], st[:, :, 2], st[:, :, 5], ALU.add).then_inc(ln_small, 1)
    e.wait_ge(ln_small, n * 5 + 3)
    e.tensor_tensor(small[:, 2, :], small[:, 0, :], small[:, 0, :], ALU.mult).then_inc(ln_small, 1)
    e.wait_ge(ln_small, n * 5 + 4)
    e.scalar_tensor_tensor(small[:, 3, :], small[:, 2, :], D / 4.0, small[:, 1, :], ALU.mult, ALU.add).then_inc(ln_small, 1)
    e.wait_ge(ln_small, n * 5 + 5)
    e.tensor_scalar(ve[:], small[:, 3, :], 1.0 / D, EPS, ALU.mult, ALU.add).then_inc(ln_var, 1)


def split(e, hi, lo, src, copied, done):
    e.tensor_copy(hi, src).then_inc(copied[0], 1)
    e.wait_ge(copied[0], copied[1])
    e.tensor_tensor(lo, src, hi, ALU.subtract).then_inc(done, 1)


def nodes_block(nc, S, x, wt, w, a12, keep, wh_dram):
    B, N, D, T, KD = S.B, S.N, S.D, S.T, S.KD
    PAIRS = B // 2
    with ExitStack() as ctx:
        sb = lambda name, shape, dt: ctx.enter_context(nc.sbuf_tensor(name, shape, dt))
        ps = lambda name, shape, dt: ctx.enter_context(nc.psum_tensor(name, shape, dt))
        sem = lambda name: ctx.enter_context(nc.semaphore(name))
        xin = [sb(f"a_xin{q}", [P, T, D], F32) for q in range(2)]
        wt32 = sb("a_wt32", [P, KD, D], F32)
        w32 = sb("a_w32", [P, KD, D], F32)
        a32 = sb("a_a32", [P, KD, 2], F32)
        wt_hi = sb("a_wt_hi", [P, KD, D], F16)
        wt_lo = sb("a_wt_lo", [P, KD, D], F16)
        u32 = sb("a_u32", [P, KD, 2], F32)
        u_hi = sb("a_u_hi", [P, KD, 2], F16)
        u_lo = sb("a_u_lo", [P, KD, 2], F16)
        st = sb("a_st", [P, T, 6], F32)
        small = sb("a_small", [P, 4, T], F32)
        sums = [sb(f"a_sums{q}", [P, T], F32) for q in range(2)]
        ve = sb("a_ve", [P, T], F32)
        rstd = sb("a_rstd", [P, 2, T], F32)
        shift = sb("a_shift", [P, 2, T], F32)
        h32 = sb("a_h32", [P, T, D], F32)
        hh = [sb(f"a_hh{q}", [P, T, D], F16) for q in range(2)]
        hl = sb("a_hl", [P, T, D], F16)
        hth = [sb(f"a_hth{q}", [P, KD, N], F16) for q in range(2)]
        htl = [sb(f"a_htl{q}", [P, KD, N], F16) for q in range(2)]
        wh = [sb(f"a_wh{q}", [P, 2, T, D], F16) for q in range(2)]
        pt_hi = ps("a_pt_hi", [P, KD, N], F16)
        pt_lo = ps("a_pt_lo", [P, KD, N], F16)
        PW = 2
        pw = [ps(f"a_pw{k}", [P, 2, D], F32) for k in range(PW)]
        bank_of = lambda q, g: pw[(q * (T // 2) + g) % PW]
        pe_ef = ps("a_pe_ef", [P, 256], F32)
        ef_ps = pe_ef[:, 0:2 * T].rearrange("p (t c) -> p t c", c=2)
        u_ps = ps("a_u_ps", [P, 512], F32)
        u_psv = u_ps[:, 0:2 * KD].rearrange("p (k c) -> p k c", c=2)

        w_loaded = sem("a_w_loaded")
        x_loaded = [sem(f"a_x_loaded{q}") for q in range(2)]
        consts = sem("a_consts")
        w_hi_done, w_lo_done = sem("a_w_hi_done"), sem("a_w_lo_done")
        u_done = sem("a_u_done")
        u_copied = sem("a_u_copied")
        ln_stats, ln_small, ln_var = sem("a_ln_stats"), sem("a_ln_small"), sem("a_ln_var")
        ln_rstd, ln_shift = sem("a_ln_rstd"), sem("a_ln_shift")
        h_ready, hh_ready, hl_ready = sem("a_h_ready"), sem("a_hh_ready"), sem("a_hl_ready")
        pt_hi_done, pt_lo_done = sem("a_pt_hi_done"), sem("a_pt_lo_done")
        hth_ready, htl_ready = sem("a_hth_ready"), sem("a_htl_ready")
        pw_done, whh_ready, pw_free = sem("a_pw_done"), sem("a_whh_ready"), sem("a_pw_free")
        ef_done, ef_ready = sem("a_ef_done"), sem("a_ef_ready")
        wh_stored = [sem(f"a_wh_stored{q}") for q in range(2)]
        block = ctx.enter_context(nc.Block())
        ident, ident16 = keep["ident"], keep["ident16"]
        G = T // 2

        @block.sync
        def _(e):
            load = lambda b, q: e.dma_start(
                xin[q][:], x[b].rearrange("(t p) d -> p t d", p=P)).then_inc(x_loaded[q], 16)
            load(0, 0)
            e.dma_start(wt32[:], wt.rearrange("(k p) o -> p k o", p=P)).then_inc(w_loaded, 16)
            e.dma_start(w32[:], w.rearrange("(k p) f -> p k f", p=P)).then_inc(w_loaded, 16)
            e.dma_start(a32[:], a12.rearrange("p (k c) -> p k c", c=2)).then_inc(w_loaded, 16)
            load(1, 1)
            with e.Fori(0, PAIRS - 1) as i:
                for q in range(2):
                    b = i * 2 + q
                    e.wait_ge(h_ready, b * T + T)
                    load(b + 2, q)

        @block.gpsimd
        def _(e):
            e.memset(ident[:], 0.0).then_inc(consts, 1)
            e.wait_ge(consts, 1)
            e.affine_select(out=ident[:], in_=ident[:], compare_op=ALU.not_equal, fill=1.0,
                            base=0, pattern=[[-1, P]], channel_multiplier=1).then_inc(consts, 1)
            e.memset(keep["minus_half"][:], -0.5).then_inc(consts, 1)
            e.memset(keep["ones"][:], 1.0).then_inc(consts, 1)
            e.wait_ge(consts, 4)
            e.tensor_copy(ident16[:], ident[:]).then_inc(consts, 1)
            e.wait_ge(consts, 5)

            def rstds(b, q):
                e.wait_ge(ln_var, b + 1)
                after(e, h_ready, (b - 1) * T)
                e.tensor_tensor(rstd[:, q, :], ve[:], keep["minus_half"][:, 0:T], ALU.pow).then_inc(ln_rstd, 1)

            for q in range(2):
                rstds(q, q)
            with e.Fori(1, PAIRS) as i:
                for q in range(2):
                    rstds(i * 2 + q, q)

        @block.vector
        def _(e):
            e.sem_inc(pw_free, PW)
            for first in (ef_done, ef_ready, *wh_stored):
                e.sem_inc(first, FIRST)

            def stats(b, q, i):
                e.wait_ge(x_loaded[q], i * 16 + 16)
                row_stats(e, b, T, D, lambda t: xin[q][:, t, :], st, small, sums[q], ve, (ln_stats, ln_small, ln_var))

            def shifts(b, q):
                e.wait_ge(ln_rstd, b + 1)
                e.scalar_tensor_tensor(shift[:, q, :], sums[q][:], -0.5, rstd[:, q, :],
                                       ALU.mult, ALU.mult).then_inc(ln_shift, 1)

            def h_low(b, q):
                e.wait_ge(hh_ready, b + 1)
                after(e, pt_lo_done, b)
                e.tensor_tensor(hl[:], h32[:], hh[q][:], ALU.subtract).then_inc(hl_ready, 1)

            def turned(b, q):
                e.wait_ge(pt_hi_done, b + 1)
                after(e, ef_done, b - 1 + FIRST)
                e.tensor_copy(hth[q][:], pt_hi[:]).then_inc(hth_ready, 1)

            def step(b, i, q, ahead=3):
                if ahead >= 2:
                    shifts(b + 2, q)
                if ahead:
                    turned(b + 1, 1 - q)
                for g in range(G):
                    if g == 3 and ahead == 3:
                        stats(b + 3, 1 - q, i + 1 + q)
                    e.wait_ge(whh_ready, b * G + g + 1)
                    e.tensor_tensor(wh[q][:, 1, 2 * g:2 * g + 2, :], bank_of(q, g)[:],
                                    wh[q][:, 0, 2 * g:2 * g + 2, :], ALU.subtract).then_inc(pw_free, 1)
                    if g == 3 and ahead >= 2:
                        h_low(b + 2, q)
                e.wait_ge(ef_done, b + 1 + FIRST)
                for c, col in enumerate((keep["ecol"], keep["fcol"])):
                    e.tensor_copy(col[:, :, bass.ds(b, 1)] if not isinstance(b, int) else col[:, :, b:b + 1],
                                  ef_ps[:, :, c:c + 1]).then_inc(ef_ready, 1)

            stats(0, 0, 0)
            shifts(0, 0)
            e.wait_ge(w_loaded, 48)
            split(e, wt_hi[:], wt_lo[:], wt32[:], (w_hi_done, 1), w_lo_done)
            stats(1, 1, 0)
            h_low(0, 0)
            shifts(1, 1)
            e.wait_ge(u_done, 1)
            e.tensor_copy(u32[:], u_psv).then_inc(u_copied, 1)
            e.wait_ge(u_copied, 1)
            split(e, u_hi[:], u_lo[:], u32[:], (w_hi_done, 2), w_lo_done)
            turned(0, 0)
            h_low(1, 1)
            stats(2, 0, 1)
            with e.Fori(0, PAIRS - 2) as i:
                for q in range(2):
                    step(i * 2 + q, i, q)
            for b in range(B - 4, B):
                step(b, b // 2, b % 2, ahead=min(3, B - 1 - b))

        @block.scalar
        def _(e):
            def h_values(b, q):
                e.wait_ge(ln_shift, b + 1)
                after(e, hl_ready, b)
                for t in range(T):
                    e.activation(h32[:, t, :], xin[q][:, t, :], ACT.Relu, bias=shift[:, q, t:t + 1],
                                 scale=rstd[:, q, t:t + 1]).then_inc(h_ready, 1)

            def h_high(b, q):
                e.wait_ge(h_ready, b * T + T)
                after(e, pt_hi_done, b - 1)
                e.activation(hh[q][:], h32[:], ACT.Copy).then_inc(hh_ready, 1)

            def turned(b, q):
                e.wait_ge(pt_lo_done, b + 1)
                after(e, ef_done, b - 1 + FIRST)
                e.activation(htl[q][:], pt_lo[:], ACT.Copy).then_inc(htl_ready, 1)

            def step(b, i, q, ahead=3):
                after(e, wh_stored[q], i * 16 + FIRST)
                for g in range(G):
                    e.wait_ge(pw_done, b * G + g + 1)
                    e.activation(wh[q][:, 0, 2 * g:2 * g + 2, :], bank_of(q, g)[:],
                                 ACT.Copy).then_inc(whh_ready, 1)
                    if g == 1 and ahead >= 2:
                        h_values(b + 2, q)
                    if g == 2 and ahead >= 2:
                        h_high(b + 2, q)
                if ahead:
                    turned(b + 1, 1 - q)
                e.wait_ge(pw_free, b * G + G + PW)
                e.dma_start(wh_dram[b], wh[q][:]).then_inc(wh_stored[q], 16)

            for q in range(2):
                h_values(q, q)
                h_high(q, q)
            turned(0, 0)
            with e.Fori(0, PAIRS - 1) as i:
                for q in range(2):
                    step(i * 2 + q, i, q)
            for q in range(2):
                step(B - 2 + q, PAIRS - 1, q, ahead=1 - q)
            for q in range(2):
                e.wait_ge(wh_stored[q], 16 * PAIRS + FIRST)

        @block.tensor
        def _(e):
            e.wait_ge(w_loaded, 48)
            for f in range(KD):
                for k in range(KD):
                    mm = e.matmul(u_psv[:, f, :], w32[:, k, f * P:(f + 1) * P], a32[:, k, :],
                                  start=(k == 0), stop=(k == KD - 1))
            mm.then_inc(u_done, 1)
            e.wait_ge(consts, 5)
            e.wait_ge(w_lo_done, 2)

            def turns(b, src, dst, ready, done, free):
                e.wait_ge(ready, b + 1)
                after(e, free, b)
                for k in range(KD):
                    for t in range(T):
                        mm = e.transpose(dst[:, k, t * P:(t + 1) * P], src[:, t, k * P:(k + 1) * P], ident16[:])
                mm.then_inc(done, 1)

            turn_high = lambda b, q: turns(b, hh[q], pt_hi, hh_ready, pt_hi_done, hth_ready)
            turn_low = lambda b: turns(b, hl, pt_lo, hl_ready, pt_lo_done, htl_ready)

            def step(b, q, ahead=True):
                if ahead:
                    turn_high(b + 1, 1 - q)
                e.wait_ge(hth_ready, b + 1)
                e.wait_ge(htl_ready, b + 1)
                hi, lo = hth[q], htl[q]
                for g in range(G):
                    e.wait_ge(pw_free, b * G + g + 1)
                    for t in (2 * g, 2 * g + 1):
                        parts = [(ht, wp, k) for k in range(KD) for ht, wp in ((hi, wt_hi), (hi, wt_lo), (lo, wt_hi))]
                        for n, (ht, wp, k) in enumerate(parts):
                            mm = e.matmul(bank_of(q, g)[:, t % 2, :], ht[:, k, t * P:(t + 1) * P], wp[:, k, :],
                                          start=(n == 0), stop=(n == len(parts) - 1))
                    mm.then_inc(pw_done, 1)
                if ahead:
                    turn_low(b + 1)
                after(e, ef_ready, b * 2 + FIRST)
                for t in range(T):
                    parts = [(ht, up, k) for k in range(KD) for ht, up in ((hi, u_hi), (hi, u_lo), (lo, u_hi))]
                    for n, (ht, up, k) in enumerate(parts):
                        mm = e.matmul(ef_ps[:, t, :], ht[:, k, t * P:(t + 1) * P], up[:, k, :],
                                      start=(n == 0), stop=(n == len(parts) - 1))
                mm.then_inc(ef_done, 1)

            turn_high(0, 0)
            turn_low(0)
            with e.Fori(0, PAIRS - 1) as i:
                for q in range(2):
                    step(i * 2 + q, q)
            for q in range(2):
                step(B - 2 + q, q, ahead=(q == 0))


def tables_block(nc, S, vecs, keep, e9_dram, e_dram, ab9_dram, gd_dram, s_dram):
    B, N, T = S.B, S.N, S.T
    PAIRS = B // 2
    RING = 4
    with ExitStack() as ctx:
        sb = lambda name, shape, dt: ctx.enter_context(nc.sbuf_tensor(name, shape, dt))
        ps = lambda name, shape, dt: ctx.enter_context(nc.psum_tensor(name, shape, dt))
        sem = lambda name: ctx.enter_context(nc.semaphore(name))
        cols = sb("b_cols", [P, 4, T], F32)
        g1, b1, g2, b2 = (cols[:, k, :] for k in range(4))
        esum = sb("b_esum", [P, B], F32)
        ebar = sb("b_ebar", [P, B], F32)
        me = sb("b_me", [P, 1], F32)
        ed = sb("b_ed", [P, T * B], F32)
        esq = sb("b_esq", [P, 2], F32)
        vE = sb("b_vE", [P, 1], F32)
        fbar = sb("b_fbar", [P, T], F32)
        fd = sb("b_fd", [P, T, B], F32)
        fq = sb("b_fq", [P, T, B], F32)
        small = sb("b_small", [P, 16, T], F32)
        var1, ve1, r1, A, mean1, Er, Vr, t1, t2, t3, ve2, r2, A2, C2, k8, sg = (
            small[:, n, :] for n in range(16))
        ebd = sb("b_ebd", [P, B], F32)
        C = keep["C"]
        mv2 = sb("b_mv2", [P, T, 2], F32)
        st2 = sb("b_st2", [P, T, B, 12], F32)
        eb = [sb(f"b_eb{q}", [P, N], F32) for q in range(2)]
        ring = sb("b_ring", [P, RING, N], F32)
        ab = sb("b_ab", [P, 3, T], F32)
        gdc = sb("b_gdc", [P, 2, T, B], F32)
        rows = sb("b_rows", [P, 4, P], F32)
        parts = sb("b_parts", [P, 4, 3, P], BF16)
        rest = sb("b_rest", [P, 4, 2, P], F32)
        pm = ps("b_pm", [P, 512], F32)
        pt = ps("b_pt", [P, 4, P], F32)

        loaded, tab, tab_pe, tab_pow = sem("b_loaded"), sem("b_tab"), sem("b_tab_pe"), sem("b_tab_pow")
        e_stored = sem("b_e_stored")
        eb_loaded = [sem(f"b_eb_loaded{q}") for q in range(2)]
        relu_done, stats_done, ring_free = sem("b_relu_done"), sem("b_stats_done"), sem("b_ring_free")
        aggr_done, row_stored = sem("b_aggr_done"), sem("b_row_stored")
        tables_ready, e_parts_ready, rows_ready = sem("b_tables_ready"), sem("b_e_parts"), sem("b_rows_ready")
        block = ctx.enter_context(nc.Block())
        ecol, fcol, ident, ones = keep["ecol"], keep["fcol"], keep["ident"], keep["ones"]
        wide = lambda ap: ap.unsqueeze(2).to_broadcast([P, T, B])

        def store_rows(e, kind):
            e.dma_start(gd_dram[kind].rearrange("k p n -> p k n"), parts[:, 1 + kind]).then_inc(row_stored, 16)
            for c in range(3):
                e.dma_start(ab9_dram[:, kind].rearrange("(k c) t n -> c t k n", c=3)[c],
                            parts[kind * T:(kind + 1) * T, 3]).then_inc(row_stored, 16)

        @block.sync
        def _(e):
            e.dma_start(cols[:], vecs.rearrange("p (k t) -> p k t", k=4)).then_inc(loaded, 16)
            e.wait_ge(e_parts_ready, 1)
            e.dma_start(e_dram, rows[:, 0, :]).then_inc(e_stored, 16)
            for r in range(3):
                e.dma_start(e9_dram[3 * r:3 * r + 3].rearrange("k p n -> p k n"), parts[:, 0]).then_inc(row_stored, 16)
            e.wait_ge(e_stored, 16)
            load = lambda b, q: e.dma_start(
                eb[q][:].rearrange("p (t n) -> p t n", t=T),
                e_dram.rearrange("(t b) n -> b t n", b=B)[b].partition_broadcast(P)).then_inc(eb_loaded[q], 16)
            for q in range(2):
                load(q, q)
            with e.Fori(0, PAIRS - 1) as i:
                for q in range(2):
                    b = i * 2 + q
                    e.wait_ge(relu_done, b * T + T)
                    load(b + 2, q)
            e.wait_ge(rows_ready, 1)
            store_rows(e, 0)
            e.dma_start(s_dram, rows[2 * T:3 * T, 3, :]).then_inc(row_stored, 16)
            e.wait_ge(row_stored, 16 * (3 + 2 + 6 + 1))

        @block.gpsimd
        def _(e):
            e.wait_ge(tab, TAB_VAR1)
            e.tensor_tensor(r1, ve1, keep["minus_half"][:, 0:T], ALU.pow).then_inc(tab_pow, 1)
            e.wait_ge(tab, TAB_VAR2)
            e.tensor_tensor(r2, ve2, keep["minus_half"][:, 0:T], ALU.pow).then_inc(tab_pow, 1)

        @block.tensor
        def _(e):
            e.transpose(pt[:, 0, :], ecol[:].rearrange("p t b -> p (t b)"), ident[:]).then_inc(tab_pe, 1)
            e.wait_ge(tab, 1)
            e.matmul(pm[:, 0:B], ones[:], esum[:], start=True, stop=True).then_inc(tab_pe, 1)
            e.wait_ge(tab, TAB_ESQ)
            e.matmul(pm[:, B:B + 1], ones[:], esq[:, 0:1], start=True, stop=True).then_inc(tab_pe, 1)
            e.wait_ge(tables_ready, 1)
            for kind in range(2):
                e.transpose(pt[:, 1 + kind, :], gdc[:, kind].rearrange("p t b -> p (t b)"), ident[:])
            e.transpose(pt[0:3 * T, 3, :], ab[:].rearrange("p c t -> p (c t)"), ident[:]).then_inc(tab_pe, 1)

        @block.scalar
        def _(e):
            e.wait_ge(tab, TAB_C)
            with e.Fori(0, PAIRS) as i:
                for q in range(2):
                    b = i * 2 + q
                    e.wait_ge(eb_loaded[q], i * 16 + 16)
                    for t in range(T):
                        e.wait_ge(ring_free, b * T + t + 1)
                        e.activation(ring[:, t % RING, :], eb[q][:], ACT.Relu, bias=C[:, t, bass.ds(b, 1)],
                                     scale=A[:, t:t + 1]).then_inc(relu_done, 1)
            e.wait_ge(rows_ready, 1)
            store_rows(e, 1)

        @block.vector
        def _(e):
            n = [0]

            def link(ins):
                n[0] += 1
                ins.then_inc(tab, 1)
                e.wait_ge(tab, n[0])

            e.sem_inc(ring_free, RING)
            link(e.tensor_reduce(esum[:], ecol[:].rearrange("p t b -> p b t"), AX, ALU.add))
            e.wait_ge(tab_pe, 1)
            link(e.tensor_copy(rows[:, 0, :], pt[:, 0, :]))
            link(e.tensor_copy(parts[:, 0, 0, :], rows[:, 0, :]))
            link(e.tensor_tensor(rest[:, 0, 0, :], rows[:, 0, :], parts[:, 0, 0, :], ALU.subtract))
            link(e.tensor_copy(parts[:, 0, 1, :], rest[:, 0, 0, :]))
            link(e.tensor_tensor(rest[:, 0, 1, :], rest[:, 0, 0, :], parts[:, 0, 1, :], ALU.subtract))
            e.tensor_copy(parts[:, 0, 2, :], rest[:, 0, 1, :]).then_inc(e_parts_ready, 1)
            e.wait_ge(tab_pe, 2)
            link(e.tensor_scalar(ebar[:], pm[:, 0:B], 1.0 / N, None, ALU.mult))
            link(e.tensor_reduce(me[:], ebar[:], AX, ALU.add))
            link(e.tensor_scalar(me[:], me[:], 1.0 / B, None, ALU.mult))
            link(e.tensor_scalar(ed[:], ecol[:].rearrange("p t b -> p (t b)"), me[:], None, ALU.subtract))
            link(e.tensor_tensor(ed[:], ed[:], ed[:], ALU.mult))
            link(e.tensor_reduce(esq[:, 0:1], ed[:], AX, ALU.add))
            assert n[0] == TAB_ESQ
            link(e.tensor_reduce(fbar[:], fcol[:], AX, ALU.add))
            link(e.tensor_scalar(fbar[:], fbar[:], 1.0 / B, None, ALU.mult))
            link(e.tensor_tensor(fd[:], fcol[:], wide(fbar[:]), ALU.subtract))
            link(e.tensor_tensor(fq[:], fd[:], fd[:], ALU.mult))
            link(e.tensor_reduce(t1, fq[:], AX, ALU.add))
            link(e.tensor_scalar(ebd[:], ebar[:], me[:], None, ALU.subtract))
            link(e.tensor_tensor(fq[:], fd[:], ebd[:].unsqueeze(1).to_broadcast([P, T, B]), ALU.mult))
            link(e.tensor_reduce(t2, fq[:], AX, ALU.add))
            link(e.scalar_tensor_tensor(t1, t2, 2.0, t1, ALU.mult, ALU.add))
            e.wait_ge(tab_pe, 3)
            link(e.tensor_scalar(vE[:], pm[:, B:B + 1], 1.0 / (N * B), None, ALU.mult))
            link(e.tensor_scalar(var1, t1, 1.0 / B, vE[:], ALU.mult, ALU.add))
            link(e.tensor_scalar(ve1, var1, EPS, None, ALU.add))
            assert n[0] == TAB_VAR1
            e.wait_ge(tab_pow, 1)
            e.wait_ge(loaded, 16)
            link(e.tensor_tensor(A, g1, r1, ALU.mult))
            link(e.tensor_scalar(mean1, fbar[:], me[:], None, ALU.add))
            link(e.tensor_tensor(C[:], fcol[:], wide(mean1), ALU.subtract))
            link(e.tensor_tensor(C[:], C[:], wide(A), ALU.mult))
            link(e.tensor_tensor(C[:], C[:], wide(b1), ALU.add))
            assert n[0] == TAB_C
            half = N // 2
            with e.Fori(0, B) as b:
                for t in range(T):
                    e.wait_ge(relu_done, b * T + t + 1)
                    e.bn_stats(st2[:, t, bass.ds(b, 1), 0:6], ring[:, t % RING, 0:half]).then_inc(stats_done, 1)
                    e.bn_stats(st2[:, t, bass.ds(b, 1), 6:12], ring[:, t % RING, half:N]).then_inc(ring_free, 1)
            e.wait_ge(stats_done, B * T)
            e.wait_ge(ring_free, B * T + RING)
            for t in range(T):
                e.bn_aggr(mv2[:, t, :], st2[:, t].rearrange("p b s -> p (b s)")).then_inc(aggr_done, 1)
            e.wait_ge(aggr_done, T)
            link(e.tensor_copy(Er, mv2[:, :, 0]))
            link(e.tensor_scalar(Vr, mv2[:, :, 1], 0.96, None, ALU.mult))
            link(e.tensor_tensor(t1, A, A, ALU.mult))
            link(e.tensor_tensor(t1, t1, var1, ALU.mult))
            link(e.scalar_tensor_tensor(t1, t1, SLOPE * SLOPE, Vr, ALU.mult, ALU.add))
            link(e.tensor_tensor(t2, Er, b1, ALU.subtract))
            link(e.tensor_tensor(t2, t2, Er, ALU.mult))
            link(e.scalar_tensor_tensor(t1, t2, 2 * SLOPE * (1 - SLOPE), t1, ALU.mult, ALU.add))
            link(e.tensor_scalar(ve2, t1, EPS, None, ALU.add))
            assert n[0] == TAB_VAR2
            e.wait_ge(tab_pow, 2)
            link(e.tensor_tensor(A2, g2, r2, ALU.mult))
            link(e.tensor_scalar(t1, b1, SLOPE, None, ALU.mult))
            link(e.scalar_tensor_tensor(t1, Er, 1 - SLOPE, t1, ALU.mult, ALU.add))
            link(e.tensor_tensor(t1, t1, A2, ALU.mult))
            link(e.tensor_tensor(C2, b2, t1, ALU.subtract))
            link(e.tensor_scalar(sg, A2, 0.0, 2.0, ALU.is_ge, ALU.mult))
            link(e.tensor_scalar(sg, sg, -1.0, None, ALU.add))
            link(e.tensor_copy(ab[:, 2, :], sg))
            link(e.tensor_tensor(k8, A2, sg, ALU.mult))
            link(e.tensor_scalar(k8, k8, 1 - SLOPE, None, ALU.mult))
            link(e.tensor_tensor(ab[:, 0, :], k8, A, ALU.mult))
            link(e.tensor_scalar(t3, A2, SLOPE, None, ALU.mult))
            link(e.tensor_tensor(ab[:, 1, :], t3, A, ALU.mult))
            link(e.tensor_tensor(gdc[:, 0], C[:], wide(k8), ALU.mult))
            link(e.tensor_tensor(gdc[:, 1], C[:], wide(t3), ALU.mult))
            e.tensor_tensor(gdc[:, 1], gdc[:, 1], wide(C2), ALU.add).then_inc(tables_ready, 1)
            e.wait_ge(tab_pe, 4)
            for n_rows, r in ((P, slice(1, 3)), (3 * T, slice(3, 4))):
                own = slice(0, n_rows)
                link(e.tensor_copy(rows[own, r, :], pt[own, r, :]))
                link(e.tensor_copy(parts[own, r, 0, :], rows[own, r, :]))
                link(e.tensor_tensor(rest[own, r, 0, :], rows[own, r, :], parts[own, r, 0, :], ALU.subtract))
                link(e.tensor_copy(parts[own, r, 1, :], rest[own, r, 0, :]))
                link(e.tensor_tensor(rest[own, r, 1, :], rest[own, r, 0, :], parts[own, r, 1, :], ALU.subtract))
                last = e.tensor_copy(parts[own, r, 2, :], rest[own, r, 1, :])
                if n_rows == P:
                    link(last)
            last.then_inc(rows_ready, 1)


TAB_ESQ = 12
TAB_VAR1 = TAB_ESQ + 12
TAB_C = TAB_VAR1 + 5
TAB_VAR2 = TAB_C + 9


def attend_block(nc, S, adj, keep, wh_dram, e9_dram, ab9_dram, gd_dram, s_dram, hp_dram, g3b3,
                 early, x, adj_t, weights):
    B, N, D, T, KD = S.B, S.N, S.D, S.T, S.KD
    ADJ = 4
    with ExitStack() as ctx:
        sb = lambda name, shape, dt: ctx.enter_context(nc.sbuf_tensor(name, shape, dt))
        ps = lambda name, shape, dt: ctx.enter_context(nc.psum_tensor(name, shape, dt))
        sem = lambda name: ctx.enter_context(nc.semaphore(name))
        ident = keep["ident"]
        erow = [sb(f"c_erow{q}", [P, N], BF16) for q in range(2)]
        lrow = [sb(f"c_lrow{q}", [P, 2, N], BF16) for q in range(2)]
        srow = sb("c_srow", [P, N], F32)
        wh = [sb(f"c_wh{q}", [P, 2, T, D], F16) for q in range(2)]
        adjr = sb("c_adjr", [P, ADJ, N], F32)
        relu = sb("c_relu", [P, 2, N], F32)
        logit = sb("c_logit", [P, 2, N], F32)
        prob = sb("c_prob", [P, 2, N], F32)
        masked = sb("c_masked", [P, 2, N], F32)
        negmax = sb("c_negmax", [P, 2], F32)
        rowsum = sb("c_rowsum", [P, 4], F32)
        rinv = sb("c_rinv", [P, 4], F32)
        pth = sb("c_pth", [P, 2, T, P], F16)
        ptl = sb("c_ptl", [P, 2, T, P], F16)
        hp = [sb(f"c_hp{q}", [P, T, D], F32) for q in range(2)]
        st3 = sb("c_st3", [P, KD, B * T // 2, 6], F32)
        mv3 = sb("c_mv3", [P, KD, 2], F32)
        sc3 = sb("c_sc3", [P, 6, KD], F32)
        g3b3_sb = sb("c_g3b3", [P, 2, KD], F32)
        diag = sb("c_diag", [P, 2, KD, P], F32)
        p_relu = ps("c_p_relu", [P, N], F32)
        p_lin = ps("c_p_lin", [P, N], F32)
        p_t = ps("c_p_t", [P, T, P], F32)
        p_o = ps("c_p_o", [P, 512], F32)
        p_s = ps("c_p_s", [P, KD, 2 * P], F32)

        rows_cleared = sem("c_rows_cleared")
        const_loaded = sem("c_const_loaded")
        rows_loaded = [sem(f"c_rows_loaded{q}") for q in range(2)]
        wh_loaded = [sem(f"c_wh_loaded{q}") for q in range(2)]
        adj_loaded = [sem(f"c_adj_loaded{k}") for k in range(ADJ)]
        lin_done, relu_done, signed_done = sem("c_lin_done"), sem("c_relu_done"), sem("c_signed_done")
        logit_done, prob_done, masked_done = sem("c_logit_done"), sem("c_prob_done"), sem("c_masked_done")
        pt_done, pth_done, ptl_done = sem("c_pt_done"), sem("c_pth_done"), sem("c_ptl_done")
        pv_done, rinv_done, hp_done = sem("c_pv_done"), sem("c_rinv_done"), sem("c_hp_done")
        ht_done, st3_done = sem("c_ht_done"), sem("c_st3_done")
        hp_stored = [sem(f"c_hp_stored{q}") for q in range(2)]
        early_loaded, early_adjt = sem("c_early_loaded"), sem("c_early_adjt")
        fin, fin_pow, fin_pe = sem("c_fin"), sem("c_fin_pow"), sem("c_fin_pe")
        block = ctx.enter_context(nc.Block())
        TILES = B * T

        @block.sync
        def _(e):
            e.dma_start(srow[:].rearrange("p (t n) -> p t n", t=T),
                        s_dram.partition_broadcast(P)).then_inc(const_loaded, 16)
            e.dma_start(g3b3_sb[:], g3b3.rearrange("p (c k) -> p c k", c=2)).then_inc(const_loaded, 16)
            e.wait_ge(rows_cleared, 4)
            for q in range(2):
                e.dma_start(lrow[q][0:9].rearrange("r c n -> r (c n)"),
                            ab9_dram.rearrange("r c t n -> r (c t n)")).then_inc(const_loaded, 16)

            def load_rows(b, q):
                e.dma_start(erow[q][0:9].rearrange("r (t n) -> r t n", t=T),
                            e9_dram.rearrange("r (t b) n -> b r t n", b=B)[b]).then_inc(rows_loaded[q], 16)
                for kind in range(2):
                    e.dma_start(lrow[q][9:12, kind].rearrange("r (t n) -> r t n", t=T),
                                gd_dram[kind].rearrange("r (t b) n -> b r t n", b=B)[b]).then_inc(rows_loaded[q], 16)

            load_wh = lambda b, q: e.dma_start(wh[q][:], wh_dram[b]).then_inc(wh_loaded[q], 16)
            for q in range(2):
                load_rows(q, q)
            for q in range(2):
                load_wh(q, q)
            def store(b, q):
                e.wait_ge(hp_done, b * T + T)
                e.dma_start(hp_dram[b], hp[q][:]).then_inc(hp_stored[q], 16)

            with e.Fori(0, B // 2 - 1) as i:
                for q in range(2):
                    b = i * 2 + q
                    e.wait_ge(pv_done, b * T + T)
                    load_rows(b + 2, q)
                    load_wh(b + 2, q)
                    store(b, q)
            e.wait_ge(hp_stored[0], 16)
            e.dma_start(early["z"][:], hp_dram[0]).then_inc(early_loaded, 16)
            for q in range(2):
                e.dma_start(early["zx"][q][:], x[q].rearrange("(t p) d -> p t d", p=P)).then_inc(early_loaded, 16)
            for dst, src in zip(early["weights"], weights):
                e.dma_start(dst, src.rearrange("(k p) o -> p k o", p=P)).then_inc(early_loaded, 16)
            for q in range(2):
                store(B - 2 + q, q)
            e.wait_ge(early_loaded, 16 * 7)

        @block.gpsimd
        def _(e):
            load = lambda b, t: e.dma_start(
                adjr[:, t % ADJ, :], adj[b, t * P:(t + 1) * P, :]).then_inc(adj_loaded[t % ADJ], 16)

            def mask(b, t):
                g = b * T + t
                e.wait_ge(prob_done, g + 1)
                e.wait_ge(adj_loaded[t % ADJ], (b * (T // ADJ) + t // ADJ + 1) * 16)
                after(e, pt_done, g - 1)
                e.tensor_tensor(masked[:, t % 2, :], prob[:, t % 2, :], adjr[:, t % ADJ, :],
                                ALU.mult).then_inc(masked_done, 1)

            for t in range(ADJ):
                load(0, t)

            def graph(b, last=False):
                for t in range(T):
                    mask(b, t)
                    e.wait_ge(masked_done, b * T + t + 1)
                    if t + ADJ < T:
                        load(b, t + ADJ)
                    elif not last:
                        load(b + 1, t + ADJ - T)

            graph(0)
            with e.Fori(1, B - 1) as b:
                graph(b)
            for q in range(2):
                e.dma_start(early["adjt"][q][:, 0:T - 1, :],
                            adj_t[q].rearrange("(t p) n -> p t n", p=P)[:, 0:T - 1, :]).then_inc(early_adjt, 16)
            graph(B - 1, last=True)
            e.wait_ge(early_adjt, 32)
            e.wait_ge(fin, FIN_VAR)
            e.tensor_tensor(sc3[:, 1, :], sc3[:, 0, :], keep["minus_half"][:, 0:KD], ALU.pow).then_inc(fin_pow, 1)

        @block.tensor
        def _(e):
            e.wait_ge(const_loaded, 64)

            def lin(b, q, i, t):
                g = b * T + t
                if t == 0:
                    e.wait_ge(rows_loaded[q], i * 48 + 48)
                e.wait_ge(relu_done, g)
                for h in range(2):
                    e.matmul(p_relu[:, h * 512:(h + 1) * 512], erow[q][:, t * P:(t + 1) * P],
                             lrow[q][:, 0, h * 512:(h + 1) * 512], start=True, stop=True)
                e.wait_ge(logit_done, g)
                for h in range(2):
                    mm = e.matmul(p_lin[:, h * 512:(h + 1) * 512], erow[q][:, t * P:(t + 1) * P],
                                  lrow[q][:, 1, h * 512:(h + 1) * 512], start=True, stop=True)
                mm.then_inc(lin_done, 1)

            def turn(g, t):
                e.wait_ge(masked_done, g + 1)
                e.wait_ge(ptl_done, g)
                for j in range(T):
                    mm = e.transpose(p_t[:, j, :], masked[:, t % 2, j * P:(j + 1) * P], ident[:])
                mm.then_inc(pt_done, 1)

            def pv(g, q, i, t):
                if t == 0:
                    e.wait_ge(wh_loaded[q], i * 16 + 16)
                e.wait_ge(ptl_done, g + 1)
                e.wait_ge(hp_done, g)
                parts = [(pp, w, j) for j in range(T) for pp, w in ((pth, 0), (pth, 1), (ptl, 0))]
                for n, (pp, w, j) in enumerate(parts):
                    mm = e.matmul(p_o[:, 0:D], pp[:, t % 2, j, :], wh[q][:, w, j, :],
                                  start=(n == 0), stop=(n == len(parts) - 1))
                mm.then_inc(pv_done, 1)

            def flip(g, q, t):
                e.wait_ge(hp_done, g + 1)
                if t % 2 == 0:
                    e.wait_ge(st3_done, g)
                for k in range(KD):
                    mm = e.transpose(p_s[:, k, (t % 2) * P:(t % 2 + 1) * P], hp[q][:, t, k * P:(k + 1) * P], ident[:])
                if t % 2:
                    mm.then_inc(ht_done, 1)

            LAGS = ((2, turn), (3, pv), (4, flip))

            def slot(i, q, t, first=False):
                b = i * 2 + q
                lin(b, q, i, t)
                for lag, what in LAGS:
                    if first and t < lag:
                        continue
                    tt = (t - lag) % T
                    late = t < lag
                    g = b * T + t - lag
                    if what is turn:
                        turn(g, tt)
                    elif what is pv:
                        if late:
                            pv(g, 1 - q, i if q else i - 1, tt)
                        else:
                            pv(g, q, i, tt)
                    else:
                        flip(g, 1 - q if late else q, tt)

            for q in range(2):
                for t in range(T):
                    slot(0, q, t, first=(q == 0))
            with e.Fori(1, B // 2) as i:
                for q in range(2):
                    for t in range(T):
                        slot(i, q, t)
            for t in range(4):
                for lag, what in LAGS:
                    if t < lag:
                        g, tt = TILES + t - lag, T + t - lag
                        if what is turn:
                            turn(g, tt)
                        elif what is pv:
                            pv(g, 1, B // 2 - 1, tt)
                        else:
                            flip(g, 1, tt)
            e.wait_ge(fin, FIN_DIAG)
            for c in range(2):
                for k in range(KD):
                    mm = e.matmul(p_relu[:, (c * KD + k) * P:(c * KD + k + 1) * P], keep["ones"][:],
                                  diag[:, c, k, :], start=True, stop=True)
            mm.then_inc(fin_pe, 1)

        @block.scalar
        def _(e):
            def relus(b, t):
                g = b * T + t
                e.wait_ge(lin_done, g + 1)
                after(e, logit_done, g - 1)
                e.activation(relu[:, t % 2, :], p_relu[:], ACT.Relu).then_inc(relu_done, 1)

            def exps(b, t):
                g = b * T + t
                e.wait_ge(logit_done, g + 1)
                after(e, masked_done, g - 1)
                after(e, rinv_done, g - 3)
                e.activation(prob[:, t % 2, :], logit[:, t % 2, :], ACT.Exp, bias=negmax[:, t % 2:t % 2 + 1],
                             scale=-1.0, accum_out=rowsum[:, t % 4:t % 4 + 1]).then_inc(prob_done, 1)

            def highs(g, t):
                e.wait_ge(pt_done, g + 1)
                after(e, pv_done, g - 1)
                e.activation(pth[:, t % 2], p_t[:], ACT.Copy).then_inc(pth_done, 1)

            def graph(b, first=False):
                for t in range(T):
                    relus(b, t)
                    if not (first and t < 2):
                        highs(b * T + t - 2, (t - 2) % T)
                    exps(b, t)
            graph(0, True)
            with e.Fori(1, B) as b:
                graph(b)
            for t in range(2):
                highs(TILES + t - 2, T + t - 2)

        @block.vector
        def _(e):
            for q in range(2):
                e.memset(erow[q][:], 1.0).then_inc(rows_cleared, 1)
                e.memset(lrow[q][:], 0.0).then_inc(rows_cleared, 1)

            def inverse(g, t):
                e.reciprocal(rinv[:, t % 4:t % 4 + 1], rowsum[:, t % 4:t % 4 + 1]).then_inc(rinv_done, 1)

            def logits(b, t):
                g = b * T + t
                e.wait_ge(relu_done, g + 1)
                e.tensor_tensor(relu[:, t % 2, :], relu[:, t % 2, :], srow[:], ALU.mult).then_inc(signed_done, 1)
                e.wait_ge(signed_done, g + 1)
                after(e, prob_done, g - 1)
                if not isinstance(g, int) or g >= 2:
                    inverse(g - 2, (t - 2) % T)
                e.tensor_tensor_reduce(logit[:, t % 2, :], relu[:, t % 2, :], p_lin[:], -1.0, BIG,
                                       ALU.add, ALU.min, negmax[:, t % 2:t % 2 + 1]).then_inc(logit_done, 1)

            def lows(g, t):
                e.wait_ge(pth_done, g + 1)
                after(e, pv_done, g - 1)
                e.tensor_tensor(ptl[:, t % 2], p_t[:], pth[:, t % 2], ALU.subtract).then_inc(ptl_done, 1)

            def outs(g, q, i, t):
                if t == 0 and not isinstance(i, int):
                    e.wait_ge(hp_stored[q], i * 16)
                    e.wait_ge(ht_done, (i * 2 + q - 1) * (T // 2))
                e.wait_ge(rinv_done, g + 1)
                e.wait_ge(pv_done, g + 1)
                e.tensor_scalar(hp[q][:, t, :], p_o[:, 0:D], rinv[:, t % 4:t % 4 + 1], None,
                                ALU.mult).then_inc(hp_done, 1)

            def stats(g2, n):
                e.wait_ge(ht_done, g2)
                for k in range(KD):
                    e.bn_stats(st3[:, k, n, :] if isinstance(n, int) else st3[:, k, bass.ds(n, 1), :],
                               p_s[:, k, :]).then_inc(st3_done, 1)

            def slot(i, q, t, first=False):
                b = i * 2 + q
                logits(b, t)
                if not (first and t < 2):
                    lows(b * T + t - 2, (t - 2) % T)
                if not (first and t < 3):
                    late = t < 3
                    outs(b * T + t - 3, 1 - q if late else q, (i if q else i - 1) if late else i, (t - 3) % T)
                if t % 2 == 1 and not (first and t < 5):
                    n = b * (T // 2) + (t - 5) // 2
                    stats(n + 1, n)

            for q in range(2):
                for t in range(T):
                    slot(0, q, t, first=(q == 0))
            with e.Fori(1, B // 2) as i:
                for q in range(2):
                    for t in range(T):
                        slot(i, q, t)
            for t in range(3):
                if t < 2:
                    e.wait_ge(prob_done, TILES + t - 1)
                    inverse(TILES + t - 2, T + t - 2)
                    lows(TILES + t - 2, T + t - 2)
                outs(TILES + t - 3, 1, B // 2 - 1, T + t - 3)
                if t == 1:
                    stats(TILES // 2 - 1, TILES // 2 - 2)
            stats(TILES // 2, TILES // 2 - 1)
            e.wait_ge(st3_done, TILES)
            n = [0]

            def link(ins):
                n[0] += 1
                ins.then_inc(fin, 1)
                e.wait_ge(fin, n[0])
            for k in range(KD):
                link(e.bn_aggr(mv3[:, k, :], st3[:, k].rearrange("p n s -> p (n s)")))
            link(e.tensor_scalar(sc3[:, 0, :], mv3[:, :, 1], EPS, None, ALU.add))
            assert n[0] == FIN_VAR
            e.wait_ge(fin_pow, 1)
            link(e.tensor_tensor(sc3[:, 2, :], g3b3_sb[:, 0, :], sc3[:, 1, :], ALU.mult))
            link(e.tensor_tensor(sc3[:, 3, :], mv3[:, :, 0], sc3[:, 2, :], ALU.mult))
            link(e.tensor_tensor(sc3[:, 4, :], g3b3_sb[:, 1, :], sc3[:, 3, :], ALU.subtract))
            for c, src in ((0, 2), (1, 4)):
                for k in range(KD):
                    link(e.tensor_scalar(diag[:, c, k, :], ident[:], sc3[:, src, k:k + 1], None, ALU.mult))
            assert n[0] == FIN_DIAG
            e.wait_ge(fin_pe, 1)
            link(e.tensor_copy(keep["norm3"][:].rearrange("p c d -> p (c d)"), p_relu[:, 0:2 * D]))
            for q in range(2):
                e.wait_ge(hp_stored[q], 16 * (B // 2))


FIN_VAR = 3
FIN_DIAG = FIN_VAR + 3 + 4


def layers_block(nc, S, x, adj, adj_t, mask, b1c, b2r, b3r, eps, keep, early, hp_dram, out):
    B, N, D, T, KD, H, KH = S.B, S.N, S.D, S.T, S.KD, S.H, S.KH
    PAIRS = B // 2
    BANKS = 4
    RING = 3
    LNS = 6

    order = []
    COVER, COVER_AT = (("mlp", 1, 1), ("pv", 0, T - 1)), 3
    turned_in = lambda layer, q: [("hi%d" % layer, q, 0), ("lo%d" % layer, q, 0)]
    for q in range(2):
        order += [("agg", q, d) for d in range(KD)] + [("hid", q, f) for f in range(KH)]
        order += turned_in(2, 0) if q == 1 else []
        order += [("mlp", q, g) for g in range(2) if ("mlp", q, g) not in COVER]
    for q in range(2):
        order += [("int", q, d) for d in range(KD)]
        for s in range(T + 3):
            order += [("sim", q, s)] if s < T else []
            order += [COVER[q]] if s == COVER_AT else []
            order += [("turn", q, s - 2)] if 2 <= s <= T + 1 else []
            order += turned_in(*((2, 1), (3, 0))[q]) if s == T + 1 else []
            order += [("pv", q, s - 3)] if s >= 3 and ("pv", q, s - 3) not in COVER else []
    for q in range(2):
        order += [("sup", q, g) for g in range(2)] + [("out", q, 0)]
        order += turned_in(3, 1) if q == 0 else []
        order += [("out", q, 1)]
    place = {key: n for n, key in enumerate(order)}
    COUNT = len(order)
    assert COUNT % BANKS == 0

    with ExitStack() as ctx:
        sb = lambda name, shape, dt: ctx.enter_context(nc.sbuf_tensor(name, shape, dt))
        ps = lambda name, shape, dt: ctx.enter_context(nc.psum_tensor(name, shape, dt))
        sem = lambda name: ctx.enter_context(nc.semaphore(name))
        ident, ident16, norm3 = keep["ident"], keep["ident16"], keep["norm3"]
        two = lambda name, shape, dt: [sb(f"d_{name}{q}", shape, dt) for q in range(2)]
        xs = [sb("d_x0", [P, T, D], F32), early["x1"]]
        adjt, z, y = early["adjt"], early["z"], early["y"]
        hh, hl = two("hh", [P, T, D], F16), two("hl", [P, T, D], F16)
        hth, htl = two("hth", [P, KD, N], F16), two("htl", [P, KD, N], F16)
        zx = early["zx"]
        zparts = [zx[q][:].rearrange("p t d -> p (t d)").bitcast(F16).rearrange("p (c k n) -> p c k n", c=2, k=KD) for q in range(2)]
        zh, zl = [v[:, 0] for v in zparts], [v[:, 1] for v in zparts]
        hidh, hidl = two("hidh", [P, KH, N], F16), two("hidl", [P, KH, N], F16)
        suph = [hidh[q][:].rearrange("p f n -> p (f n)")[:, 0:T * D].rearrange("p (t d) -> p t d", t=T) for q in range(2)]
        supl = [hidl[q][:].rearrange("p f n -> p (f n)")[:, 0:T * D].rearrange("p (t d) -> p t d", t=T) for q in range(2)]
        kept, neg = two("kept", [P, N], BF16), two("neg", [P, N], BF16)
        maski = sb("d_maski", [P, N], I32)
        tmp = sb("d_tmp", [P, T, D], F32)
        hid32 = tmp[:].rearrange("p t d -> p (t d)").rearrange("p (a n) -> p a n", a=2)
        adjr = sb("d_adjr", [P, RING, N], F32)
        h32 = {(1, 0): tmp, (1, 1): z, (2, 0): z, (2, 1): tmp, (3, 0): tmp, (3, 1): tmp}
        normed = lambda layer, q: (zx if layer == 1 else xs)[q]
        pth, ptl = sb("d_pth", [P, 2, T, P], F16), sb("d_ptl", [P, 2, T, P], F16)
        w1h, w1l = sb("d_w1h", [P, KD, H], F16), sb("d_w1l", [P, KD, H], F16)
        w2h, w2l = sb("d_w2h", [P, KH, D], F16), sb("d_w2l", [P, KH, D], F16)
        wlh, wll = sb("d_wlh", [P, KD, D], F16), sb("d_wll", [P, KD, D], F16)
        w3h, w3l = sb("d_w3h", [P, KD, D], F16), sb("d_w3l", [P, KD, D], F16)
        b1 = sb("d_b1", [P, KH], F32)
        bias = sb("d_bias", [P, 2, D], F32)
        wide_bias = lambda n: bias[:, n, :].unsqueeze(1).to_broadcast([P, T, D])
        eps1 = sb("d_eps1", [P, 1], F32)
        diah, dial = sb("d_diah", [P, P], F16), sb("d_dial", [P, P], F16)
        st, small, sums = sb("d_st", [P, T, 6], F32), sb("d_small", [P, 4, T], F32), sb("d_sums", [P, T], F32)
        ve, rstd, shift = (sb(f"d_{n}", [P, T], F32) for n in ("ve", "rstd", "shift"))
        rowmax, negmax = sb("d_rowmax", [P, 2], F32), sb("d_negmax", [P, 2], F32)
        rowsum, rinv = sb("d_rowsum", [P, 4], F32), sb("d_rinv", [P, 4], F32)
        hold = sb("d_hold", [P, 1], F32)
        bank = [ps(f"d_bank{k}", [P, N], F32) for k in range(BANKS)]
        dia32 = tmp[:].rearrange("p t d -> p (t d)")[:, 0:P]

        w_hi, w_lo, setup = sem("d_w_hi"), sem("d_w_lo"), sem("d_setup")
        consts_loaded, bias_added = sem("d_consts_loaded"), sem("d_bias_added")
        z_loaded, z_scaled, z_ready, z_min, z_exp = (
            sem(f"d_{n}") for n in ("z_loaded", "z_scaled", "z_ready", "z_min", "z_exp"))
        x_loaded = [sem(f"d_x_loaded{q}") for q in range(2)]
        x_plus, x_first, x_moved = sem("d_x_plus"), sem("d_x_first"), sem("d_x_moved")
        adjt_loaded = [[sem(f"d_adjt_loaded{q}{h}") for h in range(2)] for q in range(2)]
        row_loaded = [sem(f"d_row_loaded{k}") for k in range(RING)]
        row_kept = sem("d_row_kept")
        mask_loaded, neg_ready, kept_ready = sem("d_mask_loaded"), sem("d_neg_ready"), sem("d_kept_ready")
        ln_stats, ln_small, ln_var = sem("d_ln_stats"), sem("d_ln_small"), sem("d_ln_var")
        ln_rstd, ln_shift = sem("d_ln_rstd"), sem("d_ln_shift")
        h_ready, hh_ready, hl_ready = sem("d_h_ready"), sem("d_hh_ready"), sem("d_hl_ready")
        bank_full, bank_free = sem("d_bank_full"), sem("d_bank_free")
        hi_done = sem("d_hi_done")
        hid32_done, hidh_done = sem("d_hid32_done"), sem("d_hidh_done")
        max_found = sem("d_max_found")
        max_done, prob_done, rinv_done = sem("d_max_done"), sem("d_prob_done"), sem("d_rinv_done")
        held = sem("d_held")
        stored = [sem(f"d_stored{q}") for q in range(2)]
        block = ctx.enter_context(nc.Block())

        his, HIS = {}, 0
        for key in order:
            if key[0] in ("agg", "hi2", "int", "turn", "hi3", "sup"):
                HIS += 1
                his[key] = HIS
        full = lambda i, key: i * COUNT + place[key] + 1
        free = lambda i, key: i * COUNT + place[key] + 1 + BANKS
        hi = lambda i, key: i * HIS + his[key]
        tile = lambda key: bank[place[key] % BANKS]
        ln = lambda i, layer, q: i * LNS + 2 * (layer - 1) + q
        sims = lambda i, q, s: (i * 2 + q) * T + s

        @block.sync
        def _(e):
            def load_z(b):
                e.dma_start(z[:], hp_dram[b]).then_inc(z_loaded, 16)

            def load_x(b, q):
                e.dma_start(zx[q][:], x[b].rearrange("(t p) d -> p t d", p=P)).then_inc(x_loaded[q], 16)

            for dst, src in ((b1[:], b1c), (eps1[:], eps.partition_broadcast(P)), (bias[:, 0, :], b2r[0].partition_broadcast(P)),
                             (bias[:, 1, :], b3r[0].partition_broadcast(P))):
                e.dma_start(dst, src).then_inc(consts_loaded, 16)

            def load_row(i, g):
                q, s = g // T, g % T
                e.dma_start(adjr[:, g % RING, :], adj[i * 2 + q, s * P:(s + 1) * P, :]).then_inc(row_loaded[g % RING], 16)

            def pair(i, last=False):
                for g in range(RING):
                    load_row(i, g)
                for q in range(2):
                    b = i * 2 + q
                    e.wait_ge(neg_ready, b + FIRST)
                    e.dma_start(maski[:], mask[b].partition_broadcast(P)).then_inc(mask_loaded, 16)
                if not last:
                    e.wait_ge(hl_ready, ln(i, 2, 0) + 1)
                    load_z(i * 2 + 2)
                for g in range(RING, 2 * T):
                    p = g - RING
                    e.wait_ge(bank_free, free(i, ("sim", p // T, p % T)))
                    load_row(i, g)
                    if p == T - 1 and not last:
                        load_x(i * 2 + 2, 0)
                if not last:
                    e.wait_ge(bank_free, free(i, ("sim", 1, T - 1)))
                    load_x(i * 2 + 3, 1)
                    e.wait_ge(x_first, i * 2 + 3)
                    load_z(i * 2 + 3)
                for q in range(2):
                    result = out[i * 2 + q].rearrange("(t p) d -> p t d", p=P)
                    if last and q == 1:
                        for g, part in enumerate((slice(0, T // 2), slice(T // 2, T))):
                            e.wait_ge(bank_free, free(i, ("out", q, g)))
                            e.dma_start(result[:, part, :], xs[q][:, part, :]).then_inc(stored[q], 16)
                    else:
                        e.wait_ge(bank_free, free(i, ("out", q, 1)))
                        e.dma_start(result, xs[q][:]).then_inc(stored[q], 16)

            e.wait_ge(x_first, 1)
            load_z(1)
            with e.Fori(0, PAIRS - 1) as i:
                pair(i)
            pair(PAIRS - 1, last=True)
            for q in range(2):
                e.wait_ge(stored[q], 16 * (PAIRS + q) + FIRST)

        ROWS = [len([g for g in range(2 * T) if g % RING == k]) for k in range(RING)]

        @block.gpsimd
        def _(e):

            def load_adjt(b, q, h, tiles=slice(0, T)):
                part = slice(h * (N // 2), (h + 1) * (N // 2))
                rows = adj_t[b].rearrange("(t p) n -> p t n", p=P)
                e.dma_start(adjt[q][:, tiles, part], rows[:, tiles, part]).then_inc(adjt_loaded[q][h], 16)

            def rstds(n):
                e.wait_ge(ln_var, n + 1)
                after(e, h_ready, n * T)
                e.tensor_tensor(rstd[:], ve[:], keep["minus_half"][:, 0:T], ALU.pow).then_inc(ln_rstd, 1)

            def scale_z(b):
                e.wait_ge(z_loaded, b * 16)
                e.tensor_tensor(z[:], z[:], norm3[:, 0, :].unsqueeze(1).to_broadcast([P, T, D]), ALU.mult).then_inc(z_scaled, 1)
                e.wait_ge(z_scaled, b + 1)
                e.tensor_tensor(z[:], z[:], norm3[:, 1, :].unsqueeze(1).to_broadcast([P, T, D]), ALU.add).then_inc(z_ready, 1)

            def add_bias3(i, q):
                e.wait_ge(h_ready, (ln(i, 3, q) + 1) * T)
                e.tensor_tensor(xs[q][:], xs[q][:], wide_bias(1), ALU.add).then_inc(bias_added, 1)

            def mask_rows(i, q, first, past):
                e.wait_ge(kept_ready, i * 2 + q + 1)
                for s in range(first, past):
                    g = q * T + s
                    e.wait_ge(row_loaded[g % RING], i * (16 * ROWS[g % RING]) + 16 * (g // RING + 1))
                    row = adjr[:, g % RING, :]
                    e.tensor_tensor(row, row, kept[q][:], ALU.mult).then_inc(row_kept, 1)

            def pair(i, last=False):
                rstds(ln(i, 1, 1))
                rstds(ln(i, 2, 0))
                if not last:
                    scale_z(i * 2 + 2)
                mask_rows(i, 0, 0, 6)
                rstds(ln(i, 2, 1))
                mask_rows(i, 0, 6, T)
                mask_rows(i, 1, 0, 6)
                rstds(ln(i, 3, 0))
                mask_rows(i, 1, 6, T)
                add_bias3(i, 0)
                rstds(ln(i, 3, 1))
                add_bias3(i, 1)
                if not last:
                    rstds(ln(i + 1, 1, 0))
                    for h in range(2):
                        e.wait_ge(bank_full, full(i, ("out", 0, h)))
                        load_adjt(i * 2 + 2, 0, h)
                    scale_z(i * 2 + 3)
                    for h in range(2):
                        e.wait_ge(bank_full, full(i, ("out", 1, h)))
                        load_adjt(i * 2 + 3, 1, h)

            for q in range(2):
                for h in range(2):
                    load_adjt(q, q, h, slice(T - 1, T))
            rstds(0)
            scale_z(1)
            with e.Fori(0, PAIRS - 1) as i:
                pair(i)
            pair(PAIRS - 1, last=True)

        @block.tensor
        def _(e):
            def into(i, key):
                e.wait_ge(bank_free, i * COUNT + place[key] + 1)
                return tile(key)

            def products(dst, parts, last):
                for n, (a, m) in enumerate(parts):
                    mm = e.matmul(dst, a, m, start=(n == 0), stop=(n == len(parts) - 1))
                if last:
                    mm.then_inc(bank_full, 1)

            def add_products(dst, parts, first=False, last=False):
                for n, (a, m) in enumerate(parts):
                    mm = e.matmul(dst, a, m, start=(first and n == 0), stop=(last and n == len(parts) - 1), skip_group_check=True)
                return mm

            halves = [slice(h * 512, (h + 1) * 512) for h in range(N // 512)]
            cut = lambda n: slice(n * P, (n + 1) * P)

            def by_columns(i, keys, parts, ready):
                for step in range(2):
                    e.wait_ge(*ready[step])
                    for key in keys:
                        dst = tile(key) if step else into(i, key)
                        for half in halves:
                            mm = add_products(dst[:, half], parts(key, step, half), first=(step == 0), last=(step == 1))
                        if step == 1:
                            mm.then_inc(bank_full, 1)

            def by_rows(i, keys, parts, ready):
                per_bank = 512 // D
                for step in range(2):
                    e.wait_ge(*ready[step]) if ready[step] else None
                    for key in keys:
                        dst = tile(key) if step else into(i, key)
                        for t in range(T // 2):
                            mm = add_products(dst[:, t * D:(t + 1) * D], parts(key, step, key[2] * T // 2 + t),
                                              first=(step == 0 and t % per_bank == 0), last=(step == 1))
                        if step == 1:
                            mm.then_inc(bank_full, 1)

            e.wait_ge(setup, 4)

            def turns(i, q, layer):
                for name, src, ready in (("hi", hh[q], hh_ready), ("lo", hl[q], hl_ready)):
                    dst = into(i, (f"{name}{layer}", q, 0))
                    dst = dst[:].bitcast(F16).rearrange("p (k n) -> p k n", k=KD)
                    e.wait_ge(ready, ln(i, layer, q) + 1)
                    for k in range(KD):
                        for t in range(T):
                            mm = e.transpose(dst[:, k, cut(t)], src[:, t, cut(k)], ident16[:])
                    mm.then_inc(bank_full, 1)

            def mlp(key, step, t):
                fs = (KH - 1,) if step else range(KH - 1)
                return [(a[key[1]][:, f, cut(t)], w[:, f, :]) for f in fs for a, w in ((hidh, w2h), (hidh, w2l), (hidl, w2h))]

            def values(i, q, r):
                dst = into(i, ("pv", q, r))
                e.wait_ge(bank_free, free(i, ("turn", q, r)))
                products(dst[:, 0:D], [(a[:, r % 2, t, :], m[q][:, t, :]) for t in range(T)
                                       for a, m in ((pth, hh), (pth, hl), (ptl, hh))], True)

            def layer1(i, q):
                e.wait_ge(hl_ready, ln(i, 1, q) + 1)
                for d in range(KD):
                    key = ("agg", q, d)
                    dst = into(i, key)
                    for h, half in enumerate(halves):
                        blocks = range(h * T // 2, (h + 1) * T // 2)
                        if d == 0:
                            e.wait_ge(adjt_loaded[q][h], i * 16 + 16)
                        for t in blocks:
                            for a, dia in ((hh[q], diah), (hh[q], dial), (hl[q], diah)):
                                e.matmul(dst[:, cut(t)], a[:, t, cut(d)], dia[:], stop=False, skip_group_check=True,
                                         start=(t == blocks[0] and a is hh[q] and dia is diah))
                        for t in range(T):
                            for a in (hh[q], hl[q]):
                                mm = e.matmul(dst[:, half], a[:, t, cut(d)], adjt[q][:, t, half], start=False,
                                              stop=(t == T - 1 and a is hl[q]), skip_group_check=True)
                    mm.then_inc(bank_full, 1)
                e.wait_ge(w_lo, 4)
                def hid(key, step, half):
                    return [(w[:, step, cut(key[2])], m[q][:, step, half]) for w, m in ((w1h, zh), (w1l, zh), (w1h, zl))]
                by_columns(i, [("hid", q, f) for f in range(2)], hid,
                           [(bank_free, free(i, ("agg", q, 0))), (bank_free, free(i, ("agg", q, 1)))])
                for f in range(2, KH):
                    key = ("hid", q, f)
                    dst = into(i, key)
                    for h, half in enumerate(halves):
                        products(dst[:, half], hid(key, 0, half) + hid(key, 1, half), h == len(halves) - 1)

                if q == 1:
                    turns(i, 0, 2)
                by_rows(i, [("mlp", q, 0)], mlp, [(bank_free, free(i, ("hid", q, KH - 2))), (bank_free, free(i, ("hid", q, KH - 1)))])
                if q == 0:
                    by_rows(i, [("mlp", 0, 1)], mlp, [None, None])

            def layer2(i, q):
                e.wait_ge(bank_free, free(i, ("lo2", q, 0)))
                for d in range(KD):
                    dst = into(i, ("int", q, d))
                    for h, half in enumerate(halves):
                        products(dst[:, half], [(w[:, k, cut(d)], m[q][:, k, half]) for k in range(KD)
                                                for w, m in ((wlh, hth), (wlh, htl), (wll, hth))], h == len(halves) - 1)

                def sim(key, step, half):
                    return [(a[q][:, step, cut(key[2])], m[q][:, step, half])
                            for a, m in ((zh, hth), (zh, htl), (zl, hth))]
                by_columns(i, [("sim", q, s) for s in range(2)], sim,
                           [(bank_free, free(i, ("int", q, 0))), (bank_free, free(i, ("int", q, 1)))])
                for s in range(2, T + 3):
                    if s < T:
                        key = ("sim", q, s)
                        dst = into(i, key)
                        for h, half in enumerate(halves):
                            products(dst[:, half], sim(key, 0, half) + sim(key, 1, half), h == len(halves) - 1)
                    if s == COVER_AT and q == 0:
                        by_rows(i, [COVER[0]], mlp, [None, None])
                    elif s == COVER_AT:
                        values(i, 0, T - 1)
                    if s <= T + 1:
                        r = s - 2
                        dst = into(i, ("turn", q, r))
                        e.wait_ge(prob_done, sims(i, q, r) + 1)
                        for t in range(T):
                            mm = e.transpose(dst[:, cut(t)], y[:, r % 2, cut(t)], ident[:])
                        mm.then_inc(bank_full, 1)
                    if s == T + 1:
                        turns(i, *((1, 2), (0, 3))[q])
                    if s >= 3 and ("pv", q, s - 3) not in COVER:
                        values(i, q, s - 3)

            def layer3(i, q):
                e.wait_ge(bank_free, free(i, ("lo3", q, 0)))
                for g in range(2):
                    dst = into(i, ("sup", q, g))
                    for t in range(T // 2):
                        products(dst[:, t * D:(t + 1) * D],
                                 [(a[q][:, k, cut(g * T // 2 + t)], w[:, k, :]) for k in range(KD)
                                  for a, w in ((hth, w3h), (hth, w3l), (htl, w3h))], t == T // 2 - 1)

                def outs(key, step, t):
                    return [(adjt[q][:, m, cut(t)], sp[:, m, :]) for m in range(step * T // 2, (step + 1) * T // 2)
                            for sp in (suph[q], supl[q])]

                by_rows(i, [("out", q, 0)], outs, [(bank_free, free(i, ("sup", q, 0))), (bank_free, free(i, ("sup", q, 1)))])
                if q == 0:
                    turns(i, 1, 3)
                by_rows(i, [("out", q, 1)], outs, [None, None])

            with e.Fori(0, PAIRS) as i:
                for layer in (layer1, layer2, layer3):
                    for q in range(2):
                        layer(i, q)

        @block.scalar
        def _(e):
            def exp_z(b):
                e.wait_ge(z_min, b + 1)
                e.activation(z[:], z[:], ACT.Exp).then_inc(z_exp, 1)

            def h_values(i, layer, q):
                n = ln(i, layer, q)
                if (layer, q) == (2, 0):
                    e.wait_ge(hl_ready, n)
                e.wait_ge(ln_shift, n + 1)
                for t in range(T):
                    e.activation(h32[layer, q][:, t, :], normed(layer, q)[:, t, :], ACT.Relu, bias=shift[:, t:t + 1],
                                 scale=rstd[:, t:t + 1]).then_inc(h_ready, 1)

            def h_high(i, layer, q):
                n = ln(i, layer, q)
                e.wait_ge(h_ready, n * T + T)
                e.activation(hh[q][:], h32[layer, q][:], ACT.Copy).then_inc(hh_ready, 1)

            def high(i, key, dst, src, func=ACT.Copy, **more):
                e.wait_ge(bank_full, full(i, key))
                e.activation(dst, src, func, **more).then_inc(hi_done, 1)

            def turned(i, q, layer):
                key = (f"hi{layer}", q, 0)
                high(i, key, hth[q][:], tile(key)[:].bitcast(F16).rearrange("p (k n) -> p k n", k=KD))

            def layer1(i, q):
                n, m = ((1, 1), (2, 0))[q]
                e.wait_ge(x_moved, i * 2 + q + 1)
                high(i, ("agg", q, 0), zh[q][:, 0, :], tile(("agg", q, 0))[:])
                h_values(i, n, m)
                high(i, ("agg", q, 1), zh[q][:, 1, :], tile(("agg", q, 1))[:])
                h_high(i, n, m)
                for f in range(KH):
                    key = ("hid", q, f)
                    e.wait_ge(bank_full, full(i, key))
                    if f >= 2 or q == 1:
                        e.wait_ge(bank_free, free(i, ("hid", q, f - 2) if f >= 2 else ("hid", 0, f + 2)))
                    else:
                        e.wait_ge(hl_ready, ln(i, 1, 0) + 1)
                    e.activation(hid32[:, f % 2, :], tile(key)[:], ACT.Relu, bias=b1[:, f:f + 1]).then_inc(hid32_done, 1)
                if q == 1:
                    turned(i, 0, 2)

            def layer2(i, q, last):
                n, m = ((2, 1), (3, 0))[q]
                for d in range(KD):
                    high(i, ("int", q, d), zh[q][:, d, :], tile(("int", q, d))[:])
                for s in range(T + 2):
                    if s >= 2:
                        r = s - 2
                        if r >= 2:
                            e.wait_ge(bank_full, full(i, ("pv", q, r - 2)))
                        key = ("turn", q, r)
                        high(i, key, pth[:, r % 2], tile(key)[:].rearrange("p (t n) -> p t n", t=T))
                    if s < T:
                        e.wait_ge(max_done, sims(i, q, s) + 1)
                        e.activation(y[:, s % 2, :], y[:, s % 2, :], ACT.Exp, bias=negmax[:, s % 2:s % 2 + 1],
                                     accum_out=rowsum[:, s % 4:s % 4 + 1]).then_inc(prob_done, 1)
                    if s == 5:
                        h_values(i, n, m)
                    if s == 6:
                        h_high(i, n, m)
                turned(i, *((1, 2), (0, 3))[q])
                if q == 1 and not last:
                    exp_z(i * 2 + 2)

            def layer3(i, q, last):
                for g in range(2):
                    key = ("sup", q, g)
                    high(i, key, suph[q][:, g * T // 2:(g + 1) * T // 2, :], tile(key)[:].rearrange("p (t d) -> p t d", d=D))
                if q == 0:
                    h_values(i, 3, 1)
                    h_high(i, 3, 1)
                    turned(i, 1, 3)
                elif not last:
                    h_values(i + 1, 1, 0)
                    h_high(i + 1, 1, 0)
                    exp_z(i * 2 + 3)

            def pair(i, last=False):
                for q in range(2):
                    layer1(i, q)
                for q in range(2):
                    layer2(i, q, last)
                for q in range(2):
                    layer3(i, q, last)

            exp_z(0)
            h_values(0, 1, 0)
            h_high(0, 1, 0)
            exp_z(1)
            with e.Fori(0, PAIRS - 1) as i:
                pair(i)
            pair(PAIRS - 1, last=True)

        @block.vector
        def _(e):
            e.sem_inc(bank_free, BANKS)
            for first in (neg_ready, held, *stored):
                e.sem_inc(first, FIRST)
            e.wait_ge(consts_loaded, 64)
            e.tensor_scalar(eps1[:], eps1[:], 1.0, None, ALU.add).then_inc(setup, 1)
            e.wait_ge(setup, 1)
            e.tensor_scalar(dia32, ident[:], eps1[:], None, ALU.mult).then_inc(setup, 1)
            e.wait_ge(setup, 2)
            e.tensor_copy(diah[:], dia32).then_inc(setup, 1)
            e.wait_ge(setup, 3)
            e.tensor_tensor(dial[:], dia32, diah[:], ALU.subtract).then_inc(setup, 1)

            def split_signs(b, q, i):
                e.wait_ge(z_ready, b + 1)
                after(e, x_loaded[q], i * 16)
                e.scalar_tensor_tensor(zx[q][:], z[:], 0.0, zx[q][:], ALU.max, ALU.add).then_inc(x_plus, 1)

            def negative_part():
                e.tensor_scalar(z[:], z[:], 0.0, None, ALU.min).then_inc(z_min, 1)

            def join_signs(b, q):
                e.wait_ge(x_plus, b + 1)
                e.wait_ge(z_exp, b + 1)
                e.scalar_tensor_tensor(zx[q][:], z[:], -1.0, zx[q][:], ALU.add, ALU.add).then_inc(x_first, 1)

            def stats(i, layer, q):
                row_stats(e, ln(i, layer, q), T, D, lambda t: normed(layer, q)[:, t, :], st, small, sums, ve,
                          (ln_stats, ln_small, ln_var))

            def stats_part(i, layer, q, rows):
                for t in rows:
                    e.bn_stats(st[:, t, :], normed(layer, q)[:, t, :]).then_inc(ln_stats, 1)
                if rows[-1] == T - 1:
                    row_stats_end(e, ln(i, layer, q), T, D, st, small, sums, ve, (ln_stats, ln_small, ln_var))

            def shifts(i, layer, q):
                n = ln(i, layer, q)
                e.wait_ge(ln_rstd, n + 1)
                e.scalar_tensor_tensor(shift[:], sums[:], -0.5, rstd[:], ALU.mult, ALU.mult).then_inc(ln_shift, 1)

            def h_low(i, layer, q):
                e.wait_ge(hh_ready, ln(i, layer, q) + 1)
                e.tensor_tensor(hl[q][:], h32[layer, q][:], hh[q][:], ALU.subtract).then_inc(hl_ready, 1)

            def low(i, key, dst, src, high):
                e.wait_ge(hi_done, hi(i, key))
                e.tensor_tensor(dst, src, high, ALU.subtract).then_inc(bank_free, 1)

            def z_low(i, key):
                name, q, d = key
                low(i, key, zl[q][:, d, :], tile(key)[:], zh[q][:, d, :])

            def hidden_low(i, q, f):
                n = (i * 2 + q) * KH + f
                e.wait_ge(hid32_done, n + 1)
                e.tensor_copy(hidh[q][:, f, :], hid32[:, f % 2, :]).then_inc(hidh_done, 1)
                e.wait_ge(hidh_done, n + 1)
                e.tensor_tensor(hidl[q][:, f, :], hid32[:, f % 2, :], hidh[q][:, f, :], ALU.subtract).then_inc(bank_free, 1)

            def sup_low(i, q, g):
                key = ("sup", q, g)
                part = slice(g * T // 2, (g + 1) * T // 2)
                low(i, key, supl[q][:, part, :], tile(key)[:].rearrange("p (t d) -> p t d", d=D), suph[q][:, part, :])

            def inverse(i, q, r):
                e.wait_ge(prob_done, sims(i, q, r) + 1)
                e.reciprocal(rinv[:, r % 4:r % 4 + 1], rowsum[:, r % 4:r % 4 + 1]).then_inc(rinv_done, 1)

            def turned(i, q, layer):
                key = (f"lo{layer}", q, 0)
                e.wait_ge(hi_done, hi(i, (f"hi{layer}", q, 0)))
                e.wait_ge(bank_full, full(i, key))
                e.tensor_copy(htl[q][:], tile(key)[:].bitcast(F16).rearrange("p (k n) -> p k n", k=KD)).then_inc(bank_free, 2)

            def add(i, key, q, g):
                e.wait_ge(bank_full, full(i, key))
                if key[0] == "out":
                    e.wait_ge(bias_added, i * 2 + q + 1)
                rows = xs[q][:, g * T // 2:(g + 1) * T // 2, :]
                e.tensor_tensor(rows, tile(key)[:].rearrange("p (t d) -> p t d", d=D), rows, ALU.add).then_inc(bank_free, 1)

            def masks(i, q):
                b = i * 2 + q
                e.wait_ge(mask_loaded, b * 16 + 16)
                e.tensor_scalar(neg[q][:], maski[:], 0, NEG, ALU.is_equal, ALU.mult).then_inc(neg_ready, 1)
                e.wait_ge(neg_ready, b + 1 + FIRST)
                e.tensor_scalar(kept[q][:], neg[q][:], 0.0, None, ALU.is_equal).then_inc(kept_ready, 1)

            def move_x(i, q):
                e.wait_ge(stored[q], 16 * i + FIRST)
                e.wait_ge(x_first, 2 * i + q + 1)
                e.tensor_tensor(xs[q][:], zx[q][:], wide_bias(0), ALU.add).then_inc(x_moved, 1)

            def layer1(i, q):
                norm = ((1, 1), (2, 0))[q]
                if q == 0:
                    join_signs(i * 2 + 1, 1)
                    e.wait_ge(x_first, i * 2 + 2)
                    stats(i, 1, 1)
                else:
                    stats(i, 2, 0)
                z_low(i, ("agg", q, 0))
                shifts(i, *norm)
                z_low(i, ("agg", q, 1))
                if q == 1:
                    h_low(i, 2, 0)
                for f in range(KH):
                    hidden_low(i, q, f)
                if q == 0:
                    h_low(i, 1, 1)
                    move_x(i, 1)
                else:
                    turned(i, 0, 2)
                masks(i, q)
                for g in range(2 - q):
                    add(i, ("mlp", q, g), q, g)
                if q == 0:
                    e.wait_ge(bank_free, free(i, ("mlp", 0, 1)))

            def values(i, q, r):
                e.wait_ge(rinv_done, sims(i, q, r) + 1)
                e.wait_ge(bank_full, full(i, ("pv", q, r)))
                e.scalar_tensor_tensor(xs[q][:, r, :], tile(("pv", q, r))[:, 0:D], rinv[:, r % 4:r % 4 + 1],
                                       xs[q][:, r, :], ALU.mult, ALU.add).then_inc(bank_free, 1)

            def layer2(i, q, last):
                norm = ((2, 1), (3, 0))[q]
                for d in range(KD):
                    z_low(i, ("int", q, d))
                for s in range(T + 3):
                    if s < T:
                        key = ("sim", q, s)
                        n = sims(i, q, s)
                        e.wait_ge(bank_full, full(i, key))
                        e.wait_ge(row_kept, n + 1)
                        if s >= 2:
                            e.wait_ge(bank_full, full(i, ("turn", q, s - 2)))
                        e.tensor_tensor(y[:, s % 2, :], tile(key)[:], adjr[:, (q * T + s) % RING, :], ALU.mult).then_inc(bank_free, 1)
                        e.wait_ge(bank_free, free(i, key))
                        if s >= 2:
                            inverse(i, q, s - 2)
                        else:
                            e.wait_ge(held, 2 * (i * 2 + q) + s + FIRST)
                            e.memset(hold[:], 0.0).then_inc(held, 1)
                        e.tensor_tensor_reduce(y[:, s % 2, :], y[:, s % 2, :], neg[q][:], 1.0, -BIG,
                                               ALU.add, ALU.max, rowmax[:, s % 2:s % 2 + 1]).then_inc(max_found, 1)
                        e.wait_ge(max_found, n + 1)
                        e.tensor_scalar(negmax[:, s % 2:s % 2 + 1], rowmax[:, s % 2:s % 2 + 1], -1.0, None,
                                        ALU.mult).then_inc(max_done, 1)
                    if s == COVER_AT:
                        if q == 0:
                            add(i, COVER[0], 1, 1)
                        else:
                            values(i, 0, T - 1)
                        e.wait_ge(bank_free, free(i, COVER[q]))
                    if 2 <= s <= T + 1:
                        r = s - 2
                        if s >= T:
                            inverse(i, q, r)
                        key = ("turn", q, r)
                        low(i, key, ptl[:, r % 2], tile(key)[:].rearrange("p (t n) -> p t n", t=T), pth[:, r % 2])
                    if s == T + 1:
                        turned(i, *((1, 2), (0, 3))[q])
                    if s >= 3 and ("pv", q, s - 3) not in COVER:
                        values(i, q, s - 3)
                    if 3 <= s < 5:
                        stats_part(i, *norm, range((s - 3) * 4, (s - 2) * 4))
                    if s == 5:
                        shifts(i, *norm)
                    if s == 7:
                        h_low(i, *norm)
                    if s == 5 and q == 1 and not last:
                        split_signs(i * 2 + 2, 0, i + 1)
                    if s == 9 and q == 1 and not last:
                        negative_part()
                if q == 1:
                    e.wait_ge(bank_free, free(i, ("pv", 1, T - 1)))

            def layer3(i, q, last):
                if q == 0:
                    stats(i, 3, 1)
                    sup_low(i, q, 0)
                    shifts(i, 3, 1)
                    sup_low(i, q, 1)
                    if not last:
                        join_signs(i * 2 + 2, 0)
                    h_low(i, 3, 1)
                    add(i, ("out", 0, 0), 0, 0)
                    turned(i, 1, 3)
                    if not last:
                        e.wait_ge(x_first, i * 2 + 3)
                        stats(i + 1, 1, 0)
                    add(i, ("out", 0, 1), 0, 1)
                else:
                    if not last:
                        shifts(i + 1, 1, 0)
                    for g in range(2):
                        sup_low(i, q, g)
                    if not last:
                        h_low(i + 1, 1, 0)
                    add(i, ("out", 1, 0), 1, 0)
                    if not last:
                        split_signs(i * 2 + 3, 1, i + 1)
                        negative_part()
                        move_x(i + 1, 0)
                    add(i, ("out", 1, 1), 1, 1)

            def pair(i, last=False):
                for q in range(2):
                    layer1(i, q)
                for q in range(2):
                    layer2(i, q, last)
                for q in range(2):
                    layer3(i, q, last)

            for step, op in enumerate((ALU.mult, ALU.add)):
                after(e, z_scaled, step)
                scale_or_shift = norm3[:, step, :].unsqueeze(1).to_broadcast([P, T, D])
                e.tensor_tensor(z[:], z[:], scale_or_shift, op).then_inc((z_scaled, z_ready)[step], 1)
            split_signs(0, 0, 0)
            negative_part()
            join_signs(0, 0)
            e.wait_ge(x_first, 1)
            stats(0, 1, 0)
            shifts(0, 1, 0)
            move_x(0, 0)
            for n, (h, l) in enumerate(((w1h, w1l), (w2h, w2l), (wlh, wll), (w3h, w3l))):
                split(e, h[:], l[:], early["weights"][n], (w_hi, n + 1), w_lo)
            h_low(0, 1, 0)
            split_signs(1, 1, 0)
            negative_part()
            with e.Fori(0, PAIRS - 1) as i:
                pair(i)
            pair(PAIRS - 1, last=True)


def graph_layers(nc, x, adj, adj_t, mask, wt, w, a12, vecs, g3b3, w1, w2, wl2, w3, b1c, b2r, b3r, eps, out):
    S = Shapes(x, w1)
    B, N, D, T, KD = S.B, S.N, S.D, S.T, S.KD
    dram = lambda name, shape, dt: nc.dram_tensor(name, shape, dt, kind="Internal").ap()
    wh_dram = dram("wh_dram", [B, P, 2, T, D], F16)
    hp_dram = dram("hp_dram", [B, P, T, D], F32)
    e_dram = dram("e_dram", [P, P], F32)
    e9_dram = dram("e9_dram", [9, P, P], BF16)
    ab9_dram = dram("ab9_dram", [9, 2, T, P], BF16)
    gd_dram = dram("gd_dram", [2, 3, P, P], BF16)
    s_dram = dram("s_dram", [T, P], F32)
    with ExitStack() as ctx:
        sb = lambda name, shape, dt: ctx.enter_context(nc.sbuf_tensor(name, shape, dt))
        keep = {
            "ident": sb("ident", [P, P], F32),
            "ident16": sb("ident16", [P, P], F16),
            "ones": sb("ones", [P, P], F32),
            "minus_half": sb("minus_half", [P, T], F32),
            "norm3": sb("norm3", [P, 2, D], F32),
        }
        with ExitStack() as first:
            fsb = lambda name, shape, dt: first.enter_context(nc.sbuf_tensor(name, shape, dt))
            keep["ecol"] = fsb("ecol", [P, T, B], F32)
            keep["fcol"] = fsb("fcol", [P, T, B], F32)
            keep["C"] = fsb("att_shift", [P, T, B], F32)
            nodes_block(nc, S, x, wt, w, a12, keep, wh_dram)
            tables_block(nc, S, vecs, keep, e9_dram, e_dram, ab9_dram, gd_dram, s_dram)
        early = {
            "z": sb("d_z", [P, T, D], F32),
            "zx": [sb(f"d_zx{q}", [P, T, D], F32) for q in range(2)],
            "adjt": [sb(f"d_adjt{q}", [P, T, N], F16) for q in range(2)],
            "x1": sb("d_x1", [P, T, D], F32),
            "y": sb("d_y", [P, 2, N], F32),
        }
        flat = lambda buf: buf[:].rearrange("p a b -> p (a b)")
        early["weights"] = []
        for src, (buf, at) in zip((w1, w2, wl2, w3), (("x1", 0), ("x1", KD * S.H), ("y", 0), ("y", KD * D))):
            k, width = src.shape[0] // P, src.shape[1]
            early["weights"].append(flat(early[buf])[:, at:at + k * width].rearrange("p (k o) -> p k o", k=k))
        attend_block(nc, S, adj, keep, wh_dram, e9_dram, ab9_dram, gd_dram, s_dram, hp_dram, g3b3,
                     early, x, adj_t, (w1, w2, wl2, w3))
        layers_block(nc, S, x, adj, adj_t, mask, b1c, b2r, b3r, eps, keep, early, hp_dram, out)


def kernel(**inputs):
    import numpy as np
    import concourse.bacc as bacc
    from concourse.bass_utils import run_bass_kernel_spmd

    a = {k: np.asarray(v) for k, v in inputs.items()}
    column = lambda v: v.reshape(-1, P).T
    arrays = {
        "x": a["x"],
        "adj": a["adj"],
        "adj_t": a["adj"].transpose(0, 2, 1),
        "mask": a["nodemask"],
        "wt": a["L0_gnn_W"].T,
        "w": a["L0_gnn_W"],
        "a12": np.stack([column(a["L0_gnn_a1"]), column(a["L0_gnn_a2"])], axis=2).reshape(P, -1),
        "vecs": np.concatenate([column(a[f"L0_gnn_{n}"]) for n in ("g1", "b1", "g2", "b2")], axis=1),
        "g3b3": np.concatenate([column(a["L0_gnn_g3"]), column(a["L0_gnn_b3"])], axis=1),
        "w1": a["L1_gnn_W1"],
        "w2": a["L1_gnn_W2"],
        "wl2": a["L2_gnn_W"],
        "w3": a["L3_gnn_weight"],
        "b1c": column(a["L1_gnn_b1"]),
        "b2r": a["L1_gnn_b2"].reshape(1, -1),
        "b3r": a["L3_gnn_bias"].reshape(1, -1),
        "eps": a["L1_gnn_eps"],
    }
    arrays = {f"in_{k}": np.ascontiguousarray(v) for k, v in arrays.items()}
    nc = bacc.Bacc("TRN2", target_bir_lowering=False, num_devices=1)
    args = [nc.dram_tensor(k, v.shape, mybir.dt.from_np(v.dtype), kind="ExternalInput").ap() for k, v in arrays.items()]
    out = nc.dram_tensor("out", a["x"].shape, F32, kind="ExternalOutput").ap()
    graph_layers(nc, *args, out)
    result = run_bass_kernel_spmd(nc, [arrays], core_ids=[0])
    return result.results[0]["out"]
```
